# Optimizing a Trainium2 kernel written in Bass

```python
import numpy as np
import jax
import jax.numpy as jnp

def _softmax(x, axis=-1):
    return jax.nn.softmax(x, axis=axis)

def _gelu(x):
    return jax.nn.gelu(x, approximate=True)

def _silu(x):
    return jax.nn.silu(x)

def _sigmoid(x):
    return jax.nn.sigmoid(x)

def _layernorm(x, axis=-1, eps=1e-05):
    m = jnp.mean(x, axis=axis, keepdims=True)
    v = jnp.var(x, axis=axis, keepdims=True)
    return (x - m) / jnp.sqrt(v + eps)

def _scatter_add(tgt, idx, src, axis=0):
    return tgt.at[idx].add(src)

def _segment_sum(src, seg, n):
    return jax.ops.segment_sum(src, seg, n)
kernel_name = 'mk_perceiver_d1_seqx_r4_2cc050'

def setup_inputs(seed: int=0):
    np.random.seed(seed)
    _w = jnp.asarray

    def _rec_inputs():
        import jax
        import jax.numpy as jnp
        _rk = jax.random.key(seed)
        x = 7.22e-05 + 1 * jax.random.normal(jax.random.fold_in(_rk, 1), (128, 32, 256), jnp.float32)
        _lenS = 32 - jax.random.randint(jax.random.fold_in(_rk, 7), (128,), 0, max(1, 32 // 4) + 1, jnp.int32)
        _lenS2 = 257 - jax.random.randint(jax.random.fold_in(_rk, 8), (128,), 0, max(1, 257 // 4) + 1, jnp.int32)
        _ctx_1024P = jax.random.normal(jax.random.fold_in(_rk, 11), (128, 16, 256), jnp.float32)
        _ctx_1024c = jax.random.dirichlet(jax.random.fold_in(_rk, 511), 0.3 * jnp.ones((16,), jnp.float32), (128, 257))
        _ctx_1024t = jnp.einsum('bsk,bkd->bsd', _ctx_1024c, _ctx_1024P)
        _ctx_1024t = _ctx_1024t * jax.lax.rsqrt(jnp.mean(jnp.square(_ctx_1024t)) + 1e-12) * 0.953939
        ctx_1024 = -0.000514642 + 1.00011 * (_ctx_1024t + 0.3 * jax.random.normal(jax.random.fold_in(_rk, 611), (128, 257, 256), jnp.float32))
        return (x, ctx_1024)
    x, ctx_1024 = _rec_inputs()

    def _L0_xattn_setup():
        import jax, jax.numpy as jnp
        import numpy as np
        B, L_ENC, L_DEC, D = (16, 128, 128, 256)
        key = jax.random.key(seed)
        k1, k2, k3, k4, k5, k6 = jax.random.split(key, 6)
        encoder_hc = jax.random.normal(k1, (B, L_ENC, D), dtype=jnp.float32)
        decoder_hq = jax.random.normal(k2, (B, L_DEC, D), dtype=jnp.float32)
        w_sim = jax.random.normal(k3, (3 * D,), dtype=jnp.float32) * 0.02
        b_sim = jax.random.normal(k4, (1,), dtype=jnp.float32) * 0.02
        W_qv = jax.random.normal(k5, (4 * D, D), dtype=jnp.float32) * 0.02
        b_qv = jax.random.normal(k6, (D,), dtype=jnp.float32) * 0.02
        return {'encoder_hc': encoder_hc, 'decoder_hq': decoder_hq, 'w_sim': w_sim, 'b_sim': b_sim, 'W_qv': W_qv, 'b_qv': b_qv}
    _L0_xattn_all = _L0_xattn_setup()
    _L0_xattn_in = {k: v for k, v in _L0_xattn_all.items() if k in ('w_sim', 'b_sim', 'W_qv', 'b_qv')}
    del _L0_xattn_all

    def _L0_attn_setup():
        import jax, jax.numpy as jnp
        import numpy as np
        LN_EPS = 1e-05
        key = jax.random.key(seed)
        ks = jax.random.split(key, 7)
        B, L, D, N = (8, 512, 256, 16)
        x = jax.random.normal(ks[0], (B, L, D), jnp.float32)
        A = jax.random.normal(ks[1], (D, N, N), jnp.float32) * (0.2 / np.sqrt(N))
        Bp = jax.random.normal(ks[2], (D, N), jnp.float32)
        Cp = jax.random.normal(ks[3], (D, N), jnp.float32)
        Dp = jax.random.normal(ks[4], (D,), jnp.float32)
        Wg = jax.random.normal(ks[5], (D, D), jnp.float32) / np.sqrt(D)
        bg = jnp.zeros((D,), jnp.float32)
        gamma = jnp.ones((D,), jnp.float32)
        beta = jnp.zeros((D,), jnp.float32)
        return dict(x=x, A=A, Bp=Bp, Cp=Cp, Dp=Dp, Wg=Wg, bg=bg, gamma=gamma, beta=beta)
    _L0_attn_all = _L0_attn_setup()
    _L0_attn_in = {k: v for k, v in _L0_attn_all.items() if k in ('A', 'Bp', 'Cp', 'Dp', 'Wg', 'bg', 'gamma', 'beta')}
    del _L0_attn_all

    def _L0_ffn_setup():
        import jax, jax.numpy as jnp
        import numpy as np

        def _bitlinear(x, w_latent):
            scale = jax.lax.stop_gradient(jnp.clip(jnp.mean(jnp.abs(w_latent), axis=1, keepdims=True), 1e-05, None))
            tern = jnp.clip(jnp.round(w_latent / scale), -1.0, 1.0)
            w = w_latent + jax.lax.stop_gradient(tern - w_latent)
            return x @ (w * scale).T
        key = jax.random.key(seed)
        ks = jax.random.split(key, 6)
        dim, hidden, rank = (256, 1024, 16)
        B, S = (4, 1024)
        x = jax.random.normal(ks[0], (B, S, dim), dtype=jnp.float32)
        w_fc = 0.02 * jax.random.normal(ks[1], (hidden, dim), dtype=jnp.float32)
        w_proj = 0.02 * jax.random.normal(ks[2], (dim, hidden), dtype=jnp.float32)
        u = 0.02 * jax.random.normal(ks[3], (hidden, rank), dtype=jnp.float32)
        v = 0.02 * jax.random.normal(ks[4], (rank, dim), dtype=jnp.float32)
        fast_b = jax.random.normal(ks[5], (rank, rank), dtype=jnp.float32)
        gate = jnp.float32(0.05)
        return {'x': x, 'fast_b': fast_b, 'w_fc': w_fc, 'w_proj': w_proj, 'u': u, 'v': v, 'gate': gate}
    _L0_ffn_all = _L0_ffn_setup()
    _L0_ffn_in = {k: v for k, v in _L0_ffn_all.items() if k in ('fast_b', 'w_fc', 'w_proj', 'u', 'v', 'gate')}
    del _L0_ffn_all
    return {'x': x, 'ctx_1024': ctx_1024, 'L0_xattn_w_sim': _L0_xattn_in['w_sim'], 'L0_xattn_b_sim': _L0_xattn_in['b_sim'], 'L0_xattn_W_qv': _L0_xattn_in['W_qv'], 'L0_xattn_b_qv': _L0_xattn_in['b_qv'], 'L0_attn_A': _L0_attn_in['A'], 'L0_attn_Bp': _L0_attn_in['Bp'], 'L0_attn_Cp': _L0_attn_in['Cp'], 'L0_attn_Dp': _L0_attn_in['Dp'], 'L0_attn_Wg': _L0_attn_in['Wg'], 'L0_attn_bg': _L0_attn_in['bg'], 'L0_attn_gamma': _L0_attn_in['gamma'], 'L0_attn_beta': _L0_attn_in['beta'], 'L0_ffn_fast_b': _L0_ffn_in['fast_b'], 'L0_ffn_w_fc': _L0_ffn_in['w_fc'], 'L0_ffn_w_proj': _L0_ffn_in['w_proj'], 'L0_ffn_u': _L0_ffn_in['u'], 'L0_ffn_v': _L0_ffn_in['v'], 'L0_ffn_gate': _L0_ffn_in['gate']}

def reference(x, ctx_1024, L0_xattn_w_sim, L0_xattn_b_sim, L0_xattn_W_qv, L0_xattn_b_qv, L0_attn_A, L0_attn_Bp, L0_attn_Cp, L0_attn_Dp, L0_attn_Wg, L0_attn_bg, L0_attn_gamma, L0_attn_beta, L0_ffn_fast_b, L0_ffn_w_fc, L0_ffn_w_proj, L0_ffn_u, L0_ffn_v, L0_ffn_gate):
    import jax
    import jax.numpy as jnp

    def _L0_xattn_ref(encoder_hc, decoder_hq, w_sim, b_sim, W_qv, b_qv):
        import jax, jax.numpy as jnp
        import numpy as np
        B, L_ENC, L_DEC, D = (16, 128, 128, 256)
        d = encoder_hc.shape[-1]
        w1, w2, w3 = (w_sim[:d], w_sim[d:2 * d], w_sim[2 * d:])
        Sim = (encoder_hc @ w1)[:, :, None] + (decoder_hq @ w2)[:, None, :] + jnp.einsum('bid,bjd->bij', encoder_hc * w3, decoder_hq) + b_sim[0]
        A = jax.nn.softmax(Sim, axis=2)
        hq_hat = jnp.einsum('bij,bjd->bid', A, decoder_hq)
        Batt = jax.nn.softmax(jnp.max(Sim, axis=2), axis=1)
        hc_bar = jnp.einsum('bi,bid->bd', Batt, encoder_hc)[:, None, :]
        hc_hat = jnp.broadcast_to(hc_bar, encoder_hc.shape)
        feats = jnp.concatenate([encoder_hc, hq_hat, encoder_hc * hq_hat, encoder_hc * hc_hat], axis=-1)
        hcq = feats @ W_qv + b_qv
        return hcq

    def _L0_attn_ref(x, A, Bp, Cp, Dp, Wg, bg, gamma, beta):
        import jax, jax.numpy as jnp
        import numpy as np
        LN_EPS = 1e-05
        gate = jax.nn.sigmoid(jnp.einsum('bld,ed->ble', x, Wg) + bg)
        xg = x * gate
        Bsz, L, D = xg.shape
        N = A.shape[-1]

        def step(s, xt):
            s = jnp.einsum('bdn,dnm->bdm', s, A) + xt[..., None] * Bp
            y = jnp.einsum('bdn,dn->bd', s, Cp) + Dp * xt
            return (s, y)
        s0 = jnp.zeros((Bsz, D, N), xg.dtype)
        _, ys = jax.lax.scan(step, s0, jnp.moveaxis(xg, 1, 0))
        y = jnp.moveaxis(ys, 0, 1) + xg
        mu = jnp.mean(y, axis=-1, keepdims=True)
        var = jnp.var(y, axis=-1, keepdims=True)
        return (y - mu) * jax.lax.rsqrt(var + LN_EPS) * gamma + beta

    def _L0_ffn_ref(x, fast_b, w_fc, w_proj, u, v, gate):
        import jax, jax.numpy as jnp
        import numpy as np

        def _bitlinear(x, w_latent):
            scale = jax.lax.stop_gradient(jnp.clip(jnp.mean(jnp.abs(w_latent), axis=1, keepdims=True), 1e-05, None))
            tern = jnp.clip(jnp.round(w_latent / scale), -1.0, 1.0)
            w = w_latent + jax.lax.stop_gradient(tern - w_latent)
            return x @ (w * scale).T
        h = _bitlinear(x, w_fc) + gate * (x @ v.T @ fast_b.T @ u.T)
        r = jnp.maximum(h, 0.0)
        return _bitlinear(r * r, w_proj)
    x = x + _L0_xattn_ref(_layernorm(x, axis=-1), ctx_1024, L0_xattn_w_sim, L0_xattn_b_sim, L0_xattn_W_qv, L0_xattn_b_qv)
    x = x + _L0_attn_ref(_layernorm(x, axis=-1), L0_attn_A, L0_attn_Bp, L0_attn_Cp, L0_attn_Dp, L0_attn_Wg, L0_attn_bg, L0_attn_gamma, L0_attn_beta)
    x = x + _L0_ffn_ref(_layernorm(x, axis=-1), L0_ffn_fast_b, L0_ffn_w_fc, L0_ffn_w_proj, L0_ffn_u, L0_ffn_v, L0_ffn_gate)
    return x

_drawn_inputs = setup_inputs


def setup_inputs(seed=0):
    import zlib

    import numpy as np

    out = dict(_drawn_inputs(seed))
    spreads = {'L0_attn_bg': (0.0, 0.337), 'L0_attn_gamma': (1.0, 0.2), 'L0_attn_beta': (0.0, 0.1)}
    factors = {'L0_xattn_b_qv': 2.827,
     'L0_ffn_fast_b': 8.0,
     'L0_ffn_w_fc': 2.922,
     'L0_ffn_u': 8.0,
     'L0_ffn_v': 8.0}
    for name, (base, spread) in spreads.items():
        noise = np.random.default_rng([zlib.crc32(name.encode()), seed]).standard_normal(out[name].shape)
        drawn = base * np.exp(spread * noise) if base else spread * noise
        out[name] = jnp.asarray(drawn.astype(out[name].dtype))
    for name, factor in factors.items():
        out[name] = (out[name] * factor).astype(out[name].dtype)
    return out
```

```python
from contextlib import ExitStack

import numpy as np

import concourse.bass as bass
from concourse import mybir

F32 = mybir.dt.float32
F32R = mybir.dt.float32r
ALU = mybir.AluOpType
ACT = mybir.ActivationFunctionType
AX = mybir.AxisListType

P = 128
EPS = 1e-5


def at_least(eng, sem, count):
    if isinstance(count, int) and count <= 0:
        return
    eng.wait_ge(sem, count)


def known(eng, count):
    return count if isinstance(count, int) else eng.snap(eng.to_reg(count))


def own_waits(eng, ident_made):
    eng.wait_ge(ident_made, 2)


def perceiver_layer(nc, x, ctx, w_sim, b_sim, W_qv, b_qv, A, Bp, Cp, Dp, Wg, bg, gamma, beta,
                    fast_b, w_fc, w_proj, u, v, gate, out):
    BATCH, L, D = x.shape
    J = ctx.shape[1]
    JT = (J - 1) // P
    KD = D // P
    NB = P // L
    GROUPS = BATCH // NB
    N = A.shape[1]
    HID = w_fc.shape[0]
    MT = HID // P
    RANK = u.shape[1]
    CQ = D // NB
    CH = 4
    TOK = CH * P
    CHUNKS = GROUPS // CH
    LAG = L - 1
    assert (L, NB, KD, JT, J) == (32, 4, 2, 2, 257) and D == W_qv.shape[1]

    x_tok = x.rearrange("b t d -> (b t) d")
    out_tok = out.rearrange("b t d -> (b t) d")
    gated_dram = nc.dram_tensor("gated_tokens", [BATCH * L, D], F32, kind="Internal").ap()
    scan_dram = nc.dram_tensor("scan_tokens", [BATCH * L, D], F32, kind="Internal").ap()
    impulse_dram = nc.dram_tensor("impulse", [D, L, 2 * L], F32, kind="Internal").ap()

    def row(vector):
        return vector.rearrange("(a n) -> a n", a=1)

    def everywhere(vector):
        return bass.AP(tensor=vector.tensor, offset=vector.offset, ap=[[0, P]] + [list(d) for d in vector.ap])

    with ExitStack() as whole:
        def sb(name, shape, dt=F32, scope=whole):
            return scope.enter_context(nc.sbuf_tensor(name, shape, dt))

        def ps(name, scope, shape=(P, 512)):
            return scope.enter_context(nc.psum_tensor(name, list(shape), F32))

        def sem(name):
            return whole.enter_context(nc.semaphore(name))

        resid = sb("resid", [P, GROUPS, D])
        scan_x = sb("scan_x", [P, BATCH, CQ])
        toeplitz = sb("toeplitz", [P, CQ, P])
        ident = sb("ident", [P, P])
        fc_T = sb("fc_T", [P, KD, HID], F32R)
        proj_T = sb("proj_T", [P, MT, D], F32R)
        fc_scale = sb("fc_scale", [P, MT])
        proj_scale = sb("proj_scale", [P, KD])
        low_in = sb("low_in", [P, KD, P], F32R)
        low_out = sb("low_out", [P, HID], F32R)
        minus_lo = sb("minus_lo", [P, 1])
        neg_half = sb("neg_half", [P, 4])
        gamma_all = sb("gamma_all", [P, D])

        ident_made = sem("ident_made")
        scan_loaded = sem("scan_loaded")
        toeplitz_loaded = sem("toeplitz_loaded")

        with ExitStack() as one:
            s1 = one
            ctxn = [sb(f"ctxn{p}", [P, NB, JT, D], scope=s1) for p in range(2)]
            ctx_end = [sb(f"ctx_end{p}", [P, D], scope=s1) for p in range(2)]
            ctxT = sb("ctxT", [P, NB, KD, J], scope=s1)
            ends = sb("ends", [P, D], scope=s1)
            endsT = sb("endsT", [P, KD, BATCH], scope=s1)
            wqv = sb("wqv", [P, 4 * KD, D], scope=s1)
            wg_in = sb("wg_in", [P, KD, D], scope=s1)
            wgT = sb("wgT", [P, KD, D], scope=s1)
            w1_all = sb("w1_all", [P, D], scope=s1)
            bqv_all = sb("bqv_all", [P, D], scope=s1)
            bg_all = sb("bg_all", [P, D], scope=s1)
            beta_all = sb("beta_all", [P, D], scope=s1)
            w23 = sb("w23", [P, 2, KD], scope=s1)
            bsim_all = sb("bsim_all", [P, 1], scope=s1)
            same_batch = sb("same_batch", [P, P], scope=s1)
            hc = [sb(f"hc{p}", [P, D], scope=s1) for p in range(2)]
            hc_probT = [sb(f"hc_probT{p}", [P, 2, 2, P], scope=s1) for p in range(2)]
            hcwT = sb("hcwT", [P, KD, P], scope=s1)
            prob = [sb(f"prob{p}", [P, J], scope=s1) for p in range(2)]
            pick = sb("pick", [P, P], scope=s1)
            hq = sb("hq", [P, D], scope=s1)
            hb = sb("hb", [P, D], scope=s1)
            hqbT = sb("hqbT", [P, 2, KD, P], scope=s1)
            hcqT = sb("hcqT", [P, KD, P], scope=s1)
            z = sb("z", [P, D], scope=s1)
            zT = sb("zT", [P, KD, P], scope=s1)
            gate_in = sb("gate_in", [P, D], scope=s1)
            gate_th = sb("gate_th", [P, D], scope=s1)
            gated = [sb(f"gated{p}", [P, D], scope=s1) for p in range(2)]
            dots = sb("dots", [P, D], scope=s1)
            bn1 = sb("bn1", [P, 6], scope=s1)
            mv1 = sb("mv1", [P, 2], scope=s1)
            ve1 = sb("ve1", [P, 1], scope=s1)
            rstd1 = sb("rstd1", [P, 1], scope=s1)
            bn2 = sb("bn2", [P, 6], scope=s1)
            mv2 = sb("mv2", [P, 2], scope=s1)
            ve2 = sb("ve2", [P, 1], scope=s1)
            rstd2 = sb("rstd2", [P, 1], scope=s1)
            s1_b = [sb(f"s1_b{p}", [P, 1], scope=s1) for p in range(2)]
            s1_dot = sb("s1_dot", [P, 1], scope=s1)
            neg_max = sb("neg_max", [P, 1], scope=s1)
            row_sum = sb("row_sum", [P, 1], scope=s1)
            row_rec = sb("row_rec", [P, 1], scope=s1)
            best = sb("best", [P, 1], scope=s1)
            bestT = sb("bestT", [P, L], scope=s1)
            neg_top = sb("neg_top", [P, 1], scope=s1)
            top_e = sb("top_e", [P, 1], scope=s1)
            top_eT = sb("top_eT", [P, L], scope=s1)
            top_sum = sb("top_sum", [P, 1], scope=s1)
            top_rec = sb("top_rec", [P, 1], scope=s1)
            a_sb = sb("a_sb", [P, KD, N * N], scope=s1)
            states = sb("states", [P, KD, L + 1, N], scope=s1)
            c_sb = sb("c_sb", [P, KD, N], scope=s1)
            d_sb = sb("d_sb", [P, KD], scope=s1)
            v_next = sb("v_next", [P, KD, N, N], scope=s1)
            v_new = sb("v_new", [P, KD, N], scope=s1)
            impulse = sb("impulse_sb", [P, KD, 2 * L], scope=s1)

            turn_ps = [ps(f"turn_ps{i}", s1) for i in range(2)]
            score_ps = ps("score_ps", s1)
            side_ps = ps("side_ps", s1)
            att_ps = ps("att_ps", s1)
            feat_ps = ps("feat_ps", s1)
            qv_ps = ps("qv_ps", s1)
            gate_ps = ps("gate_ps", s1)

            consts_loaded = sem("consts_loaded")
            late_loaded = sem("late_loaded")
            states_in = sem("states_in")
            x_loaded = [sem(f"x_loaded{p}") for p in range(2)]
            ctx_loaded = [sem(f"ctx_loaded{p}") for p in range(2)]
            end_loaded = [sem(f"end_loaded{p}") for p in range(2)]
            gated_stored = [sem(f"gated_stored{p}") for p in range(2)]
            masks_made = sem("masks_made")
            zeroed = sem("zeroed")
            wg_turned = sem("wg_turned")
            wgT_ready = sem("wgT_ready")
            ends_turned = sem("ends_turned")
            endsT_ready = sem("endsT_ready")
            bn1_done, mv1_done, ve1_done, rstd1_done = (sem(n) for n in ("bn1_done", "mv1_done", "ve1_done", "rstd1_done"))
            bn2_done, mv2_done, ve2_done, rstd2_done = (sem(n) for n in ("bn2_done", "mv2_done", "ve2_done", "rstd2_done"))
            hc_ready = sem("hc_ready")
            dot_done = sem("dot_done")
            s1_ready = sem("s1_ready")
            bqv_added = sem("bqv_added")
            side_turned = sem("side_turned")
            side_copied = sem("side_copied")
            hcwT_ready = sem("hcwT_ready")
            ctx_turned = sem("ctx_turned")
            ctxT_copied = sem("ctxT_copied")
            end_placed = sem("end_placed")
            scored = sem("scored")
            neg_max_ready = sem("neg_max_ready")
            best_ready = sem("best_ready")
            bestT_ready = sem("bestT_ready")
            neg_top_ready = sem("neg_top_ready")
            exp_done = sem("exp_done")
            row_rec_ready = sem("row_rec_ready")
            prob_ready = sem("prob_ready")
            top_done = sem("top_done")
            top_rec_ready = sem("top_rec_ready")
            pick_ready = sem("pick_ready")
            pooled = sem("pooled")
            attended = sem("attended")
            hq_ready = sem("hq_ready")
            hb_ready = sem("hb_ready")
            hqb_turned = sem("hqb_turned")
            hqbT_ready = sem("hqbT_ready")
            hcqT_ready = sem("hcqT_ready")
            projected = sem("projected")
            x1_ready = sem("x1_ready")
            z_ready = sem("z_ready")
            beta_added = sem("beta_added")
            z_turned = sem("z_turned")
            zT_ready = sem("zT_ready")
            gate_summed = sem("gate_summed")
            gate_in_ready = sem("gate_in_ready")
            tanh_done = sem("tanh_done")
            gated_ready = sem("gated_ready")
            v_next_ready = sem("v_next_ready")
            v_new_ready = sem("v_new_ready")
            state_kept = sem("state_kept")
            imp_dot = sem("imp_dot")
            imp_sum = sem("imp_sum")
            imp_first = sem("imp_first")
            impulse_ready = sem("impulse_ready")
            impulse_stored = sem("impulse_stored")

            CONSTS = 4
            LATE = 7
            STATE_LOADS = 4
            STEPS = 2
            STATE_START = 2
            STATE_END = STATE_START + L // STEPS
            FIRST = 4

            def software_pipeline(eng, step, between):
                for i in range(FIRST):
                    step(i, 0, range(STEPS) if i >= STATE_START else ())
                with eng.Fori(FIRST // 2, STATE_END // 2) as pair:
                    for k in range(2):
                        step(pair * 2, k, range(STEPS))
                between()
                with eng.Fori(STATE_END // 2, GROUPS // 2 - 1) as pair:
                    for k in range(2):
                        step(pair * 2, k, ())
                for i in range(GROUPS - 2, GROUPS + 2):
                    step(i, 0, ())

            def stages(base, k):
                g = base + k
                if isinstance(g, int):
                    return g, g % 2, g < GROUPS, 1 <= g <= GROUPS, g >= 2
                return g, k, True, True, True

            def min_groups(g):
                return min(g, GROUPS) if isinstance(g, int) else g

            def sixteen(base, k, back):
                if isinstance(base, int):
                    return 16 * ((base + k - back) // 2 + 1)
                return base * 8 + 16 * ((k - back) // 2 + 1)

            block = one.enter_context(nc.Block())

            @block.sync
            def _(sp):
                def load_x(g, p):
                    sp.dma_start(resid[:, bass.ds(g, 1), :].rearrange("p a d -> p (a d)"),
                                 x_tok[bass.ds(g * P, P), :]).then_inc(x_loaded[p], 16)

                def load_ctx(g, p):
                    sp.dma_start(ctxn[p][:, :, :, :],
                                 ctx[bass.ds(g * NB, NB), 0:J - 1, :].rearrange("b (q t) d -> q b t d", t=JT)
                                 ).then_inc(ctx_loaded[p], 16)

                def load_end(g, p):
                    rows = ctx[bass.ds(g * NB, NB), J - 1, :]
                    src = bass.AP(tensor=rows.tensor, offset=rows.offset, ap=[[J * D, NB], [0, L], [1, D]])
                    sp.dma_start(ctx_end[p][:, :], src).then_inc(end_loaded[p], 16)

                load_x(0, 0)
                load_ctx(0, 0)
                sp.dma_start(ends[:, :], ctx[:, J - 1, :]).then_inc(consts_loaded, 16)
                sp.dma_start(w23[:, :, :], bass.AP(tensor=w_sim.tensor, offset=D, ap=[[1, P], [D, 2], [P, KD]]),
                             allow_slow_non_contiguous=True).then_inc(consts_loaded, 16)
                sp.dma_start(w1_all[:, :], everywhere(w_sim[0:D])).then_inc(consts_loaded, 16)
                sp.dma_start(bsim_all[:, :], everywhere(b_sim)).then_inc(consts_loaded, 16)
                load_end(0, 0)
                load_x(1, 1)
                load_ctx(1, 1)
                load_end(1, 1)
                sp.dma_start(wqv[:, :, :], W_qv.rearrange("(k p) n -> p k n", p=P)).then_inc(late_loaded, 16)
                sp.dma_start(wg_in[:, :, :], Wg.rearrange("(k p) n -> p k n", p=P)).then_inc(late_loaded, 16)
                sp.dma_start(bqv_all[:, :], everywhere(b_qv)).then_inc(late_loaded, 16)
                sp.dma_start(bg_all[:, :], everywhere(bg)).then_inc(late_loaded, 16)
                sp.dma_start(beta_all[:, :], everywhere(beta)).then_inc(late_loaded, 16)
                sp.dma_start(gamma_all[:, :], everywhere(gamma)).then_inc(late_loaded, 16)
                sp.dma_start(d_sb[:, :], Dp.rearrange("(k p) -> p k", p=P),
                             allow_slow_non_contiguous=True).then_inc(late_loaded, 16)
                sp.dma_start(a_sb[:, :, :], A.rearrange("(k p) n m -> p k (n m)", p=P)).then_inc(states_in, 16)
                sp.dma_start(v_new[:, :, :], Bp.rearrange("(k p) n -> p k n", p=P)).then_inc(states_in, 16)
                sp.dma_start(states[:, :, 0, :], Bp.rearrange("(k p) n -> p k n", p=P)).then_inc(states_in, 16)
                sp.dma_start(c_sb[:, :, :], Cp.rearrange("(k p) n -> p k n", p=P)).then_inc(states_in, 16)

                def scan_load(first_group, groups):
                    for q in range(NB):
                        rows = gated_dram[bass.ds(first_group * P, groups * P), :]
                        src = bass.AP(tensor=rows.tensor, offset=rows.offset + q * CQ,
                                      ap=[[D, L], [L * D, groups * NB], [1, CQ]])
                        sp.dma_start(scan_x[q * L:(q + 1) * L, bass.ds(first_group * NB, groups * NB), :],
                                     src).then_inc(scan_loaded, 16)

                def step(base, k, _):
                    g, p, has_a, has_b, has_c = stages(base, k)
                    inside = not isinstance(g, int)
                    if inside or g + 2 < GROUPS:
                        at_least(sp, hc_ready, g + 1)
                        load_x(g + 2, p)
                        at_least(sp, attended, g + 1)
                        load_ctx(g + 2, p)
                        at_least(sp, hq_ready, g + 1)
                        load_end(g + 2, p)
                    if has_c:
                        at_least(sp, gated_ready, g - 1)
                        sp.dma_start(gated_dram[bass.ds((g - 2) * P, P), :], gated[p][:, :]
                                     ).then_inc(gated_stored[p], 16)

                for i in range(2):
                    step(i, 0, ())

                def body(base):
                    step(base, 0, ())
                    step(base, 1, ())
                    sp.wait_ge(gated_stored[0], base * 8)
                    sp.wait_ge(gated_stored[1], base * 8)
                    scan_load(base - 2, 2)

                body(2)
                with sp.Fori(FIRST // 2, STATE_END // 2) as pair:
                    body(pair * 2)
                sp.wait_ge(impulse_ready, 1)
                for c in range(KD):
                    sp.dma_start(impulse_dram[c * P:(c + 1) * P, :, :],
                                 impulse[:, c, :].unsqueeze(1).broadcast_to([P, L, 2 * L])).then_inc(impulse_stored, 16)
                sp.wait_ge(impulse_stored, 16 * KD)
                sp.wait_ge(zeroed, FIRST)
                for q in range(NB):
                    src = bass.AP(tensor=impulse_dram.tensor, offset=q * CQ * L * 2 * L + LAG,
                                  ap=[[2 * L - 1, L], [L * 2 * L, CQ], [1, L]])
                    sp.dma_start(toeplitz[q * L:(q + 1) * L, :, q * L:(q + 1) * L], src
                                 ).then_inc(toeplitz_loaded, 16)
                with sp.Fori(STATE_END // 2, GROUPS // 2 - 1) as pair:
                    body(pair * 2)
                for i in range(GROUPS - 2, GROUPS, 2):
                    step(i, 0, ())
                    step(i + 1, 0, ())
                    sp.wait_ge(gated_stored[0], i * 8)
                    sp.wait_ge(gated_stored[1], i * 8)
                    scan_load(i - 2, 2)
                for i in range(GROUPS, GROUPS + 2):
                    step(i, 0, ())
                    sp.wait_ge(gated_stored[i % 2], 16 * (GROUPS // 2))
                    scan_load(i - 2, 1)

            @block.tensor
            def _(pe):
                pe.wait_ge(ident_made, 2)

                def turn_context(g, p, b):
                    at_least(pe, ctxT_copied, g * 4 + b - 1)
                    for c in range(KD):
                        for t in range(JT):
                            mm = pe.transpose(turn_ps[b % 2][:, (c * JT + t) * P:(c * JT + t + 1) * P],
                                              ctxn[p][:, b, t, c * P:(c + 1) * P], ident[:, :])
                    mm.then_inc(ctx_turned, 1)

                def step(base, k, _):
                    g, p, has_a, has_b, has_c = stages(base, k)
                    o = 1 - p
                    if has_a or has_b:
                        at_least(pe, side_copied, g)
                        if has_a:
                            at_least(pe, hc_ready, g + 1)
                            for c in range(KD):
                                mm = pe.transpose(side_ps[:, c * P:(c + 1) * P], hc[p][:, c * P:(c + 1) * P], ident[:, :])
                        if has_b:
                            at_least(pe, prob_ready, g)
                            for t in range(JT):
                                mm = pe.transpose(side_ps[:, 256 + t * P:256 + (t + 1) * P],
                                                  prob[o][:, t * P:(t + 1) * P], ident[:, :])
                        mm.then_inc(side_turned, 1)
                    if has_b:
                        at_least(pe, pick_ready, g)
                        at_least(pe, gate_in_ready, g - 2)
                        pe.matmul(gate_ps[:, 256:256 + D], pick[:, :], hc[o][:, :], start=True, stop=True
                                  ).then_inc(pooled, 1)
                    if has_a:
                        at_least(pe, ctx_loaded[p], sixteen(base, k, 0))
                        turn_context(g, p, 0)
                        turn_context(g, p, 1)
                    if has_b:
                        at_least(pe, side_copied, g + 1)
                        at_least(pe, hq_ready, g - 1)
                        for t in range(JT):
                            for b in range(NB):
                                mm = pe.matmul(att_ps[b * L:(b + 1) * L, 0:D], hc_probT[p][:, 1, t, b * L:(b + 1) * L],
                                               ctxn[o][:, b, t, :], start=(t == 0), stop=(t == JT - 1))
                        mm.then_inc(attended, 1)
                    if has_a:
                        turn_context(g, p, 2)
                        turn_context(g, p, 3)
                    if has_c:
                        at_least(pe, z_ready, g - 1)
                        at_least(pe, x1_ready, g - 1)
                        for c in range(KD):
                            mm = pe.transpose(qv_ps[:, 256 + c * P:256 + (c + 1) * P], z[:, c * P:(c + 1) * P],
                                              ident[:, :])
                        mm.then_inc(z_turned, 1)
                    if has_b:
                        if isinstance(g, int) and g == 1:
                            pe.wait_ge(endsT_ready, 1)
                        at_least(pe, hqbT_ready, g - 1)
                        for i, (part, ready) in enumerate(((hb, hb_ready), (hq, hq_ready))):
                            at_least(pe, ready, g)
                            for c in range(KD):
                                mm = pe.transpose(feat_ps[:, ((1 - i) * KD + c) * P:((1 - i) * KD + c + 1) * P],
                                                  part[:, c * P:(c + 1) * P], ident[:, :])
                        mm.then_inc(hqb_turned, 1)
                    if has_a:
                        at_least(pe, ctxT_copied, g * 4 + 4)
                        at_least(pe, end_placed, g + 1)
                        at_least(pe, hcwT_ready, g + 1)
                        at_least(pe, neg_max_ready, g)
                        at_least(pe, exp_done, g)
                        for c in range(KD):
                            for b in range(NB):
                                mm = pe.matmul(score_ps[b * L:(b + 1) * L, 0:J], hcwT[:, c, b * L:(b + 1) * L],
                                               ctxT[:, b, c, :], start=(c == 0), stop=(c == KD - 1))
                        mm.then_inc(scored, 1)
                    if has_c:
                        at_least(pe, zT_ready, g - 1)
                        at_least(pe, hb_ready, min_groups(g))
                        for c in range(KD):
                            mm = pe.matmul(gate_ps[:, 0:D], zT[:, c, :], wgT[:, c, :], start=(c == 0), stop=(c == KD - 1))
                        mm.then_inc(gate_summed, 1)
                    if has_b:
                        if has_c:
                            at_least(pe, zT_ready, g - 1)
                        feats = (hc_probT[o][:, 0], hqbT[:, 1], hqbT[:, 0], hcqT)
                        rows = (0, 3, 1, 2)
                        for f in range(4):
                            if f == 1:
                                at_least(pe, hqbT_ready, g)
                            if f == 3:
                                at_least(pe, hcqT_ready, g)
                            for c in range(KD):
                                mm = pe.matmul(qv_ps[:, 0:D], feats[f][:, c, :], wqv[:, rows[f] * KD + c, :],
                                               start=(f == 0 and c == 0), stop=(f == 3 and c == KD - 1))
                        mm.then_inc(projected, 1)
                    if isinstance(g, int) and g == 0:
                        pe.wait_ge(late_loaded, 16 * LATE)
                        for e in range(KD):
                            for c in range(KD):
                                mm = pe.transpose(gate_ps[:, (c * KD + e) * P:(c * KD + e + 1) * P],
                                                  wg_in[:, e, c * P:(c + 1) * P], ident[:, :])
                        mm.then_inc(wg_turned, 1)
                        pe.wait_ge(wgT_ready, 1)

                pe.wait_ge(consts_loaded, 16 * CONSTS)
                for c in range(KD):
                    mm = pe.transpose(feat_ps[:, c * P:(c + 1) * P], ends[:, c * P:(c + 1) * P], ident[:, :])
                mm.then_inc(ends_turned, 1)
                software_pipeline(pe, step, lambda: None)

            @block.scalar
            def _(act):
                act.wait_ge(ends_turned, 1)
                act.copy(endsT[:, :, :], feat_ps[:, 0:KD * BATCH].rearrange("p (k b) -> p k b", k=KD)).then_inc(endsT_ready, 1)

                act.wait_ge(consts_loaded, 16 * CONSTS)

                def step(base, k, _):
                    g, p, has_a, has_b, has_c = stages(base, k)
                    o = 1 - p
                    if has_a or has_b:
                        at_least(act, side_turned, g + 1)
                        at_least(act, projected, g - 1)
                        at_least(act, hcqT_ready, g - 1)
                        at_least(act, attended, g - 2)
                        first, last = (0 if has_a else 1), (2 if has_b else 1)
                        act.copy(hc_probT[p][:, first:last, :, :],
                                 side_ps[:, first * 256:last * 256].rearrange("p (f k t) -> p f k t", f=last - first, k=2)
                                 ).then_inc(side_copied, 1)
                    if has_a:
                        at_least(act, scored, g)
                        for b in range(NB):
                            at_least(act, ctx_turned, g * 4 + b + 1)
                            act.copy(ctxT[:, b, :, 0:J - 1], turn_ps[b % 2][:, :].rearrange("p (k j) -> p k j", k=KD)
                                     ).then_inc(ctxT_copied, 1)
                            if b == 1:
                                at_least(act, side_copied, g + 1)
                                for c in range(KD):
                                    ins = act.activation(hcwT[:, c, :], hc_probT[p][:, 0, c, :], ACT.Identity,
                                                         bias=w23[:, 0, c:c + 1], scale=w23[:, 1, c:c + 1])
                                ins.then_inc(hcwT_ready, 1)
                    if has_c:
                        at_least(act, z_turned, g - 1)
                        at_least(act, gate_summed, g - 2)
                        act.copy(zT[:, :, :], qv_ps[:, 256:256 + D].rearrange("p (k t) -> p k t", k=KD)).then_inc(zT_ready, 1)
                    if has_b:
                        at_least(act, hqb_turned, g)
                        at_least(act, projected, g - 1)
                        at_least(act, hcqT_ready, g - 1)
                        act.copy(hqbT[:, :, :, :], feat_ps[:, :].rearrange("p (f k t) -> p f k t", f=2, k=KD)
                                 ).then_inc(hqbT_ready, 1)
                    if has_a:
                        at_least(act, neg_max_ready, g + 1)
                        at_least(act, scored, g + 1)
                        at_least(act, side_turned, g)
                        at_least(act, hq_ready, g - 1)
                        at_least(act, row_rec_ready, g)
                        act.activation(prob[p][:, :], score_ps[:, 0:J], ACT.Exp, bias=neg_max[:, 0:1],
                                       accum_out=row_sum[:, 0:1]).then_inc(exp_done, 1)
                    if has_c:
                        at_least(act, gate_in_ready, g - 1)
                        at_least(act, gated_ready, g - 2)
                        act.activation(gate_th[:, :], gate_in[:, :], ACT.Tanh, scale=0.5).then_inc(tanh_done, 1)
                    if has_a:
                        at_least(act, neg_top_ready, g + 1)
                        at_least(act, pick_ready, g)
                        act.activation(top_e[:, :], best[:, :], ACT.Exp, bias=neg_top[:, 0:1])
                        at_least(act, top_done, g)
                        act.activation(top_eT[:, :], bestT[:, :], ACT.Exp, bias=neg_top[:, 0:1],
                                       accum_out=top_sum[:, 0:1]).then_inc(top_done, 1)
                    if isinstance(g, int) and g == 0:
                        act.wait_ge(wg_turned, 1)
                        act.copy(wgT[:, :, :], gate_ps[:, :].rearrange("p (k e) -> p k e", k=KD)).then_inc(wgT_ready, 1)

                software_pipeline(act, step, lambda: None)

            @block.gpsimd
            def _(pool):
                pool.memset(ident[:, :], 0.0).then_inc(ident_made, 1)
                pool.memset(neg_half[:, :], -0.5)
                pool.memset(same_batch[:, :], 0.0).then_inc(masks_made, 1)
                pool.wait_ge(ident_made, 1)
                pool.affine_select(out=ident[:, :], in_=ident[:, :], compare_op=ALU.not_equal, fill=1.0, base=0,
                                   pattern=[[-1, P]], channel_multiplier=1).then_inc(ident_made, 1)
                pool.wait_ge(masks_made, 1)
                pool.wait_ge(ident_made, 2)
                for b in range(NB):
                    last = pool.memset(same_batch[b * L:(b + 1) * L, b * L:(b + 1) * L], 1.0)
                last.then_inc(masks_made, 1)
                pool.wait_ge(masks_made, 2)

                def inverse_deviation(dst, src, ready, made, count):
                    at_least(pool, ready, count)
                    pool.tensor_tensor(dst, src, neg_half[:, 0:1], ALU.pow).then_inc(made, 1)

                def state_product(count):
                    at_least(pool, v_new_ready, count)
                    pool.tensor_tensor(v_next[:, :, :, :].rearrange("p k m n -> p k m n"),
                                       a_sb[:, :, :].rearrange("p k (n m) -> p k m n", n=N),
                                       v_new[:, :, :].unsqueeze(2).broadcast_to([P, KD, N, N]),
                                       ALU.mult).then_inc(v_next_ready, 1)

                def step(base, k, state_steps):
                    g, p, has_a, has_b, has_c = stages(base, k)
                    inside = not isinstance(g, int)
                    if has_a:
                        if not inside and g == 0:
                            pool.wait_ge(endsT_ready, 1)
                        at_least(pool, scored, g)
                        pool.tensor_copy(ctxT[:, :, :, J - 1],
                                         endsT[:, :, bass.ds(g * NB, NB)].rearrange("p k b -> p b k")
                                         ).then_inc(end_placed, 1)
                    if has_c:
                        at_least(pool, z_ready, g - 2)
                        inverse_deviation(rstd2[:, :], ve2[:, :], ve2_done, rstd2_done, g - 1)
                    for s in state_steps:
                        state_product((base - STATE_START + k) * STEPS + s)
                        if s == 0:
                            break
                    if inside or g + 1 < GROUPS:
                        at_least(pool, hc_ready, g + 1)
                        inverse_deviation(rstd1[:, :], ve1[:, :], ve1_done, rstd1_done, g + 2)
                    if has_c:
                        at_least(pool, z_ready, g - 1)
                        r = resid[:, bass.ds(g - 2, 1), :].rearrange("p a d -> p (a d)")
                        pool.tensor_tensor(r, r, beta_all[:, :], ALU.add).then_inc(beta_added, 1)
                    for s in list(state_steps)[1:]:
                        state_product((base - STATE_START + k) * STEPS + s)
                    if inside or g + 1 < GROUPS:
                        add_bqv(g + 1)
                    if not inside and g < FIRST:
                        part = CQ // FIRST
                        pool.memset(toeplitz[:, g * part:(g + 1) * part, :], 0.0).then_inc(zeroed, 1)

                def add_bqv(g):
                    at_least(pool, hc_ready, g + 1)
                    r = resid[:, bass.ds(g, 1), :].rearrange("p a d -> p (a d)")
                    pool.tensor_tensor(r, r, bqv_all[:, :], ALU.add).then_inc(bqv_added, 1)

                inverse_deviation(rstd1[:, :], ve1[:, :], ve1_done, rstd1_done, 1)
                pool.memset(impulse[:, :, :], 0.0)
                pool.wait_ge(late_loaded, 16 * LATE)
                add_bqv(0)
                pool.wait_ge(states_in, 16 * STATE_LOADS)
                software_pipeline(pool, step, lambda: None)

            @block.vector
            def _(dve):
                def layer_norm1(g, p, count):
                    count = known(dve, count)
                    after = known(dve, count + 1)
                    own_waits(dve, ident_made)
                    at_least(dve, mv1_done, count)
                    dve.bn_stats(bn1[:, :], resid[:, bass.ds(g, 1), :].rearrange("p a d -> p (a d)")).then_inc(bn1_done, 1)
                    own_waits(dve, ident_made)
                    at_least(dve, bn1_done, after)
                    at_least(dve, hc_ready, count)
                    dve.bn_aggr(mv1[:, :], bn1[:, :]).then_inc(mv1_done, 1)
                    at_least(dve, mv1_done, after)
                    at_least(dve, rstd1_done, count)
                    dve.tensor_scalar(ve1[:, :], mv1[:, 1:2], EPS, None, ALU.add).then_inc(ve1_done, 1)

                def normalise1(g, p, count):
                    at_least(dve, rstd1_done, count + 1)
                    at_least(dve, pooled, count - 1)
                    at_least(dve, hb_ready, count - 1)
                    at_least(dve, side_turned, count - 1)
                    at_least(dve, dot_done, count)
                    at_least(dve, s1_ready, count)
                    dve.tensor_scalar(hc[p][:, :], resid[:, bass.ds(g, 1), :].rearrange("p a d -> p (a d)"),
                                      mv1[:, 0:1], rstd1[:, 0:1], ALU.subtract, ALU.mult).then_inc(hc_ready, 1)
                    at_least(dve, hc_ready, count + 1)
                    dve.tensor_tensor_reduce(out=dots[:, :], in0=hc[p][:, :], in1=w1_all[:, :], scale=1.0, scalar=0.0,
                                             op0=ALU.mult, op1=ALU.add, accum_out=s1_dot[:, :]).then_inc(dot_done, 1)
                    at_least(dve, dot_done, count + 1)
                    at_least(dve, best_ready, count - 1)
                    dve.tensor_scalar(s1_b[p][:, :], s1_dot[:, :], bsim_all[:, 0:1], None, ALU.add).then_inc(s1_ready, 1)

                def state_sum(count):
                    at_least(dve, v_next_ready, count + 1)
                    at_least(dve, state_kept, count)
                    dve.tensor_reduce(v_new[:, :, :], v_next[:, :, :, :], AX.X, ALU.add).then_inc(v_new_ready, 1)

                def state_keep(count):
                    at_least(dve, v_new_ready, count + 1)
                    dve.tensor_copy(states[:, :, bass.ds(count + 1, 1), :].rearrange("p k a n -> p k (a n)"),
                                    v_new[:, :, :]).then_inc(state_kept, 1)

                def step(base, k, state_steps):
                    g, p, has_a, has_b, has_c = stages(base, k)
                    inside = not isinstance(g, int)
                    o = 1 - p
                    if has_c:
                        at_least(dve, projected, g - 1)
                        at_least(dve, bqv_added, g - 1)
                        r = resid[:, bass.ds(g - 2, 1), :].rearrange("p a d -> p (a d)")
                        dve.tensor_tensor(r, qv_ps[:, 0:D], r, ALU.add).then_inc(x1_ready, 1)
                        done, before = known(dve, g - 1), known(dve, g - 2)
                        own_waits(dve, ident_made)
                        at_least(dve, x1_ready, done)
                        at_least(dve, mv2_done, before)
                        dve.bn_stats(bn2[:, :], r).then_inc(bn2_done, 1)
                        own_waits(dve, ident_made)
                        at_least(dve, bn2_done, done)
                        at_least(dve, z_ready, before)
                        dve.bn_aggr(mv2[:, :], bn2[:, :]).then_inc(mv2_done, 1)
                        at_least(dve, mv2_done, done)
                        at_least(dve, rstd2_done, g - 2)
                        dve.tensor_scalar(ve2[:, :], mv2[:, 1:2], EPS, None, ALU.add).then_inc(ve2_done, 1)
                    if has_b:
                        at_least(dve, pooled, g)
                        at_least(dve, hqb_turned, g - 1)
                        dve.tensor_tensor(hb[:, :], gate_ps[:, 256:256 + D], hc[o][:, :], ALU.mult).then_inc(hb_ready, 1)
                    if has_c:
                        at_least(dve, rstd2_done, g - 1)
                        at_least(dve, z_turned, g - 2)
                        at_least(dve, gated_ready, g - 2)
                        dve.tensor_scalar(z[:, :], r, mv2[:, 0:1], rstd2[:, 0:1], ALU.subtract, ALU.mult
                                          ).then_inc(z_ready, 1)
                    if inside or g + 1 < GROUPS:
                        at_least(dve, x_loaded[o], sixteen(base, k, -1))
                        layer_norm1(g + 1, o, g + 1)
                    if has_b:
                        at_least(dve, attended, g)
                        at_least(dve, end_loaded[o], sixteen(base, k, 1))
                        at_least(dve, hqb_turned, g - 1)
                        dve.scalar_tensor_tensor(out=hq[:, :], in0=ctx_end[o][:, :], scalar=prob[o][:, J - 1:J],
                                                 in1=att_ps[:, 0:D], op0=ALU.mult, op1=ALU.add).then_inc(hq_ready, 1)
                    for s in list(state_steps)[:1]:
                        state_sum((base - STATE_START + k) * STEPS + s)
                    if inside or g + 1 < GROUPS:
                        normalise1(g + 1, o, g + 1)
                    if has_a:
                        at_least(dve, scored, g + 1)
                        at_least(dve, exp_done, g)
                        at_least(dve, best_ready, g)
                        dve.tensor_reduce(neg_max[:, :], score_ps[:, 0:J], AX.X, ALU.max, negate=True
                                          ).then_inc(neg_max_ready, 1)
                        at_least(dve, neg_max_ready, g + 1)
                        at_least(dve, s1_ready, g + 1)
                        at_least(dve, top_done, g)
                        dve.tensor_tensor(best[:, :], s1_b[p][:, :], neg_max[:, :], ALU.subtract).then_inc(best_ready, 1)
                        at_least(dve, best_ready, g + 1)
                        dve.transpose(bestT[:, :], best[:, 0:1].broadcast_to([P, L])).then_inc(bestT_ready, 1)
                        at_least(dve, bestT_ready, g + 1)
                        dve.tensor_reduce(neg_top[:, :], bestT[:, :], AX.X, ALU.max, negate=True
                                          ).then_inc(neg_top_ready, 1)
                    if has_b:
                        at_least(dve, hqbT_ready, g)
                        at_least(dve, side_copied, g)
                        at_least(dve, projected, g - 1)
                        dve.tensor_tensor(hcqT[:, :, :], hqbT[:, 0, :, :],
                                          hc_probT[o][:, 0, :, :], ALU.mult).then_inc(hcqT_ready, 1)
                    for s in list(state_steps)[:1]:
                        state_keep((base - STATE_START + k) * STEPS + s)
                    if isinstance(g, int) and g == 2:
                        dve.wait_ge(late_loaded, 16 * LATE)
                    if has_c:
                        at_least(dve, gate_summed, g - 1)
                        at_least(dve, tanh_done, g - 2)
                        dve.tensor_tensor(gate_in[:, :], gate_ps[:, 0:D], bg_all[:, :], ALU.add).then_inc(gate_in_ready, 1)
                    if has_a:
                        at_least(dve, exp_done, g + 1)
                        at_least(dve, prob_ready, g)
                        dve.reciprocal(row_rec[:, :], row_sum[:, :]).then_inc(row_rec_ready, 1)
                        at_least(dve, row_rec_ready, g + 1)
                        dve.tensor_scalar(prob[p][:, :], prob[p][:, :], row_rec[:, 0:1], None, ALU.mult
                                          ).then_inc(prob_ready, 1)
                    for s in list(state_steps)[1:]:
                        state_sum((base - STATE_START + k) * STEPS + s)
                    if has_c:
                        at_least(dve, tanh_done, g - 1)
                        at_least(dve, gated_stored[p], sixteen(base, k, 4))
                        dve.scalar_tensor_tensor(out=gated[p][:, :], in0=gate_th[:, :], scalar=1.0, in1=z[:, :],
                                                 op0=ALU.add, op1=ALU.mult).then_inc(gated_ready, 1)
                    if has_a:
                        at_least(dve, top_done, g + 1)
                        at_least(dve, pick_ready, g)
                        dve.reciprocal(top_rec[:, :], top_sum[:, :]).then_inc(top_rec_ready, 1)
                        at_least(dve, top_rec_ready, g + 1)
                        at_least(dve, pooled, g)
                        dve.tensor_scalar(pick[:, :], same_batch[:, :], top_e[:, 0:1], top_rec[:, 0:1],
                                          ALU.mult, ALU.mult).then_inc(pick_ready, 1)
                    for s in list(state_steps)[1:]:
                        state_keep((base - STATE_START + k) * STEPS + s)

                def impulse_response():
                    dve.wait_ge(state_kept, L)
                    w = states[:, :, 0:L, :]
                    dve.tensor_tensor(w, w, c_sb[:, :, :].unsqueeze(2).broadcast_to([P, KD, L, N]), ALU.mult).then_inc(imp_dot, 1)
                    dve.wait_ge(imp_dot, 1)
                    dve.wait_ge(zeroed, FIRST)
                    dve.tensor_reduce(impulse[:, :, LAG:LAG + L], w, AX.X, ALU.add).then_inc(imp_sum, 1)
                    dve.wait_ge(imp_sum, 1)
                    dve.scalar_tensor_tensor(out=impulse[:, :, LAG], in0=d_sb[:, :], scalar=1.0, in1=impulse[:, :, LAG],
                                             op0=ALU.add, op1=ALU.add).then_inc(imp_first, 1)
                    dve.wait_ge(imp_first, 1)
                    dve.tensor_scalar(impulse[:, :, LAG:LAG + L], impulse[:, :, LAG:LAG + L], 0.5, None, ALU.mult).then_inc(impulse_ready, 1)

                dve.wait_ge(x_loaded[0], 16)
                layer_norm1(0, 0, 0)
                dve.wait_ge(consts_loaded, 16 * CONSTS)
                normalise1(0, 0, 0)
                dve.wait_ge(masks_made, 2)
                dve.wait_ge(states_in, 16 * STATE_LOADS)
                software_pipeline(dve, step, impulse_response)

        with ExitStack() as two:
            fc_in = sb("fc_in", [P, MT, D], scope=two)
            proj_in = sb("proj_in", [P, KD, HID], scope=two)
            u_in = sb("u_in", [P, MT, RANK], scope=two)
            v_in = sb("v_in", [RANK, D], scope=two)
            fbT = sb("fbT", [RANK, RANK], scope=two)
            gate_all = sb("gate_all", [P, 1], scope=two)
            below = sb("below", [P, HID], scope=two)
            thresholds = sb("thresholds", [P, 2, MT + KD], scope=two)
            u_scaled = sb("u_scaled", [P, MT, RANK], scope=two)
            u_rec = sb("u_rec", [P, MT], scope=two)
            u_hi = sb("u_hi", [P, MT, RANK], F32R, scope=two)
            u_parts = sb("u_parts", [P, MT, 4, 2, RANK], scope=two)
            c_full = sb("c_full", [P, KD, RANK], scope=two)

            scan_ps = [ps(f"scan_ps{i}", two) for i in range(4)]
            wturn_ps = [ps(f"wturn_ps{i}", two) for i in range(2)]
            low_ps = ps("low_ps", two)

            w_loaded = sem("w_loaded")
            scanned = sem("scanned")
            scan_copied = sem("scan_copied")
            sums_done = sem("sums_done")
            scales_done = sem("scales_done")
            thresholds_done = sem("thresholds_done")
            below_done = sem("below_done")
            ternary_done = sem("ternary_done")
            u_steps = sem("u_steps")
            u_done = sem("u_done")
            low_product = sem("low_product")
            c_steps = sem("c_steps")
            w_turned = sem("w_turned")
            w_copied = sem("w_copied")
            y_stored = sem("y_stored")

            BANK = 4
            W_LOADS = 6
            SCANS = CQ // BANK
            TURNS = 2 * MT * KD // BANK + MT // BANK

            block = two.enter_context(nc.Block())

            @block.sync
            def _(sp):
                sp.dma_start(fc_in[:, :, :], w_fc.rearrange("(m p) d -> p m d", p=P)).then_inc(w_loaded, 16)
                sp.dma_start(proj_in[:, :, :], w_proj.rearrange("(k p) h -> p k h", p=P)).then_inc(w_loaded, 16)
                sp.dma_start(u_in[:, :, :], u.rearrange("(m p) r -> p m r", p=P)).then_inc(w_loaded, 16)
                sp.dma_start(v_in[:, :], v).then_inc(w_loaded, 16)
                sp.dma_start(fbT[:, :], fast_b.rearrange("a b -> b a"),
                             allow_slow_non_contiguous=True).then_inc(w_loaded, 16)
                sp.dma_start(gate_all[:, :], everywhere(gate)).then_inc(w_loaded, 16)

            @block.gpsimd
            def _(pool):
                pool.memset(minus_lo[0:P // 2, :], 0.0)
                pool.memset(minus_lo[P // 2:P, :], -1.0)

            @block.tensor
            def _(pe):
                pe.wait_ge(toeplitz_loaded, 16 * NB)
                pe.wait_ge(scan_loaded, 16 * NB * (GROUPS // 2 + 1))
                for j in range(CQ):
                    bank = j // BANK
                    if j % BANK == 0:
                        at_least(pe, scan_copied, bank - 3)
                    mm = pe.matmul(scan_ps[bank % 4][:, (j % BANK) * P:(j % BANK + 1) * P], toeplitz[:, j, :],
                                   scan_x[:, :, j], start=True, stop=True)
                    if j % BANK == BANK - 1:
                        mm.then_inc(scanned, 1)
                pe.wait_ge(w_loaded, 16 * W_LOADS)
                for c in range(KD):
                    mm = pe.matmul(low_ps[:, c * RANK:(c + 1) * RANK], v_in[:, c * P:(c + 1) * P], fbT[:, :],
                                   start=True, stop=True)
                mm.then_inc(low_product, 1)
                turn = 0
                pe.wait_ge(ternary_done, MT + KD)
                for c in range(KD):
                    for m in range(MT):
                        if m % BANK == 0:
                            at_least(pe, w_copied, turn - 1)
                        mm = pe.transpose(wturn_ps[turn % 2][:, (m % BANK) * P:(m % BANK + 1) * P],
                                          fc_in[:, m, c * P:(c + 1) * P], ident[:, :])
                        if m % BANK == BANK - 1:
                            mm.then_inc(w_turned, 1)
                            turn += 1
                for m in range(0, MT, 2):
                    at_least(pe, w_copied, turn - 1)
                    for i in range(2):
                        for c in range(KD):
                            mm = pe.transpose(wturn_ps[turn % 2][:, (i * KD + c) * P:(i * KD + c + 1) * P],
                                              proj_in[:, c, (m + i) * P:(m + i + 1) * P], ident[:, :])
                    mm.then_inc(w_turned, 1)
                    turn += 1
                pe.wait_ge(u_done, 1)
                for m in range(MT):
                    if m % BANK == 0:
                        at_least(pe, w_copied, turn - 1)
                    mm = pe.transpose(wturn_ps[turn % 2][:, (m % BANK) * P:(m % BANK + 1) * P],
                                      u_parts[:, m, :, :, :].rearrange("p q h r -> p (q h r)"), ident[:, :])
                    if m % BANK == BANK - 1:
                        mm.then_inc(w_turned, 1)
                        turn += 1

            @block.scalar
            def _(act):
                for bank in range(SCANS):
                    act.wait_ge(scanned, bank + 1)
                    act.copy(scan_x[:, :, bank * BANK:(bank + 1) * BANK].rearrange("p b j -> p j b"),
                             scan_ps[bank % 4][:, :].rearrange("p (j b) -> p j b", j=BANK)).then_inc(scan_copied, 1)
                turn = 0
                for c in range(KD):
                    for half in range(MT // BANK):
                        act.wait_ge(w_turned, turn + 1)
                        act.copy(fc_T[:, c, half * 512:(half + 1) * 512], wturn_ps[turn % 2][:, :]).then_inc(w_copied, 1)
                        turn += 1
                for m in range(0, MT, 2):
                    act.wait_ge(w_turned, turn + 1)
                    act.copy(proj_T[:, m:m + 2, :].rearrange("p m d -> p (m d)"), wturn_ps[turn % 2][:, :]).then_inc(w_copied, 1)
                    turn += 1
                for half in range(MT // BANK):
                    act.wait_ge(w_turned, turn + 1)
                    act.copy(low_out[:, half * 512:(half + 1) * 512], wturn_ps[turn % 2][:, :]).then_inc(w_copied, 1)
                    turn += 1
                assert turn == TURNS

            @block.vector
            def _(dve):
                dve.wait_ge(w_loaded, 16 * W_LOADS)
                dve.tensor_reduce(fc_scale[:, :], fc_in[:, :, :], AX.X, ALU.add, apply_absolute_value=True)
                dve.tensor_reduce(proj_scale[:, :], proj_in[:, :, :], AX.X, ALU.add, apply_absolute_value=True
                                  ).then_inc(sums_done, 1)
                dve.wait_ge(sums_done, 1)
                dve.tensor_scalar(fc_scale[:, :], fc_scale[:, :], 1.0 / D, 1e-5, ALU.mult, ALU.max)
                dve.tensor_scalar(proj_scale[:, :], proj_scale[:, :], 1.0 / HID, 1e-5, ALU.mult, ALU.max
                                  ).then_inc(scales_done, 1)
                dve.wait_ge(scales_done, 1)
                for i, half in enumerate((0.5, -0.5)):
                    dve.tensor_scalar(thresholds[:, i, 0:MT], fc_scale[:, :], half, None, ALU.mult)
                    ins = dve.tensor_scalar(thresholds[:, i, MT:], proj_scale[:, :], half, None, ALU.mult)
                ins.then_inc(thresholds_done, 1)
                dve.reciprocal(u_rec[:, :], fc_scale[:, :]).then_inc(u_steps, 1)
                dve.wait_ge(thresholds_done, 1)
                for i in range(MT + KD):
                    w = fc_in[:, i, :] if i < MT else proj_in[:, i - MT, :]
                    b = below[:, 0:D] if i < MT else below[:, :]
                    at_least(dve, ternary_done, i)
                    dve.tensor_scalar(b, w, thresholds[:, 1, i:i + 1], None, ALU.is_lt).then_inc(below_done, 1)
                    dve.wait_ge(below_done, i + 1)
                    dve.scalar_tensor_tensor(out=w, in0=w, scalar=thresholds[:, 0, i:i + 1], in1=b,
                                             op0=ALU.is_gt, op1=ALU.subtract).then_inc(ternary_done, 1)
                dve.wait_ge(u_steps, 1)
                for m in range(MT):
                    ins = dve.tensor_scalar(u_scaled[:, m, :], u_in[:, m, :], u_rec[:, m:m + 1], None, ALU.mult)
                ins.then_inc(u_steps, 1)
                dve.wait_ge(u_steps, 2)
                dve.tensor_copy(u_hi[:, :, :], u_scaled[:, :, :]).then_inc(u_steps, 1)
                dve.wait_ge(u_steps, 3)
                for q in range(4):
                    for part in range(2):
                        if q % 2 == 0:
                            ins = dve.tensor_copy(u_parts[:, :, q, part, :], u_hi[:, :, :].bitcast(F32))
                        else:
                            ins = dve.tensor_tensor(u_parts[:, :, q, part, :], u_scaled[:, :, :],
                                                    u_hi[:, :, :].bitcast(F32), ALU.subtract)
                ins.then_inc(u_done, 1)
                dve.wait_ge(low_product, 1)
                dve.tensor_scalar(c_full[:, :, :], low_ps[:, 0:KD * RANK].rearrange("p (k r) -> p k r", k=KD),
                                  gate_all[:, 0:1], None, ALU.mult).then_inc(c_steps, 1)
                dve.wait_ge(c_steps, 1)
                li = low_in[:, :, :].rearrange("p k (q h r) -> p k q h r", q=4, h=2)
                for q in range(4):
                    ins = dve.tensor_copy(li[:, :, q, 0, :], c_full[:, :, :])
                ins.then_inc(c_steps, 1)
                dve.wait_ge(c_steps, 2)
                for q in range(4):
                    ins = dve.tensor_tensor(li[:, :, q, 1, :], c_full[:, :, :], li[:, :, q, 0, :].bitcast(F32), ALU.subtract)
                ins.then_inc(c_steps, 1)
                dve.wait_ge(c_steps, 3)

        with ExitStack() as three:
            y_in = sb("y_in", [P, CH, D], scope=three)
            xn = sb("xn", [P, CH, D], scope=three)
            xn_hi = sb("xn_hi", [P, KD, TOK], F32R, scope=three)
            xn_lo = sb("xn_lo", [P, KD, TOK], F32R, scope=three)
            lr_hi = sb("lr_hi", [P, TOK], F32R, scope=three)
            lr_parts = sb("lr_parts", [P, TOK], F32R, scope=three)
            relu = [sb(f"relu{i}", [P, TOK], scope=three) for i in range(2)]
            sq = [sb(f"sq{i}", [P, TOK], scope=three) for i in range(2)]
            sq_hi = sb("sq_hi", [P, MT, TOK], F32R, scope=three)
            sq_lo = sb("sq_lo", [P, MT, TOK], F32R, scope=three)
            yT = sb("yT", [P, KD, TOK], scope=three)
            bn = sb("bn", [P, CH, 6], scope=three)
            mv = sb("mv", [P, CH, 2], scope=three)
            ve = sb("ve", [P, CH], scope=three)
            rstd = sb("rstd", [P, CH], scope=three)

            xt_ps = [ps(f"xt_ps{i}", three) for i in range(KD)]
            lr_ps = ps("lr_ps", three)
            back_ps = ps("back_ps", three)
            fc_ps = [ps(f"fc_ps{i}", three) for i in range(2)]
            proj_ps = [ps(f"proj_ps{i}", three) for i in range(KD)]

            y_loaded = sem("y_loaded")
            y_stored1 = sem("y_stored1")
            y_stored2 = sem("y_stored2")
            out_stored = sem("out_stored")
            bn_done, mv_done, ve_done, rstd_done = (sem(n) for n in ("bn_done", "mv_done", "ve_done", "rstd_done"))
            yn_done = sem("yn_done")
            gamma_done = sem("gamma_done")
            x2_done = sem("x2_done")
            xn_done = sem("xn_done")
            x_turned = sem("x_turned")
            xn_hi_done = sem("xn_hi_done")
            xn_lo_done = sem("xn_lo_done")
            lr_summed = sem("lr_summed")
            lr_hi_done = sem("lr_hi_done")
            lr_done = sem("lr_done")
            fc_summed = sem("fc_summed")
            relu_done = sem("relu_done")
            sq_done = sem("sq_done")
            sq_hi_done = sem("sq_hi_done")
            sq_lo_done = sem("sq_lo_done")
            proj_tile = sem("proj_tile")
            yT_done = sem("yT_done")
            back_turned = sem("back_turned")
            out_ready = sem("out_ready")
            EARLY = 2

            def chunk_pipeline(eng, step, first=3):
                for i in range(first):
                    step(i)
                with eng.Fori(first, CHUNKS - 1, 1) as c:
                    step(c)
                for i in range(CHUNKS - 1, CHUNKS + 2):
                    step(i)

            def has(c, back):
                return not isinstance(c, int) or 0 <= c - back < CHUNKS

            block = three.enter_context(nc.Block())

            @block.sync
            def _(sp):
                def store_scan(first, batches, done):
                    for q in range(NB):
                        dst = bass.AP(tensor=scan_dram.tensor, offset=first * L * D + q * CQ,
                                      ap=[[D, L], [L * D, batches], [1, CQ]])
                        sp.dma_start(dst, scan_x[q * L:(q + 1) * L, first:first + batches, :]).then_inc(done, 16)
                    sp.wait_ge(done, 16 * NB)

                def load_y(c):
                    sp.dma_start(y_in[:, :, :], scan_dram[bass.ds(c * TOK, TOK), :].rearrange("(r p) d -> p r d", p=P)
                                 ).then_inc(y_loaded, 16)

                def step(c):
                    if has(c, -2):
                        at_least(sp, x2_done, c + 2)
                        load_y(c + 2)
                    if has(c, 2):
                        at_least(sp, out_ready, 2 * c - 2)
                        sp.dma_start(out_tok[bass.ds((c - 2) * TOK, TOK), :].rearrange("(r p) d -> p r d", p=P),
                                     resid[:, bass.ds((c - 2) * CH, CH), :]).then_inc(out_stored, 16)

                store_scan(0, EARLY * CH * NB, y_stored1)
                load_y(0)
                store_scan(EARLY * CH * NB, BATCH - EARLY * CH * NB, y_stored2)
                sp.wait_ge(x2_done, 1)
                load_y(1)
                for i in range(2):
                    step(i)
                with sp.Fori(2, CHUNKS - 2, 1) as c:
                    step(c)
                for i in range(CHUNKS - 2, CHUNKS + 2):
                    step(i)
                sp.wait_ge(out_stored, 16 * CHUNKS)

            @block.tensor
            def _(pe):
                def turn_in(c):
                    at_least(pe, xn_done, c + 1)
                    at_least(pe, xn_hi_done, c)
                    at_least(pe, xn_lo_done, c)
                    for k in range(KD):
                        for r in range(CH):
                            mm = pe.transpose(xt_ps[k][:, r * P:(r + 1) * P], xn[:, r, k * P:(k + 1) * P], ident[:, :])
                    mm.then_inc(x_turned, 1)

                def low_rank(c):
                    at_least(pe, xn_hi_done, c + 1)
                    at_least(pe, xn_lo_done, c + 1)
                    at_least(pe, lr_done, c)
                    at_least(pe, out_ready, 2 * c - 4)
                    for k in range(KD):
                        for i, part in enumerate((xn_hi, xn_lo)):
                            mm = pe.matmul(lr_ps[:, :], low_in[:, k, :], part[:, k, :], start=(k == 0 and i == 0),
                                           stop=(k == KD - 1 and i == 1))
                    mm.then_inc(lr_summed, 1)

                def hidden(c, m):
                    at_least(pe, relu_done, c * MT + m - 1)
                    if m == 0:
                        at_least(pe, lr_done, c + 1)
                    for k in range(KD):
                        for i, part in enumerate((xn_hi, xn_lo)):
                            pe.matmul(fc_ps[m % 2][:, :], fc_T[:, k, m * P:(m + 1) * P], part[:, k, :],
                                      start=(k == 0 and i == 0), stop=False)
                    pe.matmul(fc_ps[m % 2][:, :], low_out[:, m * P:(m + 1) * P], lr_parts[:, :], start=False, stop=True
                              ).then_inc(fc_summed, 1)

                def project(c, m):
                    at_least(pe, sq_hi_done, c * MT + m + 1)
                    at_least(pe, sq_lo_done, c * MT + m + 1)
                    if m == 0:
                        at_least(pe, yT_done, c)
                    for i, part in enumerate((sq_hi, sq_lo)):
                        for k in range(KD):
                            mm = pe.matmul(proj_ps[k][:, :], proj_T[:, m, k * P:(k + 1) * P], part[:, m, :],
                                           start=(m == 0 and i == 0), stop=(m == MT - 1 and i == 1))
                    mm.then_inc(proj_tile, 1)

                def turn_back(c, half):
                    bank = (back_ps, lr_ps)[half]
                    if half == 0:
                        at_least(pe, yT_done, c + 1)
                        at_least(pe, out_ready, 2 * c - 1)
                    else:
                        at_least(pe, out_ready, 2 * c)
                    for i in range(2):
                        for k in range(KD):
                            r = 2 * half + i
                            mm = pe.transpose(bank[:, (i * KD + k) * P:(i * KD + k + 1) * P],
                                              yT[:, k, r * P:(r + 1) * P], ident[:, :])
                    mm.then_inc(back_turned, 1)

                def step(c):
                    if has(c, 0):
                        low_rank(c)
                    for m in range(MT + 2):
                        if m < MT and has(c, 0):
                            hidden(c, m)
                        if m == 1 and has(c, 2):
                            turn_back(c - 2, 0)
                        if m == 2 and has(c, 2):
                            turn_back(c - 2, 1)
                        if m >= 2 and has(c, 1):
                            project(c - 1, m - 2)
                        if m == MT - 1 and has(c, -1):
                            turn_in(c + 1)

                turn_in(0)
                chunk_pipeline(pe, step)

            @block.scalar
            def _(act):
                def split_hi(c):
                    at_least(act, x_turned, c + 1)
                    at_least(act, fc_summed, c * MT)
                    for k in range(KD):
                        ins = act.copy(xn_hi[:, k, :], xt_ps[k][:, :])
                    ins.then_inc(xn_hi_done, 1)

                def square_hi(c, m):
                    at_least(act, sq_done, c * MT + m + 1)
                    at_least(act, proj_tile, c * MT + m + 1 - MT)
                    act.copy(sq_hi[:, m, :], sq[m % 2][:, :]).then_inc(sq_hi_done, 1)

                def step(c):
                    if has(c, 2):
                        at_least(act, proj_tile, (c - 1) * MT)
                        at_least(act, back_turned, 2 * c - 4)
                        for k in range(KD):
                            ins = act.mul(yT[:, k, :], proj_ps[k][:, :], proj_scale[:, k:k + 1])
                        ins.then_inc(yT_done, 1)
                    if has(c, 0):
                        for m in range(MT):
                            at_least(act, fc_summed, c * MT + m + 1)
                            at_least(act, sq_done, c * MT + m - 1)
                            act.activation(relu[m % 2][:, :], fc_ps[m % 2][:, :], ACT.Relu, scale=fc_scale[:, m:m + 1]
                                           ).then_inc(relu_done, 1)
                            if m >= 1:
                                square_hi(c, m - 1)
                    if has(c, -1):
                        split_hi(c + 1)
                    if has(c, 0):
                        square_hi(c, MT - 1)

                split_hi(0)
                chunk_pipeline(act, step)

            @block.gpsimd
            def _(pool):
                def deviation(count):
                    at_least(pool, ve_done, count)
                    pool.tensor_tensor(rstd[:, :], ve[:, :], neg_half[:, 0:CH], ALU.pow).then_inc(rstd_done, 1)

                def times_gamma(c):
                    at_least(pool, yn_done, c + 1)
                    pool.tensor_tensor(y_in[:, :, :], y_in[:, :, :], gamma_all[:, :].unsqueeze(1).broadcast_to([P, CH, D]),
                                       ALU.mult).then_inc(gamma_done, 1)

                def square_lo(c, m):
                    at_least(pool, sq_hi_done, c * MT + m + 1)
                    at_least(pool, proj_tile, c * MT + m + 1 - MT)
                    pool.tensor_tensor(sq_lo[:, m, :], sq[m % 2][:, :], sq_hi[:, m, :].bitcast(F32), ALU.subtract
                                       ).then_inc(sq_lo_done, 1)

                def step(c):
                    more = has(c, -1)
                    for m in range(MT):
                        if m == 1 and more:
                            deviation(2 * c + 3)
                        if m == 2 and more:
                            times_gamma(c + 1)
                        if m == 4 and more:
                            deviation(2 * c + 4)
                        if has(c, 0):
                            square_lo(c, m)

                deviation(1)
                times_gamma(0)
                deviation(2)
                chunk_pipeline(pool, step)

            @block.vector
            def _(dve):
                def statistics(source, count, free):
                    free = (free[0], known(dve, free[1]))
                    count = known(dve, count)
                    after = known(dve, count + 1)
                    own_waits(dve, ident_made)
                    at_least(dve, mv_done, count)
                    for r in range(CH):
                        ins = dve.bn_stats(bn[:, r, :], source(r))
                    ins.then_inc(bn_done, 1)
                    own_waits(dve, ident_made)
                    at_least(dve, bn_done, after)
                    at_least(dve, *free)
                    for r in range(CH):
                        ins = dve.bn_aggr(mv[:, r, :], bn[:, r, :])
                    ins.then_inc(mv_done, 1)
                    at_least(dve, mv_done, after)
                    at_least(dve, rstd_done, count)
                    dve.tensor_scalar(ve[:, :], mv[:, :, 1], EPS, None, ALU.add).then_inc(ve_done, 1)

                def res(c, r):
                    return resid[:, bass.ds(c * CH + r, 1), :].rearrange("p a d -> p (a d)")

                def norm_y(c):
                    at_least(dve, rstd_done, 2 * c + 1)
                    for r in range(CH):
                        ins = dve.tensor_scalar(y_in[:, r, :], y_in[:, r, :], mv[:, r, 0:1], rstd[:, r:r + 1],
                                                ALU.subtract, ALU.mult)
                    ins.then_inc(yn_done, 1)

                def add_y(c):
                    at_least(dve, gamma_done, c + 1)
                    x2 = resid[:, bass.ds(c * CH, CH), :]
                    dve.tensor_tensor(x2, x2, y_in[:, :, :], ALU.add).then_inc(x2_done, 1)
                    at_least(dve, x2_done, c + 1)

                def norm_x(c):
                    at_least(dve, rstd_done, 2 * c + 2)
                    at_least(dve, x_turned, c)
                    for r in range(CH):
                        ins = dve.tensor_scalar(xn[:, r, :], res(c, r), mv[:, r, 0:1], rstd[:, r:r + 1],
                                                ALU.subtract, ALU.mult)
                    ins.then_inc(xn_done, 1)

                def y_stats(c):
                    at_least(dve, y_loaded, 16 * c + 16)
                    own_waits(dve, ident_made)
                    statistics(lambda r: y_in[:, r, :], 2 * c, (xn_done, c))

                def x_stats(c):
                    statistics(lambda r: res(c, r), 2 * c + 1, (yn_done, c + 1))

                def split_lo(c):
                    at_least(dve, xn_hi_done, c + 1)
                    for k in range(KD):
                        ins = dve.tensor_tensor(xn_lo[:, k, :], xt_ps[k][:, :], xn_hi[:, k, :].bitcast(F32), ALU.subtract)
                    ins.then_inc(xn_lo_done, 1)

                def result(c, half):
                    at_least(dve, back_turned, 2 * c + half + 1)
                    bank = (back_ps, lr_ps)[half]
                    part = resid[:, bass.ds(c * CH + 2 * half, 2), :]
                    dve.tensor_tensor(part, bank[:, :].rearrange("p (r d) -> p r d", r=2), part, ALU.add
                                      ).then_inc(out_ready, 1)

                def step(c):
                    if has(c, 0):
                        at_least(dve, lr_summed, c + 1)
                        at_least(dve, fc_summed, c * MT)
                        dve.tensor_copy(lr_hi[:, :], lr_ps[:, :]).then_inc(lr_hi_done, 1)
                        at_least(dve, lr_hi_done, c + 1)
                        dve.scalar_tensor_tensor(out=lr_parts[:, :], in0=lr_hi[:, :].bitcast(F32), scalar=minus_lo[:, 0:1],
                                                 in1=lr_ps[:, :], op0=ALU.mult, op1=ALU.add).then_inc(lr_done, 1)
                    more = has(c, -1)
                    for m in range(MT):
                        if has(c, 0):
                            at_least(dve, relu_done, c * MT + m + 1)
                            at_least(dve, sq_hi_done, c * MT + m - 1)
                            at_least(dve, sq_lo_done, c * MT + m - 1)
                            dve.tensor_tensor(sq[m % 2][:, :], relu[m % 2][:, :], relu[m % 2][:, :], ALU.mult
                                              ).then_inc(sq_done, 1)
                        if m == 0 and more:
                            y_stats(c + 1)
                        if m == 1 and more:
                            norm_y(c + 1)
                        if m == 1 and has(c, 2):
                            result(c - 2, 0)
                        if m == 2 and has(c, 2):
                            result(c - 2, 1)
                        if m == 3 and more:
                            add_y(c + 1)
                            x_stats(c + 1)
                        if m == 5 and more:
                            norm_x(c + 1)
                    if more:
                        split_lo(c + 1)

                y_stats(0)
                norm_y(0)
                add_y(0)
                x_stats(0)
                norm_x(0)
                split_lo(0)
                chunk_pipeline(dve, step)


_INS = ['x', 'ctx_1024', 'L0_xattn_w_sim', 'L0_xattn_b_sim', 'L0_xattn_W_qv', 'L0_xattn_b_qv', 'L0_attn_A',
        'L0_attn_Bp', 'L0_attn_Cp', 'L0_attn_Dp', 'L0_attn_Wg', 'L0_attn_bg', 'L0_attn_gamma', 'L0_attn_beta',
        'L0_ffn_fast_b', 'L0_ffn_w_fc', 'L0_ffn_w_proj', 'L0_ffn_u', 'L0_ffn_v', 'L0_ffn_gate']


def kernel(**inputs):
    import concourse.bacc as _bacc
    from concourse.bass_utils import run_bass_kernel_spmd as _run

    nc = _bacc.Bacc("TRN2", target_bir_lowering=False, num_devices=1)
    arrays, args = {}, []
    for name in _INS:
        a = np.ascontiguousarray(inputs[name])
        if a.ndim == 0:
            a = a.reshape(1)
        arrays[f"in_{name}"] = a
        args.append(nc.dram_tensor(f"in_{name}", a.shape, mybir.dt.from_np(a.dtype), kind="ExternalInput").ap())
    shape = inputs['x'].shape
    args.append(nc.dram_tensor("out_0", shape, F32, kind="ExternalOutput").ap())
    perceiver_layer(nc, *args)
    r = _run(nc, [arrays], core_ids=[0])
    return r.results[0]["out_0"]
```

```python
from contextlib import ExitStack

import numpy as np

import concourse.bass as bass
from concourse import mybir

F32 = mybir.dt.float32
F32R = mybir.dt.float32r
ALU = mybir.AluOpType
ACT = mybir.ActivationFunctionType
AX = mybir.AxisListType

P = 128
EPS = 1e-5


def at_least(eng, sem, count):
    if isinstance(count, int) and count <= 0:
        return
    eng.wait_ge(sem, count)


def known(eng, count):
    return count if isinstance(count, int) else eng.snap(eng.to_reg(count))


def own_waits(eng, ident_made):
    eng.wait_ge(ident_made, 2)


def perceiver_layer(nc, x, ctx, w_sim, b_sim, W_qv, b_qv, A, Bp, Cp, Dp, Wg, bg, gamma, beta,
                    fast_b, w_fc, w_proj, u, v, gate, out):
    BATCH, L, D = x.shape
    J = ctx.shape[1]
    JT = (J - 1) // P
    KD = D // P
    NB = P // L
    GROUPS = BATCH // NB
    N = A.shape[1]
    HID = w_fc.shape[0]
    MT = HID // P
    RANK = u.shape[1]
    CQ = D // NB
    CH = 4
    TOK = CH * P
    CHUNKS = GROUPS // CH
    LAG = L - 1
    assert (L, NB, KD, JT, J) == (32, 4, 2, 2, 257) and D == W_qv.shape[1]

    x_tok = x.rearrange("b t d -> (b t) d")
    out_tok = out.rearrange("b t d -> (b t) d")
    gated_dram = nc.dram_tensor("gated_tokens", [BATCH * L, D], F32, kind="Internal").ap()
    scan_dram = nc.dram_tensor("scan_tokens", [BATCH * L, D], F32, kind="Internal").ap()
    SHIFTS = 8
    impulse_dram = nc.dram_tensor("impulse", [D, SHIFTS, 2 * L], F32, kind="Internal").ap()

    def row(vector):
        return vector.rearrange("(a n) -> a n", a=1)

    def everywhere(vector):
        return bass.AP(tensor=vector.tensor, offset=vector.offset, ap=[[0, P]] + [list(d) for d in vector.ap])

    with ExitStack() as whole:
        def sb(name, shape, dt=F32, scope=whole):
            return scope.enter_context(nc.sbuf_tensor(name, shape, dt))

        def ps(name, scope, shape=(P, 512)):
            return scope.enter_context(nc.psum_tensor(name, list(shape), F32))

        def sem(name):
            return whole.enter_context(nc.semaphore(name))

        resid = sb("resid", [P, GROUPS, D])
        scan_x = sb("scan_x", [P, BATCH, CQ])
        toeplitz = sb("toeplitz", [P, CQ, P])
        ident = sb("ident", [P, P])
        fc_T = sb("fc_T", [P, KD, HID], F32R)
        proj_T = sb("proj_T", [P, MT, D], F32R)
        fc_scale = sb("fc_scale", [P, MT])
        proj_scale = sb("proj_scale", [P, KD])
        low_in = sb("low_in", [P, KD, P], F32R)
        low_out = sb("low_out", [P, HID], F32R)
        minus_lo = sb("minus_lo", [P, 1])
        neg_half = sb("neg_half", [P, 4])
        gamma_all = sb("gamma_all", [P, D])
        y_in = sb("y_in", [P, CH, D])

        ident_made = sem("ident_made")
        scan_loaded = sem("scan_loaded")
        y_loaded = sem("y_loaded")
        y_second_loaded = sem("y_second_loaded")
        y_stored1 = sem("y_stored1")
        y_stored2 = sem("y_stored2")
        y_stored3 = sem("y_stored3")
        toeplitz_loaded = sem("toeplitz_loaded")

        below = sb("below", [P, HID])
        y_second = below[:, :].rearrange("p (r d) -> p r d", r=CH)
        assert CH * D == HID
        early = whole.enter_context(ExitStack())
        fc_in = sb("fc_in", [P, MT, D], scope=early)
        proj_in = sb("proj_in", [P, KD, HID], scope=early)
        thresholds = sb("thresholds", [P, 2, MT + KD], scope=early)
        fc_loaded = sem("fc_loaded")
        proj_loaded = sem("proj_loaded")
        sums_done = sem("sums_done")
        scales_done = sem("scales_done")
        thresholds_done = sem("thresholds_done")
        below_done = sem("below_done")
        ternary_done = sem("ternary_done")

        def magnitudes(dve, scale, w, loaded):
            dve.wait_ge(loaded, 16)
            dve.tensor_reduce(scale, w, AX.X, ALU.add, apply_absolute_value=True).then_inc(sums_done, 1)

        def scales(dve, scale, width, columns, nth):
            dve.wait_ge(sums_done, nth)
            dve.tensor_scalar(scale, scale, 1.0 / width, 1e-5, ALU.mult, ALU.max).then_inc(scales_done, 1)
            dve.wait_ge(scales_done, nth)
            for i, half in enumerate((0.5, -0.5)):
                ins = dve.tensor_scalar(thresholds[:, i, columns], scale, half, None, ALU.mult)
            ins.then_inc(thresholds_done, 1)

        def ternary(dve, i, nth):
            w = fc_in[:, i, :] if i < MT else proj_in[:, i - MT, :]
            b = below[:, 0:D] if i < MT else below[:, :]
            dve.wait_ge(thresholds_done, nth)
            at_least(dve, ternary_done, i)
            dve.tensor_scalar(b, w, thresholds[:, 1, i:i + 1], None, ALU.is_lt).then_inc(below_done, 1)
            dve.wait_ge(below_done, i + 1)
            dve.scalar_tensor_tensor(out=w, in0=w, scalar=thresholds[:, 0, i:i + 1], in1=b,
                                     op0=ALU.is_gt, op1=ALU.subtract).then_inc(ternary_done, 1)

        with ExitStack() as one:
            s1 = one
            free_fc = fc_in[:, :, :].rearrange("p m d -> p (m d)")
            free_proj = proj_in[:, :, :].rearrange("p k h -> p (k h)")
            SQUARES = KD * N * N
            states = free_fc[:, 0:KD * (L + 1) * N].rearrange("p (k l n) -> p k l n", k=KD, l=L + 1)
            v_next = free_proj[:, 0:SQUARES].rearrange("p (k m n) -> p k m n", k=KD, m=N)
            a_sb = free_proj[:, SQUARES:2 * SQUARES].rearrange("p (k n) -> p k n", k=KD)
            wg_in = free_proj[:, 2 * SQUARES:2 * SQUARES + KD * D].rearrange("p (k d) -> p k d", k=KD)
            ends = free_proj[:, HID * KD - D:]
            ctxn = [sb(f"ctxn{p}", [P, NB, JT, D], scope=s1) for p in range(2)]
            ctx_end = [sb(f"ctx_end{p}", [P, D], scope=s1) for p in range(2)]
            ctxT = sb("ctxT", [P, NB, KD, J], scope=s1)
            endsT = sb("endsT", [P, KD, BATCH], scope=s1)
            wqv = sb("wqv", [P, 4 * KD, D], scope=s1)
            wgT = sb("wgT", [P, KD, D], scope=s1)
            w1_all = sb("w1_all", [P, D], scope=s1)
            bqv_all = sb("bqv_all", [P, D], scope=s1)
            bg_all = sb("bg_all", [P, D], scope=s1)
            beta_all = sb("beta_all", [P, D], scope=s1)
            w23 = sb("w23", [P, 2, KD], scope=s1)
            bsim_all = sb("bsim_all", [P, 1], scope=s1)
            same_batch = sb("same_batch", [P, P], scope=s1)
            hc = [sb(f"hc{p}", [P, D], scope=s1) for p in range(2)]
            hc_probT = [sb(f"hc_probT{p}", [P, 2, 2, P], scope=s1) for p in range(2)]
            hcwT = sb("hcwT", [P, KD, P], scope=s1)
            prob = [sb(f"prob{p}", [P, J], scope=s1) for p in range(2)]
            pick = sb("pick", [P, P], scope=s1)
            hq = sb("hq", [P, D], scope=s1)
            hb = sb("hb", [P, D], scope=s1)
            hqbT = sb("hqbT", [P, 2, KD, P], scope=s1)
            hcqT = sb("hcqT", [P, KD, P], scope=s1)
            z = sb("z", [P, D], scope=s1)
            zT = sb("zT", [P, KD, P], scope=s1)
            gate_in = sb("gate_in", [P, D], scope=s1)
            gate_th = sb("gate_th", [P, D], scope=s1)
            gated = [sb(f"gated{p}", [P, D], scope=s1) for p in range(2)]
            dots = sb("dots", [P, D], scope=s1)
            bn1 = sb("bn1", [P, 6], scope=s1)
            mv1 = sb("mv1", [P, 2], scope=s1)
            ve1 = sb("ve1", [P, 1], scope=s1)
            rstd1 = sb("rstd1", [P, 1], scope=s1)
            bn2 = sb("bn2", [P, 6], scope=s1)
            mv2 = sb("mv2", [P, 2], scope=s1)
            ve2 = sb("ve2", [P, 1], scope=s1)
            rstd2 = sb("rstd2", [P, 1], scope=s1)
            s1_b = [sb(f"s1_b{p}", [P, 1], scope=s1) for p in range(2)]
            s1_dot = sb("s1_dot", [P, 1], scope=s1)
            neg_max = sb("neg_max", [P, 1], scope=s1)
            row_sum = sb("row_sum", [P, 1], scope=s1)
            row_rec = sb("row_rec", [P, 1], scope=s1)
            best = sb("best", [P, 1], scope=s1)
            bestT = sb("bestT", [P, L], scope=s1)
            neg_top = sb("neg_top", [P, 1], scope=s1)
            top_e = sb("top_e", [P, 1], scope=s1)
            top_eT = sb("top_eT", [P, L], scope=s1)
            top_sum = sb("top_sum", [P, 1], scope=s1)
            top_rec = sb("top_rec", [P, 1], scope=s1)
            c_sb = sb("c_sb", [P, KD, N], scope=s1)
            d_sb = sb("d_sb", [P, KD], scope=s1)
            v_new = sb("v_new", [P, KD, N], scope=s1)
            impulse = sb("impulse_sb", [P, KD, 2 * L], scope=s1)

            turn_ps = [ps(f"turn_ps{i}", s1) for i in range(2)]
            score_ps = ps("score_ps", s1)
            side_ps = ps("side_ps", s1)
            att_ps = ps("att_ps", s1)
            feat_ps = ps("feat_ps", s1)
            qv_ps = ps("qv_ps", s1)
            gate_ps = ps("gate_ps", s1)

            consts_loaded = sem("consts_loaded")
            late_loaded = sem("late_loaded")
            states_in = sem("states_in")
            x_loaded = [sem(f"x_loaded{p}") for p in range(2)]
            ctx_loaded = [sem(f"ctx_loaded{p}") for p in range(2)]
            end_loaded = [sem(f"end_loaded{p}") for p in range(2)]
            gated_stored = [sem(f"gated_stored{p}") for p in range(2)]
            masks_made = sem("masks_made")
            zeroed = sem("zeroed")
            wg_turned = sem("wg_turned")
            wgT_ready = sem("wgT_ready")
            ends_turned = sem("ends_turned")
            endsT_ready = sem("endsT_ready")
            bn1_done, mv1_done, ve1_done, rstd1_done = (sem(n) for n in ("bn1_done", "mv1_done", "ve1_done", "rstd1_done"))
            bn2_done, mv2_done, ve2_done, rstd2_done = (sem(n) for n in ("bn2_done", "mv2_done", "ve2_done", "rstd2_done"))
            hc_ready = sem("hc_ready")
            dot_done = sem("dot_done")
            s1_ready = sem("s1_ready")
            bqv_added = sem("bqv_added")
            side_turned = sem("side_turned")
            side_copied = sem("side_copied")
            hcwT_ready = sem("hcwT_ready")
            ctx_turned = sem("ctx_turned")
            ctxT_copied = sem("ctxT_copied")
            end_placed = sem("end_placed")
            scored = sem("scored")
            neg_max_ready = sem("neg_max_ready")
            best_ready = sem("best_ready")
            bestT_ready = sem("bestT_ready")
            neg_top_ready = sem("neg_top_ready")
            exp_done = sem("exp_done")
            row_rec_ready = sem("row_rec_ready")
            prob_ready = sem("prob_ready")
            top_done = sem("top_done")
            top_rec_ready = sem("top_rec_ready")
            pick_ready = sem("pick_ready")
            pooled = sem("pooled")
            attended = sem("attended")
            hq_ready = sem("hq_ready")
            hb_ready = sem("hb_ready")
            hqb_turned = sem("hqb_turned")
            hqbT_ready = sem("hqbT_ready")
            hcqT_ready = sem("hcqT_ready")
            projected = sem("projected")
            x1_ready = sem("x1_ready")
            z_ready = sem("z_ready")
            beta_added = sem("beta_added")
            z_turned = sem("z_turned")
            zT_ready = sem("zT_ready")
            gate_summed = sem("gate_summed")
            gate_in_ready = sem("gate_in_ready")
            tanh_done = sem("tanh_done")
            gated_ready = sem("gated_ready")
            v_next_ready = sem("v_next_ready")
            v_new_ready = sem("v_new_ready")
            state_kept = sem("state_kept")
            imp_dot = sem("imp_dot")
            imp_sum = sem("imp_sum")
            imp_first = sem("imp_first")
            impulse_ready = sem("impulse_ready")
            impulse_stored = sem("impulse_stored")

            CONSTS = 4
            LATE = 7
            STATE_LOADS = 4
            STEPS = 2
            STATE_START = 2
            STATE_END = STATE_START + L // STEPS
            FIRST = 4

            def software_pipeline(eng, step, between):
                for i in range(FIRST):
                    step(i, 0, range(STEPS) if i >= STATE_START else ())
                with eng.Fori(FIRST // 2, STATE_END // 2) as pair:
                    for k in range(2):
                        step(pair * 2, k, range(STEPS))
                between()
                with eng.Fori(STATE_END // 2, GROUPS // 2 - 1) as pair:
                    for k in range(2):
                        step(pair * 2, k, ())
                for i in range(GROUPS - 2, GROUPS + 2):
                    step(i, 0, ())

            def stages(base, k):
                g = base + k
                if isinstance(g, int):
                    return g, g % 2, g < GROUPS, 1 <= g <= GROUPS, g >= 2
                return g, k, True, True, True

            def min_groups(g):
                return min(g, GROUPS) if isinstance(g, int) else g

            def sixteen(base, k, back):
                if isinstance(base, int):
                    return 16 * ((base + k - back) // 2 + 1)
                return base * 8 + 16 * ((k - back) // 2 + 1)

            block = one.enter_context(nc.Block())

            @block.sync
            def _(sp):
                def load_x(g, p):
                    sp.dma_start(resid[:, bass.ds(g, 1), :].rearrange("p a d -> p (a d)"),
                                 x_tok[bass.ds(g * P, P), :]).then_inc(x_loaded[p], 16)

                def load_ctx(g, p):
                    sp.dma_start(ctxn[p][:, :, :, :],
                                 ctx[bass.ds(g * NB, NB), 0:J - 1, :].rearrange("b (q t) d -> q b t d", t=JT)
                                 ).then_inc(ctx_loaded[p], 16)

                def load_end(g, p):
                    rows = ctx[bass.ds(g * NB, NB), J - 1, :]
                    src = bass.AP(tensor=rows.tensor, offset=rows.offset, ap=[[J * D, NB], [0, L], [1, D]])
                    sp.dma_start(ctx_end[p][:, :], src).then_inc(end_loaded[p], 16)

                load_x(0, 0)
                load_ctx(0, 0)
                sp.dma_start(ends[:, :], ctx[:, J - 1, :]).then_inc(consts_loaded, 16)
                sp.dma_start(w23[:, :, :], bass.AP(tensor=w_sim.tensor, offset=D, ap=[[1, P], [D, 2], [P, KD]]),
                             allow_slow_non_contiguous=True).then_inc(consts_loaded, 16)
                sp.dma_start(w1_all[:, :], everywhere(w_sim[0:D])).then_inc(consts_loaded, 16)
                sp.dma_start(bsim_all[:, :], everywhere(b_sim)).then_inc(consts_loaded, 16)
                load_end(0, 0)
                load_x(1, 1)
                load_ctx(1, 1)
                load_end(1, 1)
                sp.dma_start(wqv[:, :, :], W_qv.rearrange("(k p) n -> p k n", p=P)).then_inc(late_loaded, 16)
                sp.dma_start(wg_in[:, :, :], Wg.rearrange("(k p) n -> p k n", p=P)).then_inc(late_loaded, 16)
                sp.dma_start(bqv_all[:, :], everywhere(b_qv)).then_inc(late_loaded, 16)
                sp.dma_start(bg_all[:, :], everywhere(bg)).then_inc(late_loaded, 16)
                sp.dma_start(beta_all[:, :], everywhere(beta)).then_inc(late_loaded, 16)
                sp.dma_start(gamma_all[:, :], everywhere(gamma)).then_inc(late_loaded, 16)
                sp.dma_start(d_sb[:, :], Dp.rearrange("(k p) -> p k", p=P),
                             allow_slow_non_contiguous=True).then_inc(late_loaded, 16)
                sp.dma_start(a_sb[:, :, :], A.rearrange("(k p) n m -> p k (n m)", p=P)).then_inc(states_in, 16)
                sp.dma_start(v_new[:, :, :], Bp.rearrange("(k p) n -> p k n", p=P)).then_inc(states_in, 16)
                sp.dma_start(states[:, :, 0, :], Bp.rearrange("(k p) n -> p k n", p=P)).then_inc(states_in, 16)
                sp.dma_start(c_sb[:, :, :], Cp.rearrange("(k p) n -> p k n", p=P)).then_inc(states_in, 16)

                def scan_load(first_group, groups):
                    for q in range(NB):
                        rows = gated_dram[bass.ds(first_group * P, groups * P), :]
                        src = bass.AP(tensor=rows.tensor, offset=rows.offset + q * CQ,
                                      ap=[[D, L], [L * D, groups * NB], [1, CQ]])
                        sp.dma_start(scan_x[q * L:(q + 1) * L, bass.ds(first_group * NB, groups * NB), :],
                                     src).then_inc(scan_loaded, 16)

                def step(base, k, _):
                    g, p, has_a, has_b, has_c = stages(base, k)
                    inside = not isinstance(g, int)
                    if inside or g + 2 < GROUPS:
                        at_least(sp, hc_ready, g + 1)
                        load_x(g + 2, p)
                        at_least(sp, attended, g + 1)
                        load_ctx(g + 2, p)
                        at_least(sp, hq_ready, g + 1)
                        load_end(g + 2, p)
                    if has_c:
                        at_least(sp, gated_ready, g - 1)
                        sp.dma_start(gated_dram[bass.ds((g - 2) * P, P), :], gated[p][:, :]
                                     ).then_inc(gated_stored[p], 16)

                for i in range(2):
                    step(i, 0, ())

                def scan_load_pair(base):
                    sp.wait_ge(gated_stored[0], base * 8 - 16)
                    sp.wait_ge(gated_stored[1], base * 8 - 16)
                    scan_load(base - 4, 2)

                def body(base):
                    step(base, 0, ())
                    if not isinstance(base, int) or base >= 4:
                        scan_load_pair(base)
                    step(base, 1, ())

                body(2)
                with sp.Fori(FIRST // 2, STATE_END // 2) as pair:
                    body(pair * 2)
                sp.wait_ge(impulse_ready, 1)
                for c in range(KD):
                    sp.dma_start(impulse_dram[c * P:(c + 1) * P, :, :],
                                 impulse[:, c, :].unsqueeze(1).broadcast_to([P, SHIFTS, 2 * L])).then_inc(impulse_stored, 16)
                with sp.Fori(STATE_END // 2, GROUPS // 2 - 1) as pair:
                    body(pair * 2)
                sp.wait_ge(impulse_stored, 16 * KD)
                sp.wait_ge(zeroed, FIRST)

                def toeplitz_load(q):
                    for first in range(0, L, SHIFTS):
                        src = bass.AP(tensor=impulse_dram.tensor, offset=q * CQ * SHIFTS * 2 * L + LAG - first,
                                      ap=[[2 * L - 1, SHIFTS], [SHIFTS * 2 * L, CQ], [1, L]])
                        sp.dma_start(toeplitz[q * L + first:q * L + first + SHIFTS, :, q * L:(q + 1) * L], src
                                     ).then_inc(toeplitz_loaded, 16)

                sp.dma_start(fc_in[:, :, :], w_fc.rearrange("(m p) d -> p m d", p=P)).then_inc(fc_loaded, 16)
                toeplitz_load(0)
                for i in range(GROUPS - 2, GROUPS, 2):
                    step(i, 0, ())
                    sp.dma_start(proj_in[:, :, :], w_proj.rearrange("(k p) h -> p k h", p=P)).then_inc(proj_loaded, 16)
                    toeplitz_load(1)
                    scan_load_pair(i)
                    step(i + 1, 0, ())
                    scan_load_pair(i + 2)
                    toeplitz_load(2)
                    toeplitz_load(3)
                for i in range(GROUPS, GROUPS + 2):
                    step(i, 0, ())
                    sp.wait_ge(gated_stored[i % 2], 16 * (GROUPS // 2))
                    scan_load(i - 2, 1)

            @block.tensor
            def _(pe):
                pe.wait_ge(ident_made, 2)

                def turn_context(g, p, b):
                    at_least(pe, ctxT_copied, g * 4 + b - 1)
                    for c in range(KD):
                        for t in range(JT):
                            mm = pe.transpose(turn_ps[b % 2][:, (c * JT + t) * P:(c * JT + t + 1) * P],
                                              ctxn[p][:, b, t, c * P:(c + 1) * P], ident[:, :])
                    mm.then_inc(ctx_turned, 1)

                def step(base, k, _):
                    g, p, has_a, has_b, has_c = stages(base, k)
                    o = 1 - p
                    if has_a or has_b:
                        at_least(pe, side_copied, g)
                        if has_a:
                            at_least(pe, hc_ready, g + 1)
                            for c in range(KD):
                                mm = pe.transpose(side_ps[:, c * P:(c + 1) * P], hc[p][:, c * P:(c + 1) * P], ident[:, :])
                        if has_b:
                            at_least(pe, prob_ready, g)
                            for t in range(JT):
                                mm = pe.transpose(side_ps[:, 256 + t * P:256 + (t + 1) * P],
                                                  prob[o][:, t * P:(t + 1) * P], ident[:, :])
                        mm.then_inc(side_turned, 1)
                    if has_b:
                        at_least(pe, pick_ready, g)
                        at_least(pe, gate_in_ready, g - 2)
                        if isinstance(g, int) and g == 2:
                            pe.wait_ge(wgT_ready, 1)
                        pe.matmul(gate_ps[:, 256:256 + D], pick[:, :], hc[o][:, :], start=True, stop=True
                                  ).then_inc(pooled, 1)
                    if has_a:
                        at_least(pe, ctx_loaded[p], sixteen(base, k, 0))
                        turn_context(g, p, 0)
                        turn_context(g, p, 1)
                        if isinstance(g, int) and g == 0:
                            pe.wait_ge(consts_loaded, 16 * CONSTS)
                            for c in range(KD):
                                mm = pe.transpose(feat_ps[:, c * P:(c + 1) * P], ends[:, c * P:(c + 1) * P], ident[:, :])
                            mm.then_inc(ends_turned, 1)
                    if has_b:
                        at_least(pe, side_copied, g + 1)
                        at_least(pe, hq_ready, g - 1)
                        for t in range(JT):
                            for b in range(NB):
                                mm = pe.matmul(att_ps[b * L:(b + 1) * L, 0:D], hc_probT[p][:, 1, t, b * L:(b + 1) * L],
                                               ctxn[o][:, b, t, :], start=(t == 0), stop=(t == JT - 1))
                        mm.then_inc(attended, 1)
                    if has_a:
                        turn_context(g, p, 2)
                        turn_context(g, p, 3)
                    if has_c:
                        at_least(pe, z_ready, g - 1)
                        at_least(pe, x1_ready, g - 1)
                        for c in range(KD):
                            mm = pe.transpose(qv_ps[:, 256 + c * P:256 + (c + 1) * P], z[:, c * P:(c + 1) * P],
                                              ident[:, :])
                        mm.then_inc(z_turned, 1)
                    if has_b:
                        if isinstance(g, int) and g == 1:
                            pe.wait_ge(endsT_ready, 1)
                        at_least(pe, hqbT_ready, g - 1)
                        for i, (part, ready) in enumerate(((hb, hb_ready), (hq, hq_ready))):
                            at_least(pe, ready, g)
                            for c in range(KD):
                                mm = pe.transpose(feat_ps[:, ((1 - i) * KD + c) * P:((1 - i) * KD + c + 1) * P],
                                                  part[:, c * P:(c + 1) * P], ident[:, :])
                        mm.then_inc(hqb_turned, 1)
                    if has_a:
                        at_least(pe, ctxT_copied, g * 4 + 4)
                        at_least(pe, end_placed, g + 1)
                        at_least(pe, hcwT_ready, g + 1)
                        at_least(pe, neg_max_ready, g)
                        at_least(pe, exp_done, g)
                        for c in range(KD):
                            for b in range(NB):
                                mm = pe.matmul(score_ps[b * L:(b + 1) * L, 0:J], hcwT[:, c, b * L:(b + 1) * L],
                                               ctxT[:, b, c, :], start=(c == 0), stop=(c == KD - 1))
                        mm.then_inc(scored, 1)
                    if has_c:
                        at_least(pe, zT_ready, g - 1)
                        at_least(pe, hb_ready, min_groups(g))
                        for c in range(KD):
                            mm = pe.matmul(gate_ps[:, 0:D], zT[:, c, :], wgT[:, c, :], start=(c == 0), stop=(c == KD - 1))
                        mm.then_inc(gate_summed, 1)
                    if has_b:
                        if has_c:
                            at_least(pe, zT_ready, g - 1)
                        if isinstance(g, int) and g == 1:
                            pe.wait_ge(late_loaded, 16 * LATE)
                            for e in range(KD):
                                for c in range(KD):
                                    mm = pe.transpose(gate_ps[:, (c * KD + e) * P:(c * KD + e + 1) * P],
                                                      wg_in[:, e, c * P:(c + 1) * P], ident[:, :])
                            mm.then_inc(wg_turned, 1)
                        feats = (hc_probT[o][:, 0], hqbT[:, 1], hqbT[:, 0], hcqT)
                        rows = (0, 3, 1, 2)
                        for f in range(4):
                            if f == 1:
                                at_least(pe, hqbT_ready, g)
                            if f == 3:
                                at_least(pe, hcqT_ready, g)
                            for c in range(KD):
                                mm = pe.matmul(qv_ps[:, 0:D], feats[f][:, c, :], wqv[:, rows[f] * KD + c, :],
                                               start=(f == 0 and c == 0), stop=(f == 3 and c == KD - 1))
                        mm.then_inc(projected, 1)

                software_pipeline(pe, step, lambda: None)

            @block.scalar
            def _(act):
                def step(base, k, _):
                    g, p, has_a, has_b, has_c = stages(base, k)
                    o = 1 - p
                    if has_a or has_b:
                        at_least(act, side_turned, g + 1)
                        at_least(act, projected, g - 1)
                        at_least(act, hcqT_ready, g - 1)
                        at_least(act, attended, g - 2)
                        first, last = (0 if has_a else 1), (2 if has_b else 1)
                        act.copy(hc_probT[p][:, first:last, :, :],
                                 side_ps[:, first * 256:last * 256].rearrange("p (f k t) -> p f k t", f=last - first, k=2)
                                 ).then_inc(side_copied, 1)
                    if has_a:
                        at_least(act, scored, g)
                        for b in range(NB):
                            at_least(act, ctx_turned, g * 4 + b + 1)
                            act.copy(ctxT[:, b, :, 0:J - 1], turn_ps[b % 2][:, :].rearrange("p (k j) -> p k j", k=KD)
                                     ).then_inc(ctxT_copied, 1)
                            if b == 1:
                                if isinstance(g, int) and g == 0:
                                    act.wait_ge(ends_turned, 1)
                                    act.copy(endsT[:, :, :], feat_ps[:, 0:KD * BATCH].rearrange("p (k b) -> p k b", k=KD)
                                             ).then_inc(endsT_ready, 1)
                                    act.wait_ge(consts_loaded, 16 * CONSTS)
                                at_least(act, side_copied, g + 1)
                                for c in range(KD):
                                    ins = act.activation(hcwT[:, c, :], hc_probT[p][:, 0, c, :], ACT.Identity,
                                                         bias=w23[:, 0, c:c + 1], scale=w23[:, 1, c:c + 1])
                                ins.then_inc(hcwT_ready, 1)
                    if has_c:
                        at_least(act, z_turned, g - 1)
                        at_least(act, gate_summed, g - 2)
                        act.copy(zT[:, :, :], qv_ps[:, 256:256 + D].rearrange("p (k t) -> p k t", k=KD)).then_inc(zT_ready, 1)
                    if has_b:
                        at_least(act, hqb_turned, g)
                        at_least(act, projected, g - 1)
                        at_least(act, hcqT_ready, g - 1)
                        act.copy(hqbT[:, :, :, :], feat_ps[:, :].rearrange("p (f k t) -> p f k t", f=2, k=KD)
                                 ).then_inc(hqbT_ready, 1)
                    if isinstance(g, int) and g == 1:
                        act.wait_ge(wg_turned, 1)
                        act.copy(wgT[:, :, :], gate_ps[:, :].rearrange("p (k e) -> p k e", k=KD)).then_inc(wgT_ready, 1)
                    if has_a:
                        at_least(act, neg_max_ready, g + 1)
                        at_least(act, scored, g + 1)
                        at_least(act, side_turned, g)
                        at_least(act, hq_ready, g - 1)
                        at_least(act, row_rec_ready, g)
                        act.activation(prob[p][:, :], score_ps[:, 0:J], ACT.Exp, bias=neg_max[:, 0:1],
                                       accum_out=row_sum[:, 0:1]).then_inc(exp_done, 1)
                    if has_c:
                        at_least(act, gate_in_ready, g - 1)
                        at_least(act, gated_ready, g - 2)
                        act.activation(gate_th[:, :], gate_in[:, :], ACT.Tanh, scale=0.5).then_inc(tanh_done, 1)
                    if has_a:
                        at_least(act, neg_top_ready, g + 1)
                        at_least(act, pick_ready, g)
                        act.activation(top_e[:, :], best[:, :], ACT.Exp, bias=neg_top[:, 0:1])
                        at_least(act, top_done, g)
                        act.activation(top_eT[:, :], bestT[:, :], ACT.Exp, bias=neg_top[:, 0:1],
                                       accum_out=top_sum[:, 0:1]).then_inc(top_done, 1)

                software_pipeline(act, step, lambda: None)

            @block.gpsimd
            def _(pool):
                pool.memset(ident[:, :], 0.0).then_inc(ident_made, 1)
                pool.memset(neg_half[:, :], -0.5)
                pool.memset(same_batch[:, :], 0.0).then_inc(masks_made, 1)
                pool.wait_ge(ident_made, 1)
                pool.affine_select(out=ident[:, :], in_=ident[:, :], compare_op=ALU.not_equal, fill=1.0, base=0,
                                   pattern=[[-1, P]], channel_multiplier=1).then_inc(ident_made, 1)
                pool.wait_ge(masks_made, 1)
                pool.wait_ge(ident_made, 2)
                for b in range(NB):
                    last = pool.memset(same_batch[b * L:(b + 1) * L, b * L:(b + 1) * L], 1.0)
                last.then_inc(masks_made, 1)
                pool.wait_ge(masks_made, 2)

                def inverse_deviation(dst, src, ready, made, count):
                    at_least(pool, ready, count)
                    pool.tensor_tensor(dst, src, neg_half[:, 0:1], ALU.pow).then_inc(made, 1)

                def state_product(count):
                    at_least(pool, v_new_ready, count)
                    pool.tensor_tensor(v_next[:, :, :, :].rearrange("p k m n -> p k m n"),
                                       a_sb[:, :, :].rearrange("p k (n m) -> p k m n", n=N),
                                       v_new[:, :, :].unsqueeze(2).broadcast_to([P, KD, N, N]),
                                       ALU.mult).then_inc(v_next_ready, 1)

                def step(base, k, state_steps):
                    g, p, has_a, has_b, has_c = stages(base, k)
                    inside = not isinstance(g, int)
                    if has_a:
                        if not inside and g == 0:
                            pool.wait_ge(endsT_ready, 1)
                        at_least(pool, scored, g)
                        pool.tensor_copy(ctxT[:, :, :, J - 1],
                                         endsT[:, :, bass.ds(g * NB, NB)].rearrange("p k b -> p b k")
                                         ).then_inc(end_placed, 1)
                    if has_c:
                        at_least(pool, z_ready, g - 2)
                        inverse_deviation(rstd2[:, :], ve2[:, :], ve2_done, rstd2_done, g - 1)
                    if not inside and g == STATE_START:
                        pool.wait_ge(states_in, 16 * STATE_LOADS)
                    for s in state_steps:
                        state_product((base - STATE_START + k) * STEPS + s)
                        if s == 0:
                            break
                    if inside or g + 1 < GROUPS:
                        at_least(pool, hc_ready, g + 1)
                        inverse_deviation(rstd1[:, :], ve1[:, :], ve1_done, rstd1_done, g + 2)
                    if has_c:
                        at_least(pool, z_ready, g - 1)
                        r = resid[:, bass.ds(g - 2, 1), :].rearrange("p a d -> p (a d)")
                        pool.tensor_tensor(r, r, beta_all[:, :], ALU.add).then_inc(beta_added, 1)
                    for s in list(state_steps)[1:]:
                        state_product((base - STATE_START + k) * STEPS + s)
                    if not inside and g == 0:
                        pool.wait_ge(late_loaded, 16 * LATE)
                        add_bqv(0)
                    if inside or g + 1 < GROUPS:
                        add_bqv(g + 1)
                    if not inside and g < FIRST:
                        part = CQ // FIRST
                        pool.memset(toeplitz[:, g * part:(g + 1) * part, :], 0.0).then_inc(zeroed, 1)

                def add_bqv(g):
                    at_least(pool, hc_ready, g + 1)
                    r = resid[:, bass.ds(g, 1), :].rearrange("p a d -> p (a d)")
                    pool.tensor_tensor(r, r, bqv_all[:, :], ALU.add).then_inc(bqv_added, 1)

                inverse_deviation(rstd1[:, :], ve1[:, :], ve1_done, rstd1_done, 1)
                pool.memset(impulse[:, :, :], 0.0)
                software_pipeline(pool, step, lambda: None)

            @block.vector
            def _(dve):
                def layer_norm1(g, p, count):
                    count = known(dve, count)
                    after = known(dve, count + 1)
                    own_waits(dve, ident_made)
                    at_least(dve, mv1_done, count)
                    dve.bn_stats(bn1[:, :], resid[:, bass.ds(g, 1), :].rearrange("p a d -> p (a d)")).then_inc(bn1_done, 1)
                    own_waits(dve, ident_made)
                    at_least(dve, bn1_done, after)
                    at_least(dve, hc_ready, count)
                    dve.bn_aggr(mv1[:, :], bn1[:, :]).then_inc(mv1_done, 1)
                    at_least(dve, mv1_done, after)
                    at_least(dve, rstd1_done, count)
                    dve.tensor_scalar(ve1[:, :], mv1[:, 1:2], EPS, None, ALU.add).then_inc(ve1_done, 1)

                def normalise1(g, p, count):
                    at_least(dve, rstd1_done, count + 1)
                    at_least(dve, pooled, count - 1)
                    at_least(dve, hb_ready, count - 1)
                    at_least(dve, side_turned, count - 1)
                    at_least(dve, dot_done, count)
                    at_least(dve, s1_ready, count)
                    dve.tensor_scalar(hc[p][:, :], resid[:, bass.ds(g, 1), :].rearrange("p a d -> p (a d)"),
                                      mv1[:, 0:1], rstd1[:, 0:1], ALU.subtract, ALU.mult).then_inc(hc_ready, 1)
                    at_least(dve, hc_ready, count + 1)
                    if isinstance(g, int) and g == 0:
                        dve.wait_ge(consts_loaded, 16 * CONSTS)
                    dve.tensor_tensor_reduce(out=dots[:, :], in0=hc[p][:, :], in1=w1_all[:, :], scale=1.0, scalar=0.0,
                                             op0=ALU.mult, op1=ALU.add, accum_out=s1_dot[:, :]).then_inc(dot_done, 1)
                    at_least(dve, dot_done, count + 1)
                    at_least(dve, best_ready, count - 1)
                    dve.tensor_scalar(s1_b[p][:, :], s1_dot[:, :], bsim_all[:, 0:1], None, ALU.add).then_inc(s1_ready, 1)

                def state_sum(count):
                    at_least(dve, v_next_ready, count + 1)
                    at_least(dve, state_kept, count)
                    dve.tensor_reduce(v_new[:, :, :], v_next[:, :, :, :], AX.X, ALU.add).then_inc(v_new_ready, 1)

                def state_keep(count):
                    at_least(dve, v_new_ready, count + 1)
                    dve.tensor_copy(states[:, :, bass.ds(count + 1, 1), :].rearrange("p k a n -> p k (a n)"),
                                    v_new[:, :, :]).then_inc(state_kept, 1)

                def step(base, k, state_steps):
                    g, p, has_a, has_b, has_c = stages(base, k)
                    inside = not isinstance(g, int)
                    o = 1 - p
                    if isinstance(g, int) and g == STATE_START:
                        dve.wait_ge(late_loaded, 16 * LATE)
                        dve.wait_ge(states_in, 16 * STATE_LOADS)
                    if has_c:
                        at_least(dve, projected, g - 1)
                        at_least(dve, bqv_added, g - 1)
                        r = resid[:, bass.ds(g - 2, 1), :].rearrange("p a d -> p (a d)")
                        dve.tensor_tensor(r, qv_ps[:, 0:D], r, ALU.add).then_inc(x1_ready, 1)
                        done, before = known(dve, g - 1), known(dve, g - 2)
                        own_waits(dve, ident_made)
                        at_least(dve, x1_ready, done)
                        at_least(dve, mv2_done, before)
                        dve.bn_stats(bn2[:, :], r).then_inc(bn2_done, 1)
                        own_waits(dve, ident_made)
                        at_least(dve, bn2_done, done)
                        at_least(dve, z_ready, before)
                        dve.bn_aggr(mv2[:, :], bn2[:, :]).then_inc(mv2_done, 1)
                        at_least(dve, mv2_done, done)
                        at_least(dve, rstd2_done, g - 2)
                        dve.tensor_scalar(ve2[:, :], mv2[:, 1:2], EPS, None, ALU.add).then_inc(ve2_done, 1)
                    if has_b:
                        at_least(dve, pooled, g)
                        at_least(dve, hqb_turned, g - 1)
                        dve.tensor_tensor(hb[:, :], gate_ps[:, 256:256 + D], hc[o][:, :], ALU.mult).then_inc(hb_ready, 1)
                    if has_c:
                        at_least(dve, rstd2_done, g - 1)
                        at_least(dve, z_turned, g - 2)
                        at_least(dve, gated_ready, g - 2)
                        dve.tensor_scalar(z[:, :], r, mv2[:, 0:1], rstd2[:, 0:1], ALU.subtract, ALU.mult
                                          ).then_inc(z_ready, 1)
                    if inside or g + 1 < GROUPS:
                        at_least(dve, x_loaded[o], sixteen(base, k, -1))
                        layer_norm1(g + 1, o, g + 1)
                    if has_b:
                        at_least(dve, attended, g)
                        at_least(dve, end_loaded[o], sixteen(base, k, 1))
                        at_least(dve, hqb_turned, g - 1)
                        dve.scalar_tensor_tensor(out=hq[:, :], in0=ctx_end[o][:, :], scalar=prob[o][:, J - 1:J],
                                                 in1=att_ps[:, 0:D], op0=ALU.mult, op1=ALU.add).then_inc(hq_ready, 1)
                    for s in list(state_steps)[:1]:
                        state_sum((base - STATE_START + k) * STEPS + s)
                    if inside or g + 1 < GROUPS:
                        normalise1(g + 1, o, g + 1)
                    if has_a:
                        at_least(dve, scored, g + 1)
                        at_least(dve, exp_done, g)
                        at_least(dve, best_ready, g)
                        dve.tensor_reduce(neg_max[:, :], score_ps[:, 0:J], AX.X, ALU.max, negate=True
                                          ).then_inc(neg_max_ready, 1)
                        at_least(dve, neg_max_ready, g + 1)
                        at_least(dve, s1_ready, g + 1)
                        at_least(dve, top_done, g)
                        dve.tensor_tensor(best[:, :], s1_b[p][:, :], neg_max[:, :], ALU.subtract).then_inc(best_ready, 1)
                        at_least(dve, best_ready, g + 1)
                        dve.transpose(bestT[:, :], best[:, 0:1].broadcast_to([P, L])).then_inc(bestT_ready, 1)
                        at_least(dve, bestT_ready, g + 1)
                        dve.tensor_reduce(neg_top[:, :], bestT[:, :], AX.X, ALU.max, negate=True
                                          ).then_inc(neg_top_ready, 1)
                    if has_b:
                        at_least(dve, hqbT_ready, g)
                        at_least(dve, side_copied, g)
                        at_least(dve, projected, g - 1)
                        dve.tensor_tensor(hcqT[:, :, :], hqbT[:, 0, :, :],
                                          hc_probT[o][:, 0, :, :], ALU.mult).then_inc(hcqT_ready, 1)
                    for s in list(state_steps)[:1]:
                        state_keep((base - STATE_START + k) * STEPS + s)
                    if has_c:
                        at_least(dve, gate_summed, g - 1)
                        at_least(dve, tanh_done, g - 2)
                        dve.tensor_tensor(gate_in[:, :], gate_ps[:, 0:D], bg_all[:, :], ALU.add).then_inc(gate_in_ready, 1)
                    if has_a:
                        at_least(dve, exp_done, g + 1)
                        at_least(dve, prob_ready, g)
                        dve.reciprocal(row_rec[:, :], row_sum[:, :]).then_inc(row_rec_ready, 1)
                        at_least(dve, row_rec_ready, g + 1)
                        dve.tensor_scalar(prob[p][:, :], prob[p][:, :], row_rec[:, 0:1], None, ALU.mult
                                          ).then_inc(prob_ready, 1)
                    for s in list(state_steps)[1:]:
                        state_sum((base - STATE_START + k) * STEPS + s)
                    if has_c:
                        at_least(dve, tanh_done, g - 1)
                        at_least(dve, gated_stored[p], sixteen(base, k, 4))
                        dve.scalar_tensor_tensor(out=gated[p][:, :], in0=gate_th[:, :], scalar=1.0, in1=z[:, :],
                                                 op0=ALU.add, op1=ALU.mult).then_inc(gated_ready, 1)
                    if has_a:
                        at_least(dve, top_done, g + 1)
                        at_least(dve, pick_ready, g)
                        dve.reciprocal(top_rec[:, :], top_sum[:, :]).then_inc(top_rec_ready, 1)
                        at_least(dve, top_rec_ready, g + 1)
                        at_least(dve, pooled, g)
                        dve.tensor_scalar(pick[:, :], same_batch[:, :], top_e[:, 0:1], top_rec[:, 0:1],
                                          ALU.mult, ALU.mult).then_inc(pick_ready, 1)
                    for s in list(state_steps)[1:]:
                        state_keep((base - STATE_START + k) * STEPS + s)
                    if isinstance(g, int) and g == GROUPS:
                        magnitudes(dve, fc_scale[:, :], fc_in[:, :, :], fc_loaded)

                def impulse_response():
                    dve.wait_ge(state_kept, L)
                    w = states[:, :, 0:L, :]
                    dve.tensor_tensor(w, w, c_sb[:, :, :].unsqueeze(2).broadcast_to([P, KD, L, N]), ALU.mult).then_inc(imp_dot, 1)
                    dve.wait_ge(imp_dot, 1)
                    dve.wait_ge(zeroed, FIRST)
                    dve.tensor_reduce(impulse[:, :, LAG:LAG + L], w, AX.X, ALU.add).then_inc(imp_sum, 1)
                    dve.wait_ge(imp_sum, 1)
                    dve.scalar_tensor_tensor(out=impulse[:, :, LAG], in0=d_sb[:, :], scalar=1.0, in1=impulse[:, :, LAG],
                                             op0=ALU.add, op1=ALU.add).then_inc(imp_first, 1)
                    dve.wait_ge(imp_first, 1)
                    dve.tensor_scalar(impulse[:, :, LAG:LAG + L], impulse[:, :, LAG:LAG + L], 0.5, None, ALU.mult).then_inc(impulse_ready, 1)

                dve.wait_ge(x_loaded[0], 16)
                layer_norm1(0, 0, 0)
                normalise1(0, 0, 0)
                dve.wait_ge(masks_made, 2)
                software_pipeline(dve, step, impulse_response)
                scales(dve, fc_scale[:, :], D, slice(0, MT), 1)
                for i in range(MT):
                    ternary(dve, i, 1)

        with ExitStack() as two:
            u_in = sb("u_in", [P, MT, RANK], scope=two)
            v_in = sb("v_in", [RANK, D], scope=two)
            fbT = sb("fbT", [RANK, RANK], scope=two)
            gate_all = sb("gate_all", [P, 1], scope=two)
            u_scaled = sb("u_scaled", [P, MT, RANK], scope=two)
            u_rec = sb("u_rec", [P, MT], scope=two)
            u_hi = sb("u_hi", [P, MT, RANK], F32R, scope=two)
            u_parts = sb("u_parts", [P, MT, 4, 2, RANK], scope=two)
            c_full = sb("c_full", [P, KD, RANK], scope=two)

            scan_ps = [ps(f"scan_ps{i}", two) for i in range(4)]
            wturn_ps = [ps(f"wturn_ps{i}", two) for i in range(2)]
            low_ps = ps("low_ps", two)

            w_loaded = sem("w_loaded")
            scanned = sem("scanned")
            scan_copied = sem("scan_copied")
            u_steps = sem("u_steps")
            u_done = sem("u_done")
            low_product = sem("low_product")
            c_steps = sem("c_steps")
            w_turned = sem("w_turned")
            w_copied = sem("w_copied")
            y_stored = sem("y_stored")

            BANK = 4
            W_LOADS = 4
            SCANS = CQ // BANK
            TURNS = 2 * MT * KD // BANK + MT // BANK

            block = two.enter_context(nc.Block())

            @block.sync
            def _(sp):
                sp.dma_start(u_in[:, :, :], u.rearrange("(m p) r -> p m r", p=P)).then_inc(w_loaded, 16)
                sp.dma_start(v_in[:, :], v).then_inc(w_loaded, 16)
                sp.dma_start(fbT[:, :], fast_b.rearrange("a b -> b a"),
                             allow_slow_non_contiguous=True).then_inc(w_loaded, 16)
                sp.dma_start(gate_all[:, :], everywhere(gate)).then_inc(w_loaded, 16)

                def store_scan(first, batches, done):
                    for q in range(NB):
                        dst = bass.AP(tensor=scan_dram.tensor, offset=first * L * D + q * CQ,
                                      ap=[[D, L], [L * D, batches], [1, CQ]])
                        sp.dma_start(dst, scan_x[q * L:(q + 1) * L, first:first + batches, :]).then_inc(done, 16)

                sp.wait_ge(scan_copied, SCANS)
                store_scan(0, CH * NB, y_stored1)
                store_scan(CH * NB, CH * NB, y_stored2)
                sp.wait_ge(y_stored1, 16 * NB)
                sp.dma_start(y_in[:, :, :], scan_dram[0:TOK, :].rearrange("(r p) d -> p r d", p=P)).then_inc(y_loaded, 16)
                sp.wait_ge(y_stored2, 16 * NB)
                sp.wait_ge(ternary_done, MT + KD)
                sp.dma_start(y_second[:, :, :], scan_dram[TOK:2 * TOK, :].rearrange("(r p) d -> p r d", p=P)
                             ).then_inc(y_second_loaded, 16)
                store_scan(2 * CH * NB, BATCH - 2 * CH * NB, y_stored3)

            @block.gpsimd
            def _(pool):
                pool.memset(minus_lo[0:P // 2, :], 0.0)
                pool.memset(minus_lo[P // 2:P, :], -1.0)

            @block.tensor
            def _(pe):
                pe.wait_ge(toeplitz_loaded, 16 * NB * (L // SHIFTS))
                pe.wait_ge(scan_loaded, 16 * NB * (GROUPS // 2 + 1))
                for j in range(CQ):
                    bank = j // BANK
                    if j % BANK == 0:
                        at_least(pe, scan_copied, bank - 3)
                    mm = pe.matmul(scan_ps[bank % 4][:, (j % BANK) * P:(j % BANK + 1) * P], toeplitz[:, j, :],
                                   scan_x[:, :, j], start=True, stop=True)
                    if j % BANK == BANK - 1:
                        mm.then_inc(scanned, 1)
                pe.wait_ge(w_loaded, 16 * W_LOADS)
                for c in range(KD):
                    mm = pe.matmul(low_ps[:, c * RANK:(c + 1) * RANK], v_in[:, c * P:(c + 1) * P], fbT[:, :],
                                   start=True, stop=True)
                mm.then_inc(low_product, 1)
                turn = 0
                pe.wait_ge(ternary_done, MT)
                for c in range(KD):
                    for m in range(MT):
                        if m % BANK == 0:
                            at_least(pe, w_copied, turn - 1)
                        mm = pe.transpose(wturn_ps[turn % 2][:, (m % BANK) * P:(m % BANK + 1) * P],
                                          fc_in[:, m, c * P:(c + 1) * P], ident[:, :])
                        if m % BANK == BANK - 1:
                            mm.then_inc(w_turned, 1)
                            turn += 1
                pe.wait_ge(ternary_done, MT + KD)
                for m in range(0, MT, 2):
                    at_least(pe, w_copied, turn - 1)
                    for i in range(2):
                        for c in range(KD):
                            mm = pe.transpose(wturn_ps[turn % 2][:, (i * KD + c) * P:(i * KD + c + 1) * P],
                                              proj_in[:, c, (m + i) * P:(m + i + 1) * P], ident[:, :])
                    mm.then_inc(w_turned, 1)
                    turn += 1
                pe.wait_ge(u_done, 1)
                for m in range(MT):
                    if m % BANK == 0:
                        at_least(pe, w_copied, turn - 1)
                    mm = pe.transpose(wturn_ps[turn % 2][:, (m % BANK) * P:(m % BANK + 1) * P],
                                      u_parts[:, m, :, :, :].rearrange("p q h r -> p (q h r)"), ident[:, :])
                    if m % BANK == BANK - 1:
                        mm.then_inc(w_turned, 1)
                        turn += 1

            @block.scalar
            def _(act):
                for bank in range(SCANS):
                    act.wait_ge(scanned, bank + 1)
                    act.copy(scan_x[:, :, bank * BANK:(bank + 1) * BANK].rearrange("p b j -> p j b"),
                             scan_ps[bank % 4][:, :].rearrange("p (j b) -> p j b", j=BANK)).then_inc(scan_copied, 1)
                turn = 0
                for c in range(KD):
                    for half in range(MT // BANK):
                        act.wait_ge(w_turned, turn + 1)
                        act.copy(fc_T[:, c, half * 512:(half + 1) * 512], wturn_ps[turn % 2][:, :]).then_inc(w_copied, 1)
                        turn += 1
                for m in range(0, MT, 2):
                    act.wait_ge(w_turned, turn + 1)
                    act.copy(proj_T[:, m:m + 2, :].rearrange("p m d -> p (m d)"), wturn_ps[turn % 2][:, :]).then_inc(w_copied, 1)
                    turn += 1
                for half in range(MT // BANK):
                    act.wait_ge(w_turned, turn + 1)
                    act.copy(low_out[:, half * 512:(half + 1) * 512], wturn_ps[turn % 2][:, :]).then_inc(w_copied, 1)
                    turn += 1
                assert turn == TURNS

            @block.vector
            def _(dve):
                magnitudes(dve, proj_scale[:, :], proj_in[:, :, :], proj_loaded)
                scales(dve, proj_scale[:, :], HID, slice(MT, MT + KD), 2)
                dve.reciprocal(u_rec[:, :], fc_scale[:, :]).then_inc(u_steps, 1)
                for i in range(MT, MT + KD):
                    ternary(dve, i, 2)
                dve.wait_ge(w_loaded, 16 * W_LOADS)
                dve.wait_ge(u_steps, 1)
                for m in range(MT):
                    ins = dve.tensor_scalar(u_scaled[:, m, :], u_in[:, m, :], u_rec[:, m:m + 1], None, ALU.mult)
                ins.then_inc(u_steps, 1)
                dve.wait_ge(u_steps, 2)
                dve.tensor_copy(u_hi[:, :, :], u_scaled[:, :, :]).then_inc(u_steps, 1)
                dve.wait_ge(u_steps, 3)
                for q in range(4):
                    for part in range(2):
                        if q % 2 == 0:
                            ins = dve.tensor_copy(u_parts[:, :, q, part, :], u_hi[:, :, :].bitcast(F32))
                        else:
                            ins = dve.tensor_tensor(u_parts[:, :, q, part, :], u_scaled[:, :, :],
                                                    u_hi[:, :, :].bitcast(F32), ALU.subtract)
                ins.then_inc(u_done, 1)
                dve.wait_ge(low_product, 1)
                dve.tensor_scalar(c_full[:, :, :], low_ps[:, 0:KD * RANK].rearrange("p (k r) -> p k r", k=KD),
                                  gate_all[:, 0:1], None, ALU.mult).then_inc(c_steps, 1)
                dve.wait_ge(c_steps, 1)
                li = low_in[:, :, :].rearrange("p k (q h r) -> p k q h r", q=4, h=2)
                for q in range(4):
                    ins = dve.tensor_copy(li[:, :, q, 0, :], c_full[:, :, :])
                ins.then_inc(c_steps, 1)
                dve.wait_ge(c_steps, 2)
                for q in range(4):
                    ins = dve.tensor_tensor(li[:, :, q, 1, :], c_full[:, :, :], li[:, :, q, 0, :].bitcast(F32), ALU.subtract)
                ins.then_inc(c_steps, 1)
                dve.wait_ge(c_steps, 3)

        early.close()
        with ExitStack() as three:
            xn = sb("xn", [P, CH, D], scope=three)
            xn_hi = toeplitz[:, :, :].bitcast(F32R).rearrange("p (c k q) n -> p c k (q n)", c=CHUNKS, k=KD)
            xn_lo = sb("xn_lo", [P, CHUNKS, KD, TOK], F32R, scope=three)
            lr_hi = sb("lr_hi", [P, TOK], F32R, scope=three)
            lr_parts = sb("lr_parts", [P, TOK], F32R, scope=three)
            SQ = 4
            tiles = scan_x[:, :, :].rearrange("p (i t) q -> p i (t q)", i=BATCH * CQ // TOK)
            relu = [tiles[:, i, :] for i in range(2)]
            sq = [tiles[:, 2 + i, :] for i in range(SQ)]
            yT = tiles[:, 2 + SQ:2 + SQ + KD, :]
            sq_hi = sb("sq_hi", [P, MT, TOK], F32R, scope=three)
            sq_lo = sb("sq_lo", [P, MT, TOK], F32R, scope=three)
            bn_y, bn_x = (sb(n, [P, CH, 6], scope=three) for n in ("bn_y", "bn_x"))
            mv_y, mv_x = (sb(n, [P, CH, 2], scope=three) for n in ("mv_y", "mv_x"))
            ve_y, ve_x = (sb(n, [P, CH], scope=three) for n in ("ve_y", "ve_x"))
            rstd_y, rstd_x = (sb(n, [P, CH], scope=three) for n in ("rstd_y", "rstd_x"))
            shift_y = sb("shift_y", [P, CH], scope=three)

            xt_ps = [ps(f"xt_ps{i}", three) for i in range(KD)]
            lr_ps = ps("lr_ps", three)
            back_ps = ps("back_ps", three)
            fc_ps = [ps(f"fc_ps{i}", three) for i in range(2)]
            proj_ps = [ps(f"proj_ps{i}", three) for i in range(KD)]

            out_stored = sem("out_stored")
            bn_y_done, mv_y_done, ve_y_done, rstd_y_done = (sem(n) for n in ("bn_y_done", "mv_y_done", "ve_y_done", "rstd_y_done"))
            bn_x_done, mv_x_done, ve_x_done, rstd_x_done = (sem(n) for n in ("bn_x_done", "mv_x_done", "ve_x_done", "rstd_x_done"))
            shift_done = sem("shift_done")
            centred = sem("centred")
            yn_done = sem("yn_done")
            gamma_done = sem("gamma_done")
            x2_done = sem("x2_done")
            xn_done = sem("xn_done")
            x_turned = sem("x_turned")
            xn_hi_done = sem("xn_hi_done")
            xn_lo_done = sem("xn_lo_done")
            lr_summed = sem("lr_summed")
            lr_hi_done = sem("lr_hi_done")
            lr_done = sem("lr_done")
            fc_summed = sem("fc_summed")
            relu_done = sem("relu_done")
            sq_done = sem("sq_done")
            sq_hi_done = sem("sq_hi_done")
            sq_lo_done = sem("sq_lo_done")
            proj_tile = sem("proj_tile")
            yT_done = sem("yT_done")
            back_turned = sem("back_turned")
            out_ready = sem("out_ready")
            BEHIND = 3

            def chunk_pipeline(eng, step, first=2):
                for i in range(first):
                    step(i)
                with eng.Fori(first, CHUNKS - 2, 1) as c:
                    step(c)
                for i in range(CHUNKS - 2, CHUNKS + 1):
                    step(i)

            def has(c, ahead):
                return not isinstance(c, int) or 0 <= c + ahead < CHUNKS

            def tile(c, m):
                return c * MT + m

            block = three.enter_context(nc.Block())

            @block.sync
            def _(sp):
                def load_y(c):
                    at_least(sp, x2_done, c)
                    sp.dma_start(y_in[:, :, :], scan_dram[bass.ds(c * TOK, TOK), :].rearrange("(r p) d -> p r d", p=P)
                                 ).then_inc(y_loaded, 16)

                def step(c):
                    if has(c, -1):
                        at_least(sp, out_ready, 2 * c)
                        sp.dma_start(out_tok[bass.ds((c - 1) * TOK, TOK), :].rearrange("(r p) d -> p r d", p=P),
                                     resid[:, bass.ds((c - 1) * CH, CH), :]).then_inc(out_stored, 16)
                    if has(c, 3):
                        load_y(c + 3)

                sp.wait_ge(y_stored3, 16 * NB)
                load_y(2)
                for i in range(2):
                    step(i)
                with sp.Fori(2, CHUNKS - 3, 1) as c:
                    step(c)
                for i in range(CHUNKS - 3, CHUNKS + 1):
                    step(i)
                sp.wait_ge(out_stored, 16 * CHUNKS)

            def part_of(parts, c, k):
                return parts[:, bass.ds(c, 1), k, :].rearrange("p a t -> p (a t)")

            @block.tensor
            def _(pe):
                def turn_in(c):
                    at_least(pe, xn_done, c + 1)
                    at_least(pe, xn_lo_done, c)
                    for k in range(KD):
                        for r in range(CH):
                            mm = pe.transpose(xt_ps[k][:, r * P:(r + 1) * P], xn[:, r, k * P:(k + 1) * P], ident[:, :])
                    mm.then_inc(x_turned, 1)

                def low_rank(c):
                    at_least(pe, xn_hi_done, c + 1)
                    at_least(pe, xn_lo_done, c + 1)
                    at_least(pe, lr_done, c)
                    at_least(pe, out_ready, 2 * c - 3)
                    for k in range(KD):
                        for i, part in enumerate((xn_hi, xn_lo)):
                            mm = pe.matmul(lr_ps[:, :], low_in[:, k, :], part_of(part, c, k), start=(k == 0 and i == 0),
                                           stop=(k == KD - 1 and i == 1))
                    mm.then_inc(lr_summed, 1)

                def hidden(c, m):
                    at_least(pe, relu_done, tile(c, m) - 1)
                    for k in range(KD):
                        for i, part in enumerate((xn_hi, xn_lo)):
                            pe.matmul(fc_ps[m % 2][:, :], fc_T[:, k, m * P:(m + 1) * P], part_of(part, c, k),
                                      start=(k == 0 and i == 0), stop=False)
                    if m == 0:
                        at_least(pe, lr_done, c + 1)
                    pe.matmul(fc_ps[m % 2][:, :], low_out[:, m * P:(m + 1) * P], lr_parts[:, :], start=False, stop=True
                              ).then_inc(fc_summed, 1)

                def project(c, m):
                    at_least(pe, sq_hi_done, tile(c, m) + 1)
                    at_least(pe, sq_lo_done, tile(c, m) + 1)
                    if m == 0:
                        at_least(pe, yT_done, c)
                    for i, part in enumerate((sq_hi, sq_lo)):
                        for k in range(KD):
                            mm = pe.matmul(proj_ps[k][:, :], proj_T[:, m, k * P:(k + 1) * P], part[:, m, :],
                                           start=(m == 0 and i == 0), stop=(m == MT - 1 and i == 1))
                    mm.then_inc(proj_tile, 1)

                def turn_back(c, half):
                    bank = (lr_ps, back_ps)[half]
                    at_least(pe, yT_done, c + 1)
                    if half == 1:
                        at_least(pe, out_ready, 2 * c)
                    for i in range(2):
                        for k in range(KD):
                            r = 2 * half + i
                            mm = pe.transpose(bank[:, (i * KD + k) * P:(i * KD + k + 1) * P],
                                              yT[:, k, r * P:(r + 1) * P], ident[:, :])
                    mm.then_inc(back_turned, 1)

                def step(c):
                    for m in range(MT):
                        if has(c, 0):
                            hidden(c, m)
                        if m == BEHIND and has(c, 1):
                            turn_in(c + 1)
                        if m < BEHIND and has(c, -1):
                            project(c - 1, MT - BEHIND + m)
                        if m >= BEHIND and has(c, 0):
                            project(c, m - BEHIND)
                        if m in (4, 5) and has(c, -1):
                            turn_back(c - 1, m - 4)
                        if m == 6 and has(c, 1):
                            low_rank(c + 1)

                turn_in(0)
                low_rank(0)
                chunk_pipeline(pe, step)

            @block.scalar
            def _(act):
                def norm_y(c):
                    y = y_second if isinstance(c, int) and c == 1 else y_in
                    at_least(act, shift_done, c)
                    for r in range(CH):
                        ins = act.activation(y[:, r, :], y[:, r, :], ACT.Identity, bias=shift_y[:, r:r + 1],
                                             scale=rstd_y[:, r:r + 1])
                    ins.then_inc(yn_done, 1)

                def split_hi(c):
                    at_least(act, x_turned, c + 1)
                    for k in range(KD):
                        ins = act.copy(part_of(xn_hi, c, k), xt_ps[k][:, :])
                    ins.then_inc(xn_hi_done, 1)

                def low_rank_hi(c):
                    at_least(act, lr_summed, c + 1)
                    at_least(act, lr_done, c)
                    act.copy(lr_hi[:, :], lr_ps[:, :]).then_inc(lr_hi_done, 1)

                def relu_tile(c, m):
                    at_least(act, fc_summed, tile(c, m) + 1)
                    at_least(act, sq_done, tile(c, m) - 1)
                    at_least(act, sq_hi_done, tile(c, m) - 1)
                    act.activation(relu[m % 2], fc_ps[m % 2][:, :], ACT.Relu, scale=fc_scale[:, m:m + 1]
                                   ).then_inc(relu_done, 1)

                def square_hi(c, m):
                    at_least(act, relu_done, tile(c, m) + 1)
                    at_least(act, proj_tile, tile(c, m) + 1 - MT)
                    at_least(act, sq_lo_done, tile(c, m) + 1 - MT)
                    act.activation(sq_hi[:, m, :], relu[m % 2], ACT.Square).then_inc(sq_hi_done, 1)

                def result_scaled(c):
                    at_least(act, proj_tile, (c + 1) * MT)
                    at_least(act, back_turned, 2 * c)
                    for k in range(KD):
                        ins = act.mul(yT[:, k, :], proj_ps[k][:, :], proj_scale[:, k:k + 1])
                    ins.then_inc(yT_done, 1)

                def step(c):
                    for m in range(MT):
                        if has(c, 0):
                            if m == 7 and has(c, 1):
                                low_rank_hi(c + 1)
                            relu_tile(c, m)
                            if m >= 1:
                                square_hi(c, m - 1)
                        if m == 0 and has(c, -1):
                            square_hi(c - 1, MT - 1)
                        if m == BEHIND - 1 and has(c, -1):
                            result_scaled(c - 1)
                        if m == BEHIND and has(c, 1):
                            split_hi(c + 1)
                        if m == 5 and has(c, 2):
                            norm_y(c + 2)

                norm_y(1)
                split_hi(0)
                low_rank_hi(0)
                act.wait_ge(y_stored3, 16 * NB)
                chunk_pipeline(act, step)

            @block.gpsimd
            def _(pool):
                def deviation_y(c):
                    at_least(pool, ve_y_done, c + 1)
                    if isinstance(c, int) and c == 1:
                        pool.wait_ge(x2_done, 1)
                    pool.tensor_tensor(rstd_y[:, :], ve_y[:, :], neg_half[:, 0:CH], ALU.pow).then_inc(rstd_y_done, 1)

                def deviation_x(c):
                    at_least(pool, ve_x_done, c + 1)
                    pool.tensor_tensor(rstd_x[:, :], ve_x[:, :], neg_half[:, 0:CH], ALU.pow).then_inc(rstd_x_done, 1)

                def times_gamma(c):
                    y = y_second if isinstance(c, int) and c == 1 else y_in
                    at_least(pool, yn_done, c)
                    pool.tensor_tensor(y[:, :, :], y[:, :, :], gamma_all[:, :].unsqueeze(1).broadcast_to([P, CH, D]),
                                       ALU.mult).then_inc(gamma_done, 1)

                def square_lo(c, m):
                    at_least(pool, sq_done, tile(c, m) + 1)
                    at_least(pool, sq_hi_done, tile(c, m) + 1)
                    at_least(pool, proj_tile, tile(c, m) + 1 - MT)
                    pool.tensor_tensor(sq_lo[:, m, :], sq[m % SQ], sq_hi[:, m, :].bitcast(F32), ALU.subtract
                                       ).then_inc(sq_lo_done, 1)

                def step(c):
                    for m in range(MT):
                        if m == 0 and has(c, 1):
                            deviation_x(c + 1)
                        if m == 4 and has(c, 2):
                            deviation_y(c + 2)
                        if m == 5 and has(c, 2):
                            times_gamma(c + 2)
                        if has(c, 0):
                            square_lo(c, m)

                deviation_y(0)
                deviation_x(0)
                deviation_y(1)
                times_gamma(1)
                chunk_pipeline(pool, step)

            @block.vector
            def _(dve):
                def statistics(source, count, bn, mv, ve, bn_done, mv_done, ve_done, rstd_done):
                    count = known(dve, count)
                    after = known(dve, count + 1)
                    own_waits(dve, ident_made)
                    at_least(dve, mv_done, count)
                    for r in range(CH):
                        ins = dve.bn_stats(bn[:, r, :], source(r))
                    ins.then_inc(bn_done, 1)
                    own_waits(dve, ident_made)
                    at_least(dve, bn_done, after)
                    for r in range(CH):
                        ins = dve.bn_aggr(mv[:, r, :], bn[:, r, :])
                    ins.then_inc(mv_done, 1)
                    at_least(dve, mv_done, after)
                    at_least(dve, rstd_done, count)
                    dve.tensor_scalar(ve[:, :], mv[:, :, 1], EPS, None, ALU.add).then_inc(ve_done, 1)

                def res(c, r):
                    return resid[:, bass.ds(c * CH + r, 1), :].rearrange("p a d -> p (a d)")

                def y_stats(c):
                    y = y_in
                    if isinstance(c, int) and c == 1:
                        y = y_second
                        dve.wait_ge(y_second_loaded, 16)
                    elif isinstance(c, int) and c == 0:
                        dve.wait_ge(y_loaded, 16)
                    else:
                        at_least(dve, y_loaded, 16 * c)
                    statistics(lambda r: y[:, r, :], c, bn_y, mv_y, ve_y, bn_y_done, mv_y_done, ve_y_done, rstd_y_done)

                def shift(c):
                    at_least(dve, rstd_y_done, c + 1)
                    at_least(dve, yn_done, c - 1)
                    dve.scalar_tensor_tensor(out=shift_y[:, :], in0=mv_y[:, :, 0], scalar=-1.0, in1=rstd_y[:, :],
                                             op0=ALU.mult, op1=ALU.mult).then_inc(shift_done, 1)

                def add_y(c):
                    y = y_second if isinstance(c, int) and c == 1 else y_in
                    at_least(dve, gamma_done, c)
                    x2 = resid[:, bass.ds(c * CH, CH), :]
                    dve.tensor_tensor(x2, x2, y[:, :, :], ALU.add).then_inc(x2_done, 1)

                def centre_first():
                    for r in range(CH):
                        ins = dve.scalar_tensor_tensor(out=y_in[:, r, :], in0=y_in[:, r, :], scalar=mv_y[:, r, 0:1],
                                                       in1=gamma_all[:, :], op0=ALU.subtract, op1=ALU.mult)
                    ins.then_inc(centred, 1)

                def add_first():
                    dve.wait_ge(centred, 1)
                    dve.wait_ge(rstd_y_done, 1)
                    for r in range(CH):
                        ins = dve.scalar_tensor_tensor(out=resid[:, r, :], in0=y_in[:, r, :], scalar=rstd_y[:, r:r + 1],
                                                       in1=resid[:, r, :], op0=ALU.mult, op1=ALU.add)
                    ins.then_inc(x2_done, 1)

                def x_stats(c):
                    at_least(dve, x2_done, c + 1)
                    statistics(lambda r: res(c, r), c, bn_x, mv_x, ve_x, bn_x_done, mv_x_done, ve_x_done, rstd_x_done)

                def norm_x(c):
                    at_least(dve, rstd_x_done, c + 1)
                    at_least(dve, x_turned, c)
                    for r in range(CH):
                        ins = dve.tensor_scalar(xn[:, r, :], res(c, r), mv_x[:, r, 0:1], rstd_x[:, r:r + 1],
                                                ALU.subtract, ALU.mult)
                    ins.then_inc(xn_done, 1)

                def split_lo(c):
                    at_least(dve, xn_hi_done, c + 1)
                    for k in range(KD):
                        ins = dve.tensor_tensor(part_of(xn_lo, c, k), xt_ps[k][:, :], part_of(xn_hi, c, k).bitcast(F32),
                                                ALU.subtract)
                    ins.then_inc(xn_lo_done, 1)

                def low_rank_parts(c):
                    at_least(dve, lr_hi_done, c + 1)
                    at_least(dve, fc_summed, c * MT)
                    dve.scalar_tensor_tensor(out=lr_parts[:, :], in0=lr_hi[:, :].bitcast(F32), scalar=minus_lo[:, 0:1],
                                             in1=lr_ps[:, :], op0=ALU.mult, op1=ALU.add).then_inc(lr_done, 1)

                def square(c, m):
                    at_least(dve, relu_done, tile(c, m) + 1)
                    at_least(dve, sq_lo_done, tile(c, m) + 1 - SQ)
                    dve.tensor_tensor(sq[m % SQ], relu[m % 2], relu[m % 2], ALU.mult
                                      ).then_inc(sq_done, 1)

                def result(c, half):
                    at_least(dve, back_turned, 2 * c + half + 1)
                    bank = (lr_ps, back_ps)[half]
                    part = resid[:, bass.ds(c * CH + 2 * half, 2), :]
                    dve.tensor_tensor(part, bank[:, :].rearrange("p (r d) -> p r d", r=2), part, ALU.add
                                      ).then_inc(out_ready, 1)

                def step(c):
                    for m in range(MT):
                        if m == 7 and has(c, 1):
                            low_rank_parts(c + 1)
                        if m == 5 and has(c, 2):
                            shift(c + 2)
                        if m == 0 and has(c, 1):
                            x_stats(c + 1)
                        if has(c, 0):
                            square(c, m)
                        if m == 1 and has(c, 1):
                            norm_x(c + 1)
                        if m == 3 and has(c, 2):
                            y_stats(c + 2)
                        if m == 3 and has(c, 1):
                            split_lo(c + 1)
                        if m in (5, 6) and has(c, -1):
                            result(c - 1, m - 5)
                        if m == 7 and has(c, 2):
                            add_y(c + 2)

                y_stats(0)
                centre_first()
                add_first()
                x_stats(0)
                y_stats(1)
                norm_x(0)
                shift(1)
                split_lo(0)
                low_rank_parts(0)
                add_y(1)
                dve.wait_ge(y_stored3, 16 * NB)
                chunk_pipeline(dve, step)


_INS = ['x', 'ctx_1024', 'L0_xattn_w_sim', 'L0_xattn_b_sim', 'L0_xattn_W_qv', 'L0_xattn_b_qv', 'L0_attn_A',
        'L0_attn_Bp', 'L0_attn_Cp', 'L0_attn_Dp', 'L0_attn_Wg', 'L0_attn_bg', 'L0_attn_gamma', 'L0_attn_beta',
        'L0_ffn_fast_b', 'L0_ffn_w_fc', 'L0_ffn_w_proj', 'L0_ffn_u', 'L0_ffn_v', 'L0_ffn_gate']


def kernel(**inputs):
    import concourse.bacc as _bacc
    from concourse.bass_utils import run_bass_kernel_spmd as _run

    nc = _bacc.Bacc("TRN2", target_bir_lowering=False, num_devices=1)
    arrays, args = {}, []
    for name in _INS:
        a = np.ascontiguousarray(inputs[name])
        if a.ndim == 0:
            a = a.reshape(1)
        arrays[f"in_{name}"] = a
        args.append(nc.dram_tensor(f"in_{name}", a.shape, mybir.dt.from_np(a.dtype), kind="ExternalInput").ap())
    shape = inputs['x'].shape
    args.append(nc.dram_tensor("out_0", shape, F32, kind="ExternalOutput").ap())
    perceiver_layer(nc, *args)
    r = _run(nc, [arrays], core_ids=[0])
    return r.results[0]["out_0"]
```

```python
from contextlib import ExitStack

import numpy as np

import concourse.bass as bass
from concourse import mybir

F32 = mybir.dt.float32
F32R = mybir.dt.float32r
ALU = mybir.AluOpType
ACT = mybir.ActivationFunctionType
AX = mybir.AxisListType

P = 128
EPS = 1e-5


def at_least(eng, sem, count):
    if isinstance(count, int) and count <= 0:
        return
    eng.wait_ge(sem, count)


def known(eng, count):
    return count if isinstance(count, int) else eng.snap(eng.to_reg(count))


def own_waits(eng, ident_made):
    eng.wait_ge(ident_made, 2)


def perceiver_layer(nc, x, ctx, w_sim, b_sim, W_qv, b_qv, A, Bp, Cp, Dp, Wg, bg, gamma, beta,
                    fast_b, w_fc, w_proj, u, v, gate, out):
    BATCH, L, D = x.shape
    J = ctx.shape[1]
    JT = (J - 1) // P
    KD = D // P
    NB = P // L
    GROUPS = BATCH // NB
    N = A.shape[1]
    HID = w_fc.shape[0]
    MT = HID // P
    RANK = u.shape[1]
    CQ = D // NB
    CH = 4
    TOK = CH * P
    CHUNKS = GROUPS // CH
    LAG = L - 1
    assert (L, NB, KD, JT, J) == (32, 4, 2, 2, 257) and D == W_qv.shape[1]

    x_tok = x.rearrange("b t d -> (b t) d")
    out_tok = out.rearrange("b t d -> (b t) d")
    gated_dram = nc.dram_tensor("gated_tokens", [BATCH * L, D], F32, kind="Internal").ap()
    scan_dram = nc.dram_tensor("scan_tokens", [BATCH * L, D], F32, kind="Internal").ap()
    SHIFTS = 8
    impulse_dram = nc.dram_tensor("impulse", [D, SHIFTS, 2 * L], F32, kind="Internal").ap()

    def row(vector):
        return vector.rearrange("(a n) -> a n", a=1)

    def everywhere(vector):
        return bass.AP(tensor=vector.tensor, offset=vector.offset, ap=[[0, P]] + [list(d) for d in vector.ap])

    with ExitStack() as whole:
        def sb(name, shape, dt=F32, scope=whole):
            return scope.enter_context(nc.sbuf_tensor(name, shape, dt))

        def ps(name, scope, shape=(P, 512)):
            return scope.enter_context(nc.psum_tensor(name, list(shape), F32))

        def sem(name):
            return whole.enter_context(nc.semaphore(name))

        resid = sb("resid", [P, GROUPS, D])
        scan_x = sb("scan_x", [P, BATCH, CQ])
        toeplitz = sb("toeplitz", [P, CQ, P])
        ident = sb("ident", [P, P])
        fc_T = sb("fc_T", [P, KD, HID], F32R)
        proj_T = sb("proj_T", [P, MT, D], F32R)
        fc_scale = sb("fc_scale", [P, MT])
        proj_scale = sb("proj_scale", [P, KD])
        low_in = sb("low_in", [P, KD, P], F32R)
        low_out = sb("low_out", [P, HID], F32R)
        minus_lo = sb("minus_lo", [P, 1])
        neg_half = sb("neg_half", [P, 4])
        gamma_all = sb("gamma_all", [P, D])
        xn = sb("xn", [P, CH, D])
        bn_y, bn_x = (sb(n, [P, CH, 6]) for n in ("bn_y", "bn_x"))
        mv_y, mv_x = (sb(n, [P, CH, 2]) for n in ("mv_y", "mv_x"))
        ve_y, ve_x = (sb(n, [P, CH]) for n in ("ve_y", "ve_x"))
        rstd_y, rstd_x = (sb(n, [P, CH]) for n in ("rstd_y", "rstd_x"))
        shift_y = sb("shift_y", [P, CH])
        y_in = sb("y_in", [P, CH, D])

        ident_made = sem("ident_made")
        scan_loaded = sem("scan_loaded")
        gated_stored = [sem(f"gated_stored{p}") for p in range(2)]
        y_loaded = sem("y_loaded")
        y_second_loaded = sem("y_second_loaded")
        y_stored1 = sem("y_stored1")
        y_stored2 = sem("y_stored2")
        y_stored3 = sem("y_stored3")
        toeplitz_loaded = sem("toeplitz_loaded")

        below = sb("below", [P, HID])
        y_second = below[:, :].rearrange("p (r d) -> p r d", r=CH)
        assert CH * D == HID
        early = whole.enter_context(ExitStack())
        fc_in = sb("fc_in", [P, MT, D], scope=early)
        proj_in = sb("proj_in", [P, KD, HID], scope=early)
        thresholds = sb("thresholds", [P, 2, MT + KD], scope=early)
        fc_loaded = sem("fc_loaded")
        proj_loaded = sem("proj_loaded")
        sums_done = sem("sums_done")
        scales_done = sem("scales_done")
        thresholds_done = sem("thresholds_done")
        below_done = sem("below_done")
        ternary_done = sem("ternary_done")

        def magnitudes(dve, scale, w, loaded):
            dve.wait_ge(loaded, 16)
            dve.tensor_reduce(scale, w, AX.X, ALU.add, apply_absolute_value=True).then_inc(sums_done, 1)

        def scales(dve, scale, width, columns, nth):
            dve.wait_ge(sums_done, nth)
            dve.tensor_scalar(scale, scale, 1.0 / width, 1e-5, ALU.mult, ALU.max).then_inc(scales_done, 1)
            dve.wait_ge(scales_done, nth)
            for i, half in enumerate((0.5, -0.5)):
                ins = dve.tensor_scalar(thresholds[:, i, columns], scale, half, None, ALU.mult)
            ins.then_inc(thresholds_done, 1)

        def ternary(dve, i, nth):
            w = fc_in[:, i, :] if i < MT else proj_in[:, i - MT, :]
            b = below[:, 0:D] if i < MT else below[:, :]
            dve.wait_ge(thresholds_done, nth)
            at_least(dve, ternary_done, i)
            dve.tensor_scalar(b, w, thresholds[:, 1, i:i + 1], None, ALU.is_lt).then_inc(below_done, 1)
            dve.wait_ge(below_done, i + 1)
            dve.scalar_tensor_tensor(out=w, in0=w, scalar=thresholds[:, 0, i:i + 1], in1=b,
                                     op0=ALU.is_gt, op1=ALU.subtract).then_inc(ternary_done, 1)

        def scan_load(sp, first_group, groups):
            for q in range(NB):
                rows = gated_dram[bass.ds(first_group * P, groups * P), :]
                src = bass.AP(tensor=rows.tensor, offset=rows.offset + q * CQ,
                              ap=[[D, L], [L * D, groups * NB], [1, CQ]])
                sp.dma_start(scan_x[q * L:(q + 1) * L, bass.ds(first_group * NB, groups * NB), :],
                             src).then_inc(scan_loaded, 16)

        with ExitStack() as one:
            s1 = one
            free_fc = fc_in[:, :, :].rearrange("p m d -> p (m d)")
            free_proj = proj_in[:, :, :].rearrange("p k h -> p (k h)")
            SQUARES = KD * N * N
            states = free_fc[:, 0:KD * (L + 1) * N].rearrange("p (k l n) -> p k l n", k=KD, l=L + 1)
            v_next = free_proj[:, 0:SQUARES].rearrange("p (k m n) -> p k m n", k=KD, m=N)
            a_sb = free_proj[:, SQUARES:2 * SQUARES].rearrange("p (k n) -> p k n", k=KD)
            wg_in = free_proj[:, 2 * SQUARES:2 * SQUARES + KD * D].rearrange("p (k d) -> p k d", k=KD)
            ends = free_proj[:, HID * KD - D:]
            ctxn = [sb(f"ctxn{p}", [P, NB, JT, D], scope=s1) for p in range(2)]
            ctx_end = [sb(f"ctx_end{p}", [P, D], scope=s1) for p in range(2)]
            ctxT = sb("ctxT", [P, NB, KD, J], scope=s1)
            endsT = sb("endsT", [P, KD, BATCH], scope=s1)
            wqv_raw = scan_x[:, BATCH - 4 * KD * D // CQ:, :].rearrange("p (k i) c -> p k (i c)", k=4 * KD)
            wqv_hi = proj_T[:, :, :]
            wqv_lo = fc_T[:, :, :].rearrange("p k (j d) -> p (k j) d", d=D)
            assert MT == 4 * KD == KD * HID // D
            wgT = sb("wgT", [P, KD, D], scope=s1)
            w1_all = sb("w1_all", [P, D], scope=s1)
            bqv_all = sb("bqv_all", [P, D], scope=s1)
            bg_all = sb("bg_all", [P, D], scope=s1)
            beta_all = sb("beta_all", [P, D], scope=s1)
            w23 = sb("w23", [P, 2, KD], scope=s1)
            bsim_all = sb("bsim_all", [P, 1], scope=s1)
            same_batch = sb("same_batch", [P, P], scope=s1)
            hc = [sb(f"hc{p}", [P, D], scope=s1) for p in range(2)]
            hc_probT = [sb(f"hc_probT{p}", [P, 2, 2, P], scope=s1) for p in range(2)]
            hcwT = sb("hcwT", [P, KD, P], scope=s1)
            prob = [sb(f"prob{p}", [P, J], scope=s1) for p in range(2)]
            pick = sb("pick", [P, P], scope=s1)
            hqbT = sb("hqbT", [P, 2, KD, P], scope=s1)
            hcqT = sb("hcqT", [P, KD, P], scope=s1)
            hc_hi, hc_lo, hcq_hi, hcq_lo = (sb(n, [P, KD, P], F32R, scope=s1) for n in ("hc_hi", "hc_lo", "hcq_hi", "hcq_lo"))
            hqb_hi, hqb_lo = (sb(n, [P, 2, KD, P], F32R, scope=s1) for n in ("hqb_hi", "hqb_lo"))
            z = sb("z", [P, D], scope=s1)
            zT = sb("zT", [P, KD, P], scope=s1)
            gate_in, gate_th, dots = (y_in[:, i, :] for i in range(3))
            hq, hb = (xn[:, i, :] for i in range(2))
            gated = [sb(f"gated{p}", [P, D], scope=s1) for p in range(2)]
            bn1 = sb("bn1", [P, 6], scope=s1)
            mv1 = sb("mv1", [P, 2], scope=s1)
            ve1 = sb("ve1", [P, 1], scope=s1)
            rstd1 = sb("rstd1", [P, 1], scope=s1)
            bn2 = sb("bn2", [P, 6], scope=s1)
            mv2 = sb("mv2", [P, 2], scope=s1)
            ve2 = sb("ve2", [P, 1], scope=s1)
            rstd2 = sb("rstd2", [P, 1], scope=s1)
            s1_b = [sb(f"s1_b{p}", [P, 1], scope=s1) for p in range(2)]
            s1_dot = sb("s1_dot", [P, 1], scope=s1)
            neg_max = sb("neg_max", [P, 1], scope=s1)
            row_sum = sb("row_sum", [P, 1], scope=s1)
            row_rec = sb("row_rec", [P, 1], scope=s1)
            best = sb("best", [P, 1], scope=s1)
            bestT = sb("bestT", [P, L], scope=s1)
            neg_top = sb("neg_top", [P, 1], scope=s1)
            top_e = sb("top_e", [P, 1], scope=s1)
            top_eT = sb("top_eT", [P, L], scope=s1)
            top_sum = sb("top_sum", [P, 1], scope=s1)
            top_rec = sb("top_rec", [P, 1], scope=s1)
            c_sb = sb("c_sb", [P, KD, N], scope=s1)
            d_sb = sb("d_sb", [P, KD], scope=s1)
            v_new = sb("v_new", [P, KD, N], scope=s1)
            impulse = sb("impulse_sb", [P, KD, 2 * L], scope=s1)

            turn_ps = [ps(f"turn_ps{i}", s1) for i in range(2)]
            score_ps = ps("score_ps", s1)
            side_ps = ps("side_ps", s1)
            att_ps = ps("att_ps", s1)
            feat_ps = ps("feat_ps", s1)
            qv_ps = ps("qv_ps", s1)
            gate_ps = ps("gate_ps", s1)

            consts_loaded = sem("consts_loaded")
            late_loaded = sem("late_loaded")
            states_in = sem("states_in")
            x_loaded = [sem(f"x_loaded{p}") for p in range(2)]
            ctx_loaded = [sem(f"ctx_loaded{p}") for p in range(2)]
            end_loaded = [sem(f"end_loaded{p}") for p in range(2)]
            masks_made = sem("masks_made")
            zeroed = sem("zeroed")
            wg_turned = sem("wg_turned")
            wgT_ready = sem("wgT_ready")
            ends_turned = sem("ends_turned")
            endsT_ready = sem("endsT_ready")
            bn1_done, mv1_done, ve1_done, rstd1_done = (sem(n) for n in ("bn1_done", "mv1_done", "ve1_done", "rstd1_done"))
            bn2_done, mv2_done, ve2_done, rstd2_done = (sem(n) for n in ("bn2_done", "mv2_done", "ve2_done", "rstd2_done"))
            hc_ready = sem("hc_ready")
            dot_done = sem("dot_done")
            s1_ready = sem("s1_ready")
            bqv_added = sem("bqv_added")
            side_turned = sem("side_turned")
            side_copied = sem("side_copied")
            hcwT_ready = sem("hcwT_ready")
            ctx_turned = sem("ctx_turned")
            ctxT_copied = sem("ctxT_copied")
            end_placed = sem("end_placed")
            scored = sem("scored")
            neg_max_ready = sem("neg_max_ready")
            best_ready = sem("best_ready")
            bestT_ready = sem("bestT_ready")
            neg_top_ready = sem("neg_top_ready")
            exp_done = sem("exp_done")
            row_rec_ready = sem("row_rec_ready")
            prob_ready = sem("prob_ready")
            top_done = sem("top_done")
            top_rec_ready = sem("top_rec_ready")
            pick_ready = sem("pick_ready")
            pooled = sem("pooled")
            attended = sem("attended")
            hq_ready = sem("hq_ready")
            hb_ready = sem("hb_ready")
            hqb_turned = sem("hqb_turned")
            hqbT_ready = sem("hqbT_ready")
            hcqT_ready = sem("hcqT_ready")
            hc_hi_ready, hc_lo_ready = sem("hc_hi_ready"), sem("hc_lo_ready")
            hqb_hi_ready, hqb_lo_ready = sem("hqb_hi_ready"), sem("hqb_lo_ready")
            hcq_hi_ready, hcq_lo_ready = sem("hcq_hi_ready"), sem("hcq_lo_ready")
            wqv_hi_ready, wqv_lo_ready = sem("wqv_hi_ready"), sem("wqv_lo_ready")
            projected = sem("projected")
            x1_ready = sem("x1_ready")
            z_ready = sem("z_ready")
            beta_added = sem("beta_added")
            z_turned = sem("z_turned")
            zT_ready = sem("zT_ready")
            gate_summed = sem("gate_summed")
            gate_in_ready = sem("gate_in_ready")
            tanh_done = sem("tanh_done")
            gated_ready = sem("gated_ready")
            v_next_ready = sem("v_next_ready")
            v_new_ready = sem("v_new_ready")
            state_kept = sem("state_kept")
            imp_dot = sem("imp_dot")
            imp_sum = sem("imp_sum")
            imp_first = sem("imp_first")
            impulse_ready = sem("impulse_ready")
            impulse_stored = sem("impulse_stored")

            CONSTS = 4
            LATE = 7
            STATE_LOADS = 4
            STATE_COUNTS = {1: (0,), 2: (1, 2), 3: (3, 4)}
            assert GROUPS - 2 + 1 == L - 1
            FIRST = 4

            def software_pipeline(eng, step):
                for i in range(FIRST):
                    step(i, 0, STATE_COUNTS.get(i, ()))
                with eng.Fori(FIRST // 2, GROUPS // 2 - 1) as pair:
                    for k in range(2):
                        step(pair * 2, k, (pair * 2 + k + 1,))
                for i in range(GROUPS - 2, GROUPS + 2):
                    step(i, 0, ())

            def stages(base, k):
                g = base + k
                if isinstance(g, int):
                    return g, g % 2, g < GROUPS, 1 <= g <= GROUPS, g >= 2
                return g, k, True, True, True

            def min_groups(g):
                return min(g, GROUPS) if isinstance(g, int) else g

            def sixteen(base, k, back):
                if isinstance(base, int):
                    return 16 * ((base + k - back) // 2 + 1)
                return base * 8 + 16 * ((k - back) // 2 + 1)

            block = one.enter_context(nc.Block())

            @block.sync
            def _(sp):
                def load_x(g, p):
                    sp.dma_start(resid[:, bass.ds(g, 1), :].rearrange("p a d -> p (a d)"),
                                 x_tok[bass.ds(g * P, P), :]).then_inc(x_loaded[p], 16)

                def load_ctx(g, p):
                    sp.dma_start(ctxn[p][:, :, :, :],
                                 ctx[bass.ds(g * NB, NB), 0:J - 1, :].rearrange("b (q t) d -> q b t d", t=JT)
                                 ).then_inc(ctx_loaded[p], 16)

                def load_end(g, p):
                    rows = ctx[bass.ds(g * NB, NB), J - 1, :]
                    src = bass.AP(tensor=rows.tensor, offset=rows.offset, ap=[[J * D, NB], [0, L], [1, D]])
                    sp.dma_start(ctx_end[p][:, :], src).then_inc(end_loaded[p], 16)

                load_x(0, 0)
                load_ctx(0, 0)
                sp.dma_start(ends[:, :], ctx[:, J - 1, :]).then_inc(consts_loaded, 16)
                sp.dma_start(w23[:, :, :], bass.AP(tensor=w_sim.tensor, offset=D, ap=[[1, P], [D, 2], [P, KD]]),
                             allow_slow_non_contiguous=True).then_inc(consts_loaded, 16)
                sp.dma_start(w1_all[:, :], everywhere(w_sim[0:D])).then_inc(consts_loaded, 16)
                sp.dma_start(bsim_all[:, :], everywhere(b_sim)).then_inc(consts_loaded, 16)
                load_end(0, 0)
                load_x(1, 1)
                load_ctx(1, 1)
                load_end(1, 1)
                sp.dma_start(wqv_raw, W_qv.rearrange("(k p) n -> p k n", p=P)).then_inc(late_loaded, 16)
                sp.dma_start(wg_in[:, :, :], Wg.rearrange("(k p) n -> p k n", p=P)).then_inc(late_loaded, 16)
                sp.dma_start(bqv_all[:, :], everywhere(b_qv)).then_inc(late_loaded, 16)
                sp.dma_start(bg_all[:, :], everywhere(bg)).then_inc(late_loaded, 16)
                sp.dma_start(beta_all[:, :], everywhere(beta)).then_inc(late_loaded, 16)
                sp.dma_start(gamma_all[:, :], everywhere(gamma)).then_inc(late_loaded, 16)
                sp.dma_start(d_sb[:, :], Dp.rearrange("(k p) -> p k", p=P),
                             allow_slow_non_contiguous=True).then_inc(late_loaded, 16)
                sp.dma_start(a_sb[:, :, :], A.rearrange("(k p) n m -> p k (n m)", p=P)).then_inc(states_in, 16)
                sp.dma_start(v_new[:, :, :], Bp.rearrange("(k p) n -> p k n", p=P)).then_inc(states_in, 16)
                sp.dma_start(states[:, :, 0, :], Bp.rearrange("(k p) n -> p k n", p=P)).then_inc(states_in, 16)
                sp.dma_start(c_sb[:, :, :], Cp.rearrange("(k p) n -> p k n", p=P)).then_inc(states_in, 16)

                def step(base, k, _):
                    g, p, has_a, has_b, has_c = stages(base, k)
                    inside = not isinstance(g, int)
                    if inside or g + 2 < GROUPS:
                        at_least(sp, hc_ready, g + 1)
                        load_x(g + 2, p)
                        at_least(sp, attended, g + 1)
                        load_ctx(g + 2, p)
                        at_least(sp, hq_ready, g + 1)
                        load_end(g + 2, p)
                    if has_c:
                        at_least(sp, gated_ready, g - 1)
                        sp.dma_start(gated_dram[bass.ds((g - 2) * P, P), :], gated[p][:, :]
                                     ).then_inc(gated_stored[p], 16)

                for i in range(2):
                    step(i, 0, ())

                def scan_load_pair(base):
                    sp.wait_ge(gated_stored[0], base * 8 - 16)
                    sp.wait_ge(gated_stored[1], base * 8 - 16)
                    scan_load(sp, base - 4, 2)

                def body(base):
                    step(base, 0, ())
                    if not isinstance(base, int) or base >= 4:
                        scan_load_pair(base)
                    step(base, 1, ())

                body(2)
                with sp.Fori(FIRST // 2, GROUPS // 2 - 1) as pair:
                    body(pair * 2)
                def toeplitz_load(q):
                    for first in range(0, L, SHIFTS):
                        src = bass.AP(tensor=impulse_dram.tensor, offset=q * CQ * SHIFTS * 2 * L + LAG - first,
                                      ap=[[2 * L - 1, SHIFTS], [SHIFTS * 2 * L, CQ], [1, L]])
                        sp.dma_start(toeplitz[q * L + first:q * L + first + SHIFTS, :, q * L:(q + 1) * L], src
                                     ).then_inc(toeplitz_loaded, 16)

                step(GROUPS - 2, 0, ())
                scan_load_pair(GROUPS - 2)
                sp.wait_ge(impulse_ready, 1)
                for c in range(KD):
                    sp.dma_start(impulse_dram[c * P:(c + 1) * P, :, :],
                                 impulse[:, c, :].unsqueeze(1).broadcast_to([P, SHIFTS, 2 * L])).then_inc(impulse_stored, 16)
                sp.dma_start(fc_in[:, :, :], w_fc.rearrange("(m p) d -> p m d", p=P)).then_inc(fc_loaded, 16)
                sp.dma_start(proj_in[:, :, :], w_proj.rearrange("(k p) h -> p k h", p=P)).then_inc(proj_loaded, 16)
                sp.wait_ge(impulse_stored, 16 * KD)
                sp.wait_ge(zeroed, FIRST)
                toeplitz_load(0)
                toeplitz_load(1)
                step(GROUPS - 1, 0, ())
                scan_load_pair(GROUPS)
                toeplitz_load(2)
                toeplitz_load(3)
                step(GROUPS, 0, ())
                sp.wait_ge(scan_loaded, 16 * NB * (GROUPS // 2 - 1))
                sp.wait_ge(gated_stored[0], 16 * (GROUPS // 2))
                scan_load(sp, GROUPS - 2, 1)
                step(GROUPS + 1, 0, ())

            @block.tensor
            def _(pe):
                pe.wait_ge(ident_made, 2)

                def turn_context(g, p, b):
                    at_least(pe, ctxT_copied, g * 4 + b - 1)
                    for c in range(KD):
                        for t in range(JT):
                            mm = pe.transpose(turn_ps[b % 2][:, (c * JT + t) * P:(c * JT + t + 1) * P],
                                              ctxn[p][:, b, t, c * P:(c + 1) * P], ident[:, :])
                    mm.then_inc(ctx_turned, 1)

                def step(base, k, _):
                    g, p, has_a, has_b, has_c = stages(base, k)
                    o = 1 - p
                    if has_a or has_b:
                        at_least(pe, side_copied, g)
                        if has_a:
                            at_least(pe, hc_ready, g + 1)
                            for c in range(KD):
                                mm = pe.transpose(side_ps[:, c * P:(c + 1) * P], hc[p][:, c * P:(c + 1) * P], ident[:, :])
                        if has_b:
                            at_least(pe, prob_ready, g)
                            for t in range(JT):
                                mm = pe.transpose(side_ps[:, 256 + t * P:256 + (t + 1) * P],
                                                  prob[o][:, t * P:(t + 1) * P], ident[:, :])
                        mm.then_inc(side_turned, 1)
                    if has_b:
                        at_least(pe, pick_ready, g)
                        at_least(pe, gate_in_ready, g - 2)
                        if isinstance(g, int) and g == 2:
                            pe.wait_ge(wgT_ready, 1)
                        pe.matmul(gate_ps[:, 256:256 + D], pick[:, :], hc[o][:, :], start=True, stop=True
                                  ).then_inc(pooled, 1)
                    if has_a:
                        at_least(pe, ctx_loaded[p], sixteen(base, k, 0))
                        turn_context(g, p, 0)
                        turn_context(g, p, 1)
                        if isinstance(g, int) and g == 0:
                            pe.wait_ge(consts_loaded, 16 * CONSTS)
                            for c in range(KD):
                                mm = pe.transpose(feat_ps[:, c * P:(c + 1) * P], ends[:, c * P:(c + 1) * P], ident[:, :])
                            mm.then_inc(ends_turned, 1)
                    if has_b:
                        at_least(pe, side_copied, g + 1)
                        at_least(pe, hq_ready, g - 1)
                        for t in range(JT):
                            for b in range(NB):
                                mm = pe.matmul(att_ps[b * L:(b + 1) * L, 0:D], hc_probT[p][:, 1, t, b * L:(b + 1) * L],
                                               ctxn[o][:, b, t, :], start=(t == 0), stop=(t == JT - 1))
                        mm.then_inc(attended, 1)
                    if has_a:
                        turn_context(g, p, 2)
                        turn_context(g, p, 3)
                    if has_c:
                        at_least(pe, z_ready, g - 1)
                        at_least(pe, x1_ready, g - 1)
                        for c in range(KD):
                            mm = pe.transpose(qv_ps[:, 256 + c * P:256 + (c + 1) * P], z[:, c * P:(c + 1) * P],
                                              ident[:, :])
                        mm.then_inc(z_turned, 1)
                    if has_b:
                        if isinstance(g, int) and g == 1:
                            pe.wait_ge(endsT_ready, 1)
                        at_least(pe, hqb_hi_ready, g - 1)
                        for i, (part, ready) in enumerate(((hb, hb_ready), (hq, hq_ready))):
                            at_least(pe, ready, g)
                            for c in range(KD):
                                mm = pe.transpose(feat_ps[:, ((1 - i) * KD + c) * P:((1 - i) * KD + c + 1) * P],
                                                  part[:, c * P:(c + 1) * P], ident[:, :])
                        mm.then_inc(hqb_turned, 1)
                    if has_a:
                        at_least(pe, ctxT_copied, g * 4 + 4)
                        at_least(pe, end_placed, g + 1)
                        at_least(pe, hcwT_ready, g + 1)
                        at_least(pe, neg_max_ready, g)
                        at_least(pe, exp_done, g)
                        for c in range(KD):
                            for b in range(NB):
                                mm = pe.matmul(score_ps[b * L:(b + 1) * L, 0:J], hcwT[:, c, b * L:(b + 1) * L],
                                               ctxT[:, b, c, :], start=(c == 0), stop=(c == KD - 1))
                        mm.then_inc(scored, 1)
                    if has_c:
                        at_least(pe, zT_ready, g - 1)
                        at_least(pe, hb_ready, min_groups(g))
                        for c in range(KD):
                            mm = pe.matmul(gate_ps[:, 0:D], zT[:, c, :], wgT[:, c, :], start=(c == 0), stop=(c == KD - 1))
                        mm.then_inc(gate_summed, 1)
                    if has_b:
                        if has_c:
                            at_least(pe, zT_ready, g - 1)
                        if isinstance(g, int) and g == 1:
                            pe.wait_ge(late_loaded, 16 * LATE)
                            for e in range(KD):
                                for c in range(KD):
                                    mm = pe.transpose(gate_ps[:, (c * KD + e) * P:(c * KD + e + 1) * P],
                                                      wg_in[:, e, c * P:(c + 1) * P], ident[:, :])
                            mm.then_inc(wg_turned, 1)
                            pe.wait_ge(wqv_lo_ready, 1)
                        feats = ((hc_hi, hc_lo), (hqb_hi[:, 1], hqb_lo[:, 1]), (hqb_hi[:, 0], hqb_lo[:, 0]), (hcq_hi, hcq_lo))
                        ready = ((hc_hi_ready, hc_lo_ready), (hqb_hi_ready, hqb_lo_ready), None, (hcq_hi_ready, hcq_lo_ready))
                        rows = (0, 3, 1, 2)
                        for f in range(4):
                            if ready[f]:
                                at_least(pe, ready[f][0], g)
                            for i, w in ((0, wqv_hi), (0, wqv_lo), (1, wqv_hi)):
                                if ready[f] and i == 1:
                                    at_least(pe, ready[f][1], g)
                                for c in range(KD):
                                    mm = pe.matmul(qv_ps[:, 0:D], feats[f][i][:, c, :], w[:, rows[f] * KD + c, :],
                                                   start=(f == 0 and i == 0 and c == 0 and w is wqv_hi),
                                                   stop=(f == 3 and i == 1 and c == KD - 1))
                        mm.then_inc(projected, 1)

                software_pipeline(pe, step)

            @block.scalar
            def _(act):
                def step(base, k, _):
                    g, p, has_a, has_b, has_c = stages(base, k)
                    o = 1 - p
                    if has_a or has_b:
                        at_least(act, side_turned, g + 1)
                        at_least(act, hc_lo_ready, g - 1)
                        at_least(act, hcqT_ready, g - 1)
                        at_least(act, attended, g - 2)
                        first, last = (0 if has_a else 1), (2 if has_b else 1)
                        act.copy(hc_probT[p][:, first:last, :, :],
                                 side_ps[:, first * 256:last * 256].rearrange("p (f k t) -> p f k t", f=last - first, k=2)
                                 ).then_inc(side_copied, 1)
                    if has_b:
                        at_least(act, side_copied, g)
                        at_least(act, projected, g - 1)
                        at_least(act, hc_lo_ready, g - 1)
                        act.copy(hc_hi[:, :, :], hc_probT[o][:, 0, :, :]).then_inc(hc_hi_ready, 1)
                    if has_a:
                        at_least(act, scored, g)
                        for b in range(NB):
                            at_least(act, ctx_turned, g * 4 + b + 1)
                            act.copy(ctxT[:, b, :, 0:J - 1], turn_ps[b % 2][:, :].rearrange("p (k j) -> p k j", k=KD)
                                     ).then_inc(ctxT_copied, 1)
                            if b == 1:
                                if isinstance(g, int) and g == 0:
                                    act.wait_ge(ends_turned, 1)
                                    act.copy(endsT[:, :, :], feat_ps[:, 0:KD * BATCH].rearrange("p (k b) -> p k b", k=KD)
                                             ).then_inc(endsT_ready, 1)
                                    act.wait_ge(consts_loaded, 16 * CONSTS)
                                at_least(act, side_copied, g + 1)
                                for c in range(KD):
                                    ins = act.activation(hcwT[:, c, :], hc_probT[p][:, 0, c, :], ACT.Identity,
                                                         bias=w23[:, 0, c:c + 1], scale=w23[:, 1, c:c + 1])
                                ins.then_inc(hcwT_ready, 1)
                    if has_c:
                        at_least(act, z_turned, g - 1)
                        at_least(act, gate_summed, g - 2)
                        act.copy(zT[:, :, :], qv_ps[:, 256:256 + D].rearrange("p (k t) -> p k t", k=KD)).then_inc(zT_ready, 1)
                    if has_b:
                        at_least(act, hqb_turned, g)
                        at_least(act, hqb_lo_ready, g - 1)
                        at_least(act, hcqT_ready, g - 1)
                        act.copy(hqbT[:, :, :, :], feat_ps[:, :].rearrange("p (f k t) -> p f k t", f=2, k=KD)
                                 ).then_inc(hqbT_ready, 1)
                        at_least(act, projected, g - 1)
                        act.copy(hqb_hi[:, :, :, :], feat_ps[:, :].rearrange("p (f k t) -> p f k t", f=2, k=KD)
                                 ).then_inc(hqb_hi_ready, 1)
                    if isinstance(g, int) and g == 1:
                        act.wait_ge(wg_turned, 1)
                        act.copy(wgT[:, :, :], gate_ps[:, :].rearrange("p (k e) -> p k e", k=KD)).then_inc(wgT_ready, 1)
                    if has_a:
                        at_least(act, neg_max_ready, g + 1)
                        at_least(act, scored, g + 1)
                        at_least(act, side_turned, g)
                        at_least(act, hq_ready, g - 1)
                        at_least(act, row_rec_ready, g)
                        act.activation(prob[p][:, :], score_ps[:, 0:J], ACT.Exp, bias=neg_max[:, 0:1],
                                       accum_out=row_sum[:, 0:1]).then_inc(exp_done, 1)
                    if has_b:
                        at_least(act, hcqT_ready, g)
                        at_least(act, projected, g - 1)
                        at_least(act, hcq_lo_ready, g - 1)
                        act.copy(hcq_hi[:, :, :], hcqT[:, :, :]).then_inc(hcq_hi_ready, 1)
                    if has_c:
                        at_least(act, gate_in_ready, g - 1)
                        at_least(act, gated_ready, g - 2)
                        act.activation(gate_th, gate_in, ACT.Tanh, scale=0.5).then_inc(tanh_done, 1)
                    if has_a:
                        at_least(act, neg_top_ready, g + 1)
                        at_least(act, pick_ready, g)
                        act.activation(top_e[:, :], best[:, :], ACT.Exp, bias=neg_top[:, 0:1])
                        at_least(act, top_done, g)
                        act.activation(top_eT[:, :], bestT[:, :], ACT.Exp, bias=neg_top[:, 0:1],
                                       accum_out=top_sum[:, 0:1]).then_inc(top_done, 1)

                    if isinstance(g, int) and g == 0:
                        act.wait_ge(late_loaded, 16 * LATE)
                        act.copy(wqv_hi, wqv_raw).then_inc(wqv_hi_ready, 1)

                software_pipeline(act, step)

            @block.gpsimd
            def _(pool):
                pool.memset(ident[:, :], 0.0).then_inc(ident_made, 1)
                pool.memset(neg_half[:, :], -0.5)
                pool.memset(same_batch[:, :], 0.0).then_inc(masks_made, 1)
                pool.wait_ge(ident_made, 1)
                pool.affine_select(out=ident[:, :], in_=ident[:, :], compare_op=ALU.not_equal, fill=1.0, base=0,
                                   pattern=[[-1, P]], channel_multiplier=1).then_inc(ident_made, 1)
                pool.wait_ge(masks_made, 1)
                pool.wait_ge(ident_made, 2)
                for b in range(NB):
                    last = pool.memset(same_batch[b * L:(b + 1) * L, b * L:(b + 1) * L], 1.0)
                last.then_inc(masks_made, 1)
                pool.wait_ge(masks_made, 2)

                def inverse_deviation(dst, src, ready, made, count):
                    at_least(pool, ready, count)
                    pool.tensor_tensor(dst, src, neg_half[:, 0:1], ALU.pow).then_inc(made, 1)

                def state_product(count):
                    at_least(pool, v_new_ready, count)
                    pool.tensor_tensor(v_next[:, :, :, :].rearrange("p k m n -> p k m n"),
                                       a_sb[:, :, :].rearrange("p k (n m) -> p k m n", n=N),
                                       v_new[:, :, :].unsqueeze(2).broadcast_to([P, KD, N, N]),
                                       ALU.mult).then_inc(v_next_ready, 1)

                def step(base, k, state_steps):
                    g, p, has_a, has_b, has_c = stages(base, k)
                    inside = not isinstance(g, int)
                    o = 1 - p
                    if has_a:
                        if not inside and g == 0:
                            pool.wait_ge(endsT_ready, 1)
                        at_least(pool, scored, g)
                        pool.tensor_copy(ctxT[:, :, :, J - 1],
                                         endsT[:, :, bass.ds(g * NB, NB)].rearrange("p k b -> p b k")
                                         ).then_inc(end_placed, 1)
                    if has_c:
                        at_least(pool, z_ready, g - 2)
                        inverse_deviation(rstd2[:, :], ve2[:, :], ve2_done, rstd2_done, g - 1)
                    if has_b:
                        low_part(hc_lo[:, :, :], hc_probT[o][:, 0, :, :], hc_hi[:, :, :], hc_hi_ready, hc_lo_ready, g)
                    if inside or g + 1 < GROUPS:
                        at_least(pool, hc_ready, g + 1)
                        inverse_deviation(rstd1[:, :], ve1[:, :], ve1_done, rstd1_done, g + 2)
                    if not inside and g == 1:
                        pool.wait_ge(states_in, 16 * STATE_LOADS)
                    for s in state_steps[:1]:
                        state_product(s)
                    if not inside and g == GROUPS - 2:
                        pool.wait_ge(state_kept, L - 1)
                        w = states[:, :, 0:L, :]
                        pool.tensor_tensor(w, w, c_sb[:, :, :].unsqueeze(2).broadcast_to([P, KD, L, N]), ALU.mult
                                           ).then_inc(imp_dot, 1)
                    if has_b:
                        at_least(pool, hqbT_ready, g)
                        at_least(pool, side_copied, g)
                        at_least(pool, hcq_hi_ready, g - 1)
                        pool.tensor_tensor(hcqT[:, :, :], hqbT[:, 0, :, :], hc_probT[o][:, 0, :, :], ALU.mult
                                           ).then_inc(hcqT_ready, 1)
                    if has_b:
                        low_part(hqb_lo[:, :, :, :], hqbT[:, :, :, :], hqb_hi[:, :, :, :], hqb_hi_ready, hqb_lo_ready, g)
                        low_part(hcq_lo[:, :, :], hcqT[:, :, :], hcq_hi[:, :, :], hcq_hi_ready, hcq_lo_ready, g)
                    for s in state_steps[1:]:
                        state_product(s)
                    if has_c:
                        at_least(pool, z_ready, g - 1)
                        r = resid[:, bass.ds(g - 2, 1), :].rearrange("p a d -> p (a d)")
                        pool.tensor_tensor(r, r, beta_all[:, :], ALU.add).then_inc(beta_added, 1)
                    if not inside and g == 0:
                        pool.wait_ge(late_loaded, 16 * LATE)
                        add_bqv(0)
                    if inside or g + 1 < GROUPS:
                        add_bqv(g + 1)
                    if not inside and g < FIRST:
                        part = CQ // FIRST
                        pool.memset(toeplitz[:, g * part:(g + 1) * part, :], 0.0).then_inc(zeroed, 1)

                def low_part(lo, full, hi, hi_ready, lo_ready, count):
                    at_least(pool, hi_ready, count)
                    at_least(pool, projected, count - 1)
                    pool.tensor_tensor(lo, full, hi.bitcast(F32), ALU.subtract).then_inc(lo_ready, 1)

                def add_bqv(g):
                    at_least(pool, hc_ready, g + 1)
                    r = resid[:, bass.ds(g, 1), :].rearrange("p a d -> p (a d)")
                    pool.tensor_tensor(r, r, bqv_all[:, :], ALU.add).then_inc(bqv_added, 1)

                inverse_deviation(rstd1[:, :], ve1[:, :], ve1_done, rstd1_done, 1)
                pool.memset(impulse[:, :, :], 0.0)
                software_pipeline(pool, step)

            @block.vector
            def _(dve):
                def layer_norm1(g, p, count):
                    count = known(dve, count)
                    after = known(dve, count + 1)
                    own_waits(dve, ident_made)
                    at_least(dve, mv1_done, count)
                    dve.bn_stats(bn1[:, :], resid[:, bass.ds(g, 1), :].rearrange("p a d -> p (a d)")).then_inc(bn1_done, 1)
                    own_waits(dve, ident_made)
                    at_least(dve, bn1_done, after)
                    at_least(dve, hc_ready, count)
                    dve.bn_aggr(mv1[:, :], bn1[:, :]).then_inc(mv1_done, 1)
                    at_least(dve, mv1_done, after)
                    at_least(dve, rstd1_done, count)
                    dve.tensor_scalar(ve1[:, :], mv1[:, 1:2], EPS, None, ALU.add).then_inc(ve1_done, 1)

                def normalise1(g, p, count):
                    at_least(dve, rstd1_done, count + 1)
                    at_least(dve, pooled, count - 1)
                    at_least(dve, hb_ready, count - 1)
                    at_least(dve, side_turned, count - 1)
                    at_least(dve, dot_done, count)
                    at_least(dve, s1_ready, count)
                    dve.tensor_scalar(hc[p][:, :], resid[:, bass.ds(g, 1), :].rearrange("p a d -> p (a d)"),
                                      mv1[:, 0:1], rstd1[:, 0:1], ALU.subtract, ALU.mult).then_inc(hc_ready, 1)
                    at_least(dve, hc_ready, count + 1)
                    if isinstance(g, int) and g == 0:
                        dve.wait_ge(consts_loaded, 16 * CONSTS)
                    dve.tensor_tensor_reduce(out=dots, in0=hc[p][:, :], in1=w1_all[:, :], scale=1.0, scalar=0.0,
                                             op0=ALU.mult, op1=ALU.add, accum_out=s1_dot[:, :]).then_inc(dot_done, 1)
                    at_least(dve, dot_done, count + 1)
                    at_least(dve, best_ready, count - 1)
                    dve.tensor_scalar(s1_b[p][:, :], s1_dot[:, :], bsim_all[:, 0:1], None, ALU.add).then_inc(s1_ready, 1)

                def state_sum(count):
                    at_least(dve, v_next_ready, count + 1)
                    at_least(dve, state_kept, count)
                    dve.tensor_reduce(v_new[:, :, :], v_next[:, :, :, :], AX.X, ALU.add).then_inc(v_new_ready, 1)

                def impulse_response():
                    dve.wait_ge(imp_dot, 1)
                    dve.wait_ge(zeroed, FIRST)
                    dve.tensor_reduce(impulse[:, :, LAG:LAG + L], states[:, :, 0:L, :], AX.X, ALU.add).then_inc(imp_sum, 1)
                    dve.wait_ge(imp_sum, 1)
                    dve.scalar_tensor_tensor(out=impulse[:, :, LAG], in0=d_sb[:, :], scalar=1.0, in1=impulse[:, :, LAG],
                                             op0=ALU.add, op1=ALU.add).then_inc(imp_first, 1)
                    dve.wait_ge(imp_first, 1)
                    dve.tensor_scalar(impulse[:, :, LAG:LAG + L], impulse[:, :, LAG:LAG + L], 0.5, None, ALU.mult).then_inc(impulse_ready, 1)

                def state_keep(count):
                    at_least(dve, v_new_ready, count + 1)
                    dve.tensor_copy(states[:, :, bass.ds(count + 1, 1), :].rearrange("p k a n -> p k (a n)"),
                                    v_new[:, :, :]).then_inc(state_kept, 1)

                def step(base, k, state_steps):
                    g, p, has_a, has_b, has_c = stages(base, k)
                    inside = not isinstance(g, int)
                    o = 1 - p
                    if isinstance(g, int) and g == 1:
                        dve.wait_ge(wqv_hi_ready, 1)
                        dve.tensor_tensor(wqv_lo, wqv_raw, wqv_hi.bitcast(F32), ALU.subtract).then_inc(wqv_lo_ready, 1)
                    if isinstance(g, int) and g == 2:
                        dve.wait_ge(late_loaded, 16 * LATE)
                    if has_c:
                        at_least(dve, projected, g - 1)
                        at_least(dve, bqv_added, g - 1)
                        r = resid[:, bass.ds(g - 2, 1), :].rearrange("p a d -> p (a d)")
                        dve.tensor_tensor(r, qv_ps[:, 0:D], r, ALU.add).then_inc(x1_ready, 1)
                        done, before = known(dve, g - 1), known(dve, g - 2)
                        own_waits(dve, ident_made)
                        at_least(dve, x1_ready, done)
                        at_least(dve, mv2_done, before)
                        dve.bn_stats(bn2[:, :], r).then_inc(bn2_done, 1)
                        own_waits(dve, ident_made)
                        at_least(dve, bn2_done, done)
                        at_least(dve, z_ready, before)
                        dve.bn_aggr(mv2[:, :], bn2[:, :]).then_inc(mv2_done, 1)
                        at_least(dve, mv2_done, done)
                        at_least(dve, rstd2_done, g - 2)
                        dve.tensor_scalar(ve2[:, :], mv2[:, 1:2], EPS, None, ALU.add).then_inc(ve2_done, 1)
                    if has_b:
                        at_least(dve, pooled, g)
                        at_least(dve, hqb_turned, g - 1)
                        dve.tensor_tensor(hb[:, :], gate_ps[:, 256:256 + D], hc[o][:, :], ALU.mult).then_inc(hb_ready, 1)
                    if has_c:
                        at_least(dve, rstd2_done, g - 1)
                        at_least(dve, z_turned, g - 2)
                        at_least(dve, gated_ready, g - 2)
                        dve.tensor_scalar(z[:, :], r, mv2[:, 0:1], rstd2[:, 0:1], ALU.subtract, ALU.mult
                                          ).then_inc(z_ready, 1)
                    if inside or g + 1 < GROUPS:
                        at_least(dve, x_loaded[o], sixteen(base, k, -1))
                        layer_norm1(g + 1, o, g + 1)
                    if has_b:
                        at_least(dve, attended, g)
                        at_least(dve, end_loaded[o], sixteen(base, k, 1))
                        at_least(dve, hqb_turned, g - 1)
                        dve.scalar_tensor_tensor(out=hq[:, :], in0=ctx_end[o][:, :], scalar=prob[o][:, J - 1:J],
                                                 in1=att_ps[:, 0:D], op0=ALU.mult, op1=ALU.add).then_inc(hq_ready, 1)
                    if inside or g + 1 < GROUPS:
                        normalise1(g + 1, o, g + 1)
                    if has_a:
                        at_least(dve, scored, g + 1)
                        at_least(dve, exp_done, g)
                        at_least(dve, best_ready, g)
                        dve.tensor_reduce(neg_max[:, :], score_ps[:, 0:J], AX.X, ALU.max, negate=True
                                          ).then_inc(neg_max_ready, 1)
                        at_least(dve, neg_max_ready, g + 1)
                        at_least(dve, s1_ready, g + 1)
                        at_least(dve, top_done, g)
                        dve.tensor_tensor(best[:, :], s1_b[p][:, :], neg_max[:, :], ALU.subtract).then_inc(best_ready, 1)
                        at_least(dve, best_ready, g + 1)
                        dve.transpose(bestT[:, :], best[:, 0:1].broadcast_to([P, L])).then_inc(bestT_ready, 1)
                        at_least(dve, bestT_ready, g + 1)
                        dve.tensor_reduce(neg_top[:, :], bestT[:, :], AX.X, ALU.max, negate=True
                                          ).then_inc(neg_top_ready, 1)
                    for s in state_steps[:1]:
                        state_sum(s)
                    if has_c:
                        at_least(dve, gate_summed, g - 1)
                        at_least(dve, tanh_done, g - 2)
                        dve.tensor_tensor(gate_in, gate_ps[:, 0:D], bg_all[:, :], ALU.add).then_inc(gate_in_ready, 1)
                    if has_a:
                        at_least(dve, exp_done, g + 1)
                        at_least(dve, prob_ready, g)
                        dve.reciprocal(row_rec[:, :], row_sum[:, :]).then_inc(row_rec_ready, 1)
                        at_least(dve, row_rec_ready, g + 1)
                        dve.tensor_scalar(prob[p][:, :], prob[p][:, :], row_rec[:, 0:1], None, ALU.mult
                                          ).then_inc(prob_ready, 1)
                    for s in state_steps[:1]:
                        state_keep(s)
                    if has_c:
                        at_least(dve, tanh_done, g - 1)
                        at_least(dve, gated_stored[p], sixteen(base, k, 4))
                        dve.scalar_tensor_tensor(out=gated[p][:, :], in0=gate_th, scalar=1.0, in1=z[:, :],
                                                 op0=ALU.add, op1=ALU.mult).then_inc(gated_ready, 1)
                    if has_a:
                        at_least(dve, top_done, g + 1)
                        at_least(dve, pick_ready, g)
                        dve.reciprocal(top_rec[:, :], top_sum[:, :]).then_inc(top_rec_ready, 1)
                        at_least(dve, top_rec_ready, g + 1)
                        at_least(dve, pooled, g)
                        dve.tensor_scalar(pick[:, :], same_batch[:, :], top_e[:, 0:1], top_rec[:, 0:1],
                                          ALU.mult, ALU.mult).then_inc(pick_ready, 1)
                    for s in state_steps[1:]:
                        state_sum(s)
                        state_keep(s)
                    if isinstance(g, int) and g == GROUPS - 2:
                        impulse_response()
                    if isinstance(g, int) and g == GROUPS:
                        magnitudes(dve, fc_scale[:, :], fc_in[:, :, :], fc_loaded)

                dve.wait_ge(x_loaded[0], 16)
                layer_norm1(0, 0, 0)
                normalise1(0, 0, 0)
                dve.wait_ge(masks_made, 2)
                software_pipeline(dve, step)

        bn_y_done, mv_y_done, ve_y_done, rstd_y_done = (sem(n) for n in ("bn_y_done", "mv_y_done", "ve_y_done", "rstd_y_done"))
        bn_x_done, mv_x_done, ve_x_done, rstd_x_done = (sem(n) for n in ("bn_x_done", "mv_x_done", "ve_x_done", "rstd_x_done"))
        shift_done = sem("shift_done")
        centred = sem("centred")
        yn_done = sem("yn_done")
        gamma_done = sem("gamma_done")
        x2_done = sem("x2_done")
        xn_done = sem("xn_done")
        x_turned = sem("x_turned")

        def statistics(dve, source, count, bn, mv, ve, bn_done, mv_done, ve_done, rstd_done):
            count = known(dve, count)
            after = known(dve, count + 1)
            own_waits(dve, ident_made)
            at_least(dve, mv_done, count)
            for r in range(CH):
                ins = dve.bn_stats(bn[:, r, :], source(r))
            ins.then_inc(bn_done, 1)
            own_waits(dve, ident_made)
            at_least(dve, bn_done, after)
            for r in range(CH):
                ins = dve.bn_aggr(mv[:, r, :], bn[:, r, :])
            ins.then_inc(mv_done, 1)
            at_least(dve, mv_done, after)
            at_least(dve, rstd_done, count)
            dve.tensor_scalar(ve[:, :], mv[:, :, 1], EPS, None, ALU.add).then_inc(ve_done, 1)

        def res(c, r):
            return resid[:, bass.ds(c * CH + r, 1), :].rearrange("p a d -> p (a d)")

        def y_stats(dve, c):
            y = y_in
            if isinstance(c, int) and c == 1:
                y = y_second
                dve.wait_ge(y_second_loaded, 16)
            elif isinstance(c, int) and c == 0:
                dve.wait_ge(y_loaded, 16)
            else:
                at_least(dve, y_loaded, 16 * c)
            statistics(dve, lambda r: y[:, r, :], c, bn_y, mv_y, ve_y, bn_y_done, mv_y_done, ve_y_done, rstd_y_done)

        def shift(dve, c):
            at_least(dve, rstd_y_done, c + 1)
            at_least(dve, yn_done, c - 1)
            dve.scalar_tensor_tensor(out=shift_y[:, :], in0=mv_y[:, :, 0], scalar=-1.0, in1=rstd_y[:, :],
                                     op0=ALU.mult, op1=ALU.mult).then_inc(shift_done, 1)

        def add_y(dve, c):
            y = y_second if isinstance(c, int) and c == 1 else y_in
            at_least(dve, gamma_done, c)
            x2 = resid[:, bass.ds(c * CH, CH), :]
            dve.tensor_tensor(x2, x2, y[:, :, :], ALU.add).then_inc(x2_done, 1)

        def centre_first(dve):
            for r in range(CH):
                ins = dve.scalar_tensor_tensor(out=y_in[:, r, :], in0=y_in[:, r, :], scalar=mv_y[:, r, 0:1],
                                               in1=gamma_all[:, :], op0=ALU.subtract, op1=ALU.mult)
            ins.then_inc(centred, 1)

        def add_first(dve):
            dve.wait_ge(centred, 1)
            dve.wait_ge(rstd_y_done, 1)
            for r in range(CH):
                ins = dve.scalar_tensor_tensor(out=resid[:, r, :], in0=y_in[:, r, :], scalar=rstd_y[:, r:r + 1],
                                               in1=resid[:, r, :], op0=ALU.mult, op1=ALU.add)
            ins.then_inc(x2_done, 1)

        def x_stats(dve, c):
            at_least(dve, x2_done, c + 1)
            statistics(dve, lambda r: res(c, r), c, bn_x, mv_x, ve_x, bn_x_done, mv_x_done, ve_x_done, rstd_x_done)

        def norm_x(dve, c):
            at_least(dve, rstd_x_done, c + 1)
            at_least(dve, x_turned, c)
            for r in range(CH):
                ins = dve.tensor_scalar(xn[:, r, :], res(c, r), mv_x[:, r, 0:1], rstd_x[:, r:r + 1],
                                        ALU.subtract, ALU.mult)
            ins.then_inc(xn_done, 1)

        def norm_y(act, c):
            y = y_second if isinstance(c, int) and c == 1 else y_in
            at_least(act, shift_done, c)
            for r in range(CH):
                ins = act.activation(y[:, r, :], y[:, r, :], ACT.Identity, bias=shift_y[:, r:r + 1],
                                     scale=rstd_y[:, r:r + 1])
            ins.then_inc(yn_done, 1)

        def deviation_y(pool, c):
            at_least(pool, ve_y_done, c + 1)
            if isinstance(c, int) and c == 1:
                pool.wait_ge(x2_done, 1)
            pool.tensor_tensor(rstd_y[:, :], ve_y[:, :], neg_half[:, 0:CH], ALU.pow).then_inc(rstd_y_done, 1)

        def deviation_x(pool, c):
            at_least(pool, ve_x_done, c + 1)
            pool.tensor_tensor(rstd_x[:, :], ve_x[:, :], neg_half[:, 0:CH], ALU.pow).then_inc(rstd_x_done, 1)

        def times_gamma(pool, c):
            y = y_second if isinstance(c, int) and c == 1 else y_in
            at_least(pool, yn_done, c)
            pool.tensor_tensor(y[:, :, :], y[:, :, :], gamma_all[:, :].unsqueeze(1).broadcast_to([P, CH, D]),
                               ALU.mult).then_inc(gamma_done, 1)

        with ExitStack() as two:
            u_in = sb("u_in", [P, MT, RANK], scope=two)
            v_in = sb("v_in", [RANK, D], scope=two)
            fbT = sb("fbT", [RANK, RANK], scope=two)
            gate_all = sb("gate_all", [P, 1], scope=two)
            u_scaled = sb("u_scaled", [P, MT, RANK], scope=two)
            u_rec = sb("u_rec", [P, MT], scope=two)
            u_hi = sb("u_hi", [P, MT, RANK], F32R, scope=two)
            u_parts = sb("u_parts", [P, MT, 4, 2, RANK], scope=two)
            c_full = sb("c_full", [P, KD, RANK], scope=two)

            EARLY = 2 * CH * NB
            y_turned = sb("y_turned", [P, CQ // NB, P], scope=two)
            y_early = sb("y_early", [P, EARLY, CQ], scope=two)
            LATE = BATCH - EARLY
            assert EARLY == L

            scan_ps = [ps(f"scan_ps{i}", two) for i in range(4)]
            wturn_ps = [ps(f"wturn_ps{i}", two) for i in range(2)]
            low_ps = ps("low_ps", two)

            w_loaded = sem("w_loaded")
            minus_lo_made = sem("minus_lo_made")
            early_scanned = sem("early_scanned")
            early_copied = sem("early_copied")
            early_turned = sem("early_turned")
            early_placed = sem("early_placed")
            scanned = sem("scanned")
            scan_copied = sem("scan_copied")
            u_steps = sem("u_steps")
            u_done = sem("u_done")
            low_product = sem("low_product")
            c_steps = sem("c_steps")
            w_turned = sem("w_turned")
            w_copied = sem("w_copied")
            y_stored = sem("y_stored")

            BANK = 4
            W_LOADS = 4
            SCANS = CQ // BANK
            TURNS = 2 * MT * KD // BANK + MT // BANK

            block = two.enter_context(nc.Block())

            @block.sync
            def _(sp):
                sp.wait_ge(gated_stored[1], 16 * (GROUPS // 2))
                scan_load(sp, GROUPS - 1, 1)
                sp.dma_start(u_in[:, :, :], u.rearrange("(m p) r -> p m r", p=P)).then_inc(w_loaded, 16)
                sp.dma_start(v_in[:, :], v).then_inc(w_loaded, 16)
                sp.dma_start(fbT[:, :], fast_b.rearrange("a b -> b a"),
                             allow_slow_non_contiguous=True).then_inc(w_loaded, 16)
                sp.dma_start(gate_all[:, :], everywhere(gate)).then_inc(w_loaded, 16)

                def store_scan(source, first, batches, done):
                    for q in range(NB):
                        dst = bass.AP(tensor=scan_dram.tensor, offset=first * L * D + q * CQ,
                                      ap=[[D, L], [L * D, batches], [1, CQ]])
                        sp.dma_start(dst, source[q * L:(q + 1) * L, first:first + batches, :]).then_inc(done, 16)

                sp.wait_ge(early_placed, SCANS // 4)
                store_scan(y_early, 0, CH * NB, y_stored1)
                store_scan(y_early, CH * NB, CH * NB, y_stored2)
                sp.wait_ge(y_stored1, 16 * NB)
                sp.dma_start(y_in[:, :, :], scan_dram[0:TOK, :].rearrange("(r p) d -> p r d", p=P)).then_inc(y_loaded, 16)
                sp.wait_ge(y_stored2, 16 * NB)
                sp.wait_ge(ternary_done, MT + KD)
                sp.dma_start(y_second[:, :, :], scan_dram[TOK:2 * TOK, :].rearrange("(r p) d -> p r d", p=P)
                             ).then_inc(y_second_loaded, 16)
                sp.wait_ge(scan_copied, SCANS)
                store_scan(scan_x, EARLY, BATCH - EARLY, y_stored3)

            @block.gpsimd
            def _(pool):
                pool.memset(minus_lo[0:P // 2, :], 0.0)
                pool.memset(minus_lo[P // 2:P, :], -1.0).then_inc(minus_lo_made, 1)
                pool.wait_ge(minus_lo_made, 1)
                deviation_y(pool, 0)
                deviation_x(pool, 0)
                deviation_y(pool, 1)

            @block.tensor
            def _(pe):
                pe.wait_ge(toeplitz_loaded, 16 * NB * (L // SHIFTS))
                for j in range(CQ):
                    bank, col, place = j // 16, j % 16 // 4, j % 4
                    mm = pe.matmul(scan_ps[bank][place * L:(place + 1) * L, col * P:(col + 1) * P],
                                   scan_x[:, 0:EARLY, j], toeplitz[:, j, :], start=True, stop=True)
                    if j % 16 == 15:
                        mm.then_inc(early_scanned, 1)
                for bank in range(SCANS // 4):
                    pe.wait_ge(early_copied, bank + 1)
                    at_least(pe, early_placed, bank - 1)
                    for i in range(BANK):
                        mm = pe.transpose(wturn_ps[bank % 2][:, i * P:(i + 1) * P], y_turned[:, bank * BANK + i, :],
                                          ident[:, :])
                    mm.then_inc(early_turned, 1)
                pe.wait_ge(scan_loaded, 16 * NB * (GROUPS // 2 + 1))
                for j in range(CQ):
                    bank = j // BANK
                    if j % BANK == 0:
                        pe.wait_ge(early_copied, min(bank, 3) + 1)
                        at_least(pe, scan_copied, bank - 3)
                    mm = pe.matmul(scan_ps[bank % 4][:, (j % BANK) * LATE:(j % BANK + 1) * LATE], toeplitz[:, j, :],
                                   scan_x[:, EARLY:, j], start=True, stop=True)
                    if j % BANK == BANK - 1:
                        mm.then_inc(scanned, 1)
                    if j == CQ // 2:
                        pe.wait_ge(w_loaded, 16 * W_LOADS)
                        for c in range(KD):
                            low = pe.matmul(low_ps[:, c * RANK:(c + 1) * RANK], v_in[:, c * P:(c + 1) * P], fbT[:, :],
                                           start=True, stop=True)
                        low.then_inc(low_product, 1)
                turn = 0
                pe.wait_ge(early_placed, SCANS // 4)
                pe.wait_ge(ternary_done, MT)
                for c in range(KD):
                    for m in range(MT):
                        if m % BANK == 0:
                            at_least(pe, w_copied, turn - 1)
                        mm = pe.transpose(wturn_ps[turn % 2][:, (m % BANK) * P:(m % BANK + 1) * P],
                                          fc_in[:, m, c * P:(c + 1) * P], ident[:, :])
                        if m % BANK == BANK - 1:
                            mm.then_inc(w_turned, 1)
                            turn += 1
                pe.wait_ge(ternary_done, MT + KD)
                for m in range(0, MT, 2):
                    at_least(pe, w_copied, turn - 1)
                    for i in range(2):
                        for c in range(KD):
                            mm = pe.transpose(wturn_ps[turn % 2][:, (i * KD + c) * P:(i * KD + c + 1) * P],
                                              proj_in[:, c, (m + i) * P:(m + i + 1) * P], ident[:, :])
                    mm.then_inc(w_turned, 1)
                    turn += 1
                pe.wait_ge(u_done, 1)
                for m in range(MT):
                    if m % BANK == 0:
                        at_least(pe, w_copied, turn - 1)
                    mm = pe.transpose(wturn_ps[turn % 2][:, (m % BANK) * P:(m % BANK + 1) * P],
                                      u_parts[:, m, :, :, :].rearrange("p q h r -> p (q h r)"), ident[:, :])
                    if m % BANK == BANK - 1:
                        mm.then_inc(w_turned, 1)
                        turn += 1

            @block.scalar
            def _(act):
                for bank in range(SCANS // 4):
                    act.wait_ge(early_scanned, bank + 1)
                    act.copy(y_turned[:, bank * BANK:(bank + 1) * BANK, :],
                             scan_ps[bank][:, :].rearrange("p (i s) -> p i s", i=BANK)).then_inc(early_copied, 1)
                for bank in range(SCANS // 4):
                    act.wait_ge(early_turned, bank + 1)
                    act.copy(y_early[:, :, bank * 16:(bank + 1) * 16].rearrange("p b c -> p c b"),
                             wturn_ps[bank % 2][:, :].rearrange("p (c b) -> p c b", c=16)).then_inc(early_placed, 1)
                for bank in range(SCANS):
                    act.wait_ge(scanned, bank + 1)
                    act.copy(scan_x[:, EARLY:, bank * BANK:(bank + 1) * BANK].rearrange("p b j -> p j b"),
                             scan_ps[bank % 4][:, 0:BANK * LATE].rearrange("p (j b) -> p j b", j=BANK)
                             ).then_inc(scan_copied, 1)
                turn = 0
                for c in range(KD):
                    for half in range(MT // BANK):
                        act.wait_ge(w_turned, turn + 1)
                        act.copy(fc_T[:, c, half * 512:(half + 1) * 512], wturn_ps[turn % 2][:, :]).then_inc(w_copied, 1)
                        turn += 1
                for m in range(0, MT, 2):
                    act.wait_ge(w_turned, turn + 1)
                    act.copy(proj_T[:, m:m + 2, :].rearrange("p m d -> p (m d)"), wturn_ps[turn % 2][:, :]).then_inc(w_copied, 1)
                    turn += 1
                for half in range(MT // BANK):
                    act.wait_ge(w_turned, turn + 1)
                    act.copy(low_out[:, half * 512:(half + 1) * 512], wturn_ps[turn % 2][:, :]).then_inc(w_copied, 1)
                    turn += 1
                assert turn == TURNS

            @block.vector
            def _(dve):
                scales(dve, fc_scale[:, :], D, slice(0, MT), 1)
                for i in range(MT):
                    ternary(dve, i, 1)
                magnitudes(dve, proj_scale[:, :], proj_in[:, :, :], proj_loaded)
                scales(dve, proj_scale[:, :], HID, slice(MT, MT + KD), 2)
                dve.reciprocal(u_rec[:, :], fc_scale[:, :]).then_inc(u_steps, 1)
                for i in range(MT, MT + KD):
                    ternary(dve, i, 2)
                dve.wait_ge(w_loaded, 16 * W_LOADS)
                dve.wait_ge(u_steps, 1)
                for m in range(MT):
                    ins = dve.tensor_scalar(u_scaled[:, m, :], u_in[:, m, :], u_rec[:, m:m + 1], None, ALU.mult)
                ins.then_inc(u_steps, 1)
                dve.wait_ge(u_steps, 2)
                dve.tensor_copy(u_hi[:, :, :], u_scaled[:, :, :]).then_inc(u_steps, 1)
                dve.wait_ge(u_steps, 3)
                for q in range(4):
                    for part in range(2):
                        if q % 2 == 0:
                            ins = dve.tensor_copy(u_parts[:, :, q, part, :], u_hi[:, :, :].bitcast(F32))
                        else:
                            ins = dve.tensor_tensor(u_parts[:, :, q, part, :], u_scaled[:, :, :],
                                                    u_hi[:, :, :].bitcast(F32), ALU.subtract)
                ins.then_inc(u_done, 1)
                dve.wait_ge(low_product, 1)
                dve.tensor_scalar(c_full[:, :, :], low_ps[:, 0:KD * RANK].rearrange("p (k r) -> p k r", k=KD),
                                  gate_all[:, 0:1], None, ALU.mult).then_inc(c_steps, 1)
                dve.wait_ge(c_steps, 1)
                li = low_in[:, :, :].rearrange("p k (q h r) -> p k q h r", q=4, h=2)
                for q in range(4):
                    ins = dve.tensor_copy(li[:, :, q, 0, :], c_full[:, :, :])
                ins.then_inc(c_steps, 1)
                dve.wait_ge(c_steps, 2)
                for q in range(4):
                    ins = dve.tensor_tensor(li[:, :, q, 1, :], c_full[:, :, :], li[:, :, q, 0, :].bitcast(F32), ALU.subtract)
                ins.then_inc(c_steps, 1)
                dve.wait_ge(c_steps, 3)

                y_stats(dve, 0)
                centre_first(dve)
                add_first(dve)
                x_stats(dve, 0)
                y_stats(dve, 1)
                norm_x(dve, 0)
                shift(dve, 1)

        early.close()
        with ExitStack() as three:
            xn_hi = toeplitz[:, :, :].bitcast(F32R).rearrange("p (c k q) n -> p c k (q n)", c=CHUNKS, k=KD)
            xn_lo = sb("xn_lo", [P, CHUNKS, KD, TOK], F32R, scope=three)
            lr_hi = sb("lr_hi", [P, TOK], F32R, scope=three)
            lr_parts = sb("lr_parts", [P, TOK], F32R, scope=three)
            SQ = 4
            tiles = scan_x[:, :, :].rearrange("p (i t) q -> p i (t q)", i=BATCH * CQ // TOK)
            sq = [tiles[:, i, :] for i in range(SQ)]
            yT = tiles[:, SQ:SQ + KD, :]
            assert SQ * TOK <= 2 * CH * NB * CQ
            relu_sb = sb("relu", [P, 2, TOK], scope=three)
            relu = [relu_sb[:, i, :] for i in range(2)]
            sq_hi = sb("sq_hi", [P, MT, TOK], F32R, scope=three)
            sq_lo = sb("sq_lo", [P, MT, TOK], F32R, scope=three)

            xt_ps = [ps(f"xt_ps{i}", three) for i in range(KD)]
            lr_ps = ps("lr_ps", three)
            back_ps = ps("back_ps", three)
            fc_ps = [ps(f"fc_ps{i}", three) for i in range(2)]
            proj_ps = [ps(f"proj_ps{i}", three) for i in range(KD)]

            out_stored = sem("out_stored")
            xn_hi_done = sem("xn_hi_done")
            xn_lo_done = sem("xn_lo_done")
            lr_summed = sem("lr_summed")
            lr_hi_done = sem("lr_hi_done")
            lr_done = sem("lr_done")
            fc_summed = sem("fc_summed")
            relu_done = sem("relu_done")
            sq_done = sem("sq_done")
            sq_hi_done = sem("sq_hi_done")
            sq_lo_done = sem("sq_lo_done")
            proj_tile = sem("proj_tile")
            yT_done = sem("yT_done")
            back_turned = sem("back_turned")
            out_ready = sem("out_ready")
            BEHIND = 3

            def chunk_pipeline(eng, step, first=2):
                for i in range(first):
                    step(i)
                with eng.Fori(first, CHUNKS - 2, 1) as c:
                    step(c)
                for i in range(CHUNKS - 2, CHUNKS + 1):
                    step(i)

            def has(c, ahead):
                return not isinstance(c, int) or 0 <= c + ahead < CHUNKS

            def tile(c, m):
                return c * MT + m

            block = three.enter_context(nc.Block())

            @block.sync
            def _(sp):
                def load_y(c):
                    at_least(sp, x2_done, c)
                    sp.dma_start(y_in[:, :, :], scan_dram[bass.ds(c * TOK, TOK), :].rearrange("(r p) d -> p r d", p=P)
                                 ).then_inc(y_loaded, 16)

                def step(c):
                    if has(c, -1):
                        at_least(sp, out_ready, 2 * c)
                        sp.dma_start(out_tok[bass.ds((c - 1) * TOK, TOK), :].rearrange("(r p) d -> p r d", p=P),
                                     resid[:, bass.ds((c - 1) * CH, CH), :]).then_inc(out_stored, 16)
                    if has(c, 3):
                        load_y(c + 3)

                sp.wait_ge(y_stored3, 16 * NB)
                load_y(2)
                for i in range(2):
                    step(i)
                with sp.Fori(2, CHUNKS - 3, 1) as c:
                    step(c)
                for i in range(CHUNKS - 3, CHUNKS + 1):
                    step(i)
                sp.wait_ge(out_stored, 16 * CHUNKS)

            def part_of(parts, c, k):
                return parts[:, bass.ds(c, 1), k, :].rearrange("p a t -> p (a t)")

            @block.tensor
            def _(pe):
                def turn_in(c):
                    at_least(pe, xn_done, c + 1)
                    at_least(pe, xn_lo_done, c)
                    for k in range(KD):
                        for r in range(CH):
                            mm = pe.transpose(xt_ps[k][:, r * P:(r + 1) * P], xn[:, r, k * P:(k + 1) * P], ident[:, :])
                    mm.then_inc(x_turned, 1)

                def low_rank(c):
                    at_least(pe, xn_hi_done, c + 1)
                    at_least(pe, xn_lo_done, c + 1)
                    at_least(pe, lr_done, c)
                    at_least(pe, out_ready, 2 * c - 3)
                    for k in range(KD):
                        for i, part in enumerate((xn_hi, xn_lo)):
                            mm = pe.matmul(lr_ps[:, :], low_in[:, k, :], part_of(part, c, k), start=(k == 0 and i == 0),
                                           stop=(k == KD - 1 and i == 1))
                    mm.then_inc(lr_summed, 1)

                def hidden(c, m):
                    at_least(pe, relu_done, tile(c, m) - 1)
                    for k in range(KD):
                        for i, part in enumerate((xn_hi, xn_lo)):
                            pe.matmul(fc_ps[m % 2][:, :], fc_T[:, k, m * P:(m + 1) * P], part_of(part, c, k),
                                      start=(k == 0 and i == 0), stop=False)
                    if m == 0:
                        at_least(pe, lr_done, c + 1)
                    pe.matmul(fc_ps[m % 2][:, :], low_out[:, m * P:(m + 1) * P], lr_parts[:, :], start=False, stop=True
                              ).then_inc(fc_summed, 1)

                def project(c, m):
                    at_least(pe, sq_hi_done, tile(c, m) + 1)
                    at_least(pe, sq_lo_done, tile(c, m) + 1)
                    if m == 0:
                        at_least(pe, yT_done, c)
                    for i, part in enumerate((sq_hi, sq_lo)):
                        for k in range(KD):
                            mm = pe.matmul(proj_ps[k][:, :], proj_T[:, m, k * P:(k + 1) * P], part[:, m, :],
                                           start=(m == 0 and i == 0), stop=(m == MT - 1 and i == 1))
                    mm.then_inc(proj_tile, 1)

                def turn_back(c, half):
                    bank = (lr_ps, back_ps)[half]
                    at_least(pe, yT_done, c + 1)
                    if half == 1:
                        at_least(pe, out_ready, 2 * c)
                    for i in range(2):
                        for k in range(KD):
                            r = 2 * half + i
                            mm = pe.transpose(bank[:, (i * KD + k) * P:(i * KD + k + 1) * P],
                                              yT[:, k, r * P:(r + 1) * P], ident[:, :])
                    mm.then_inc(back_turned, 1)

                def step(c):
                    for m in range(MT):
                        if has(c, 0):
                            hidden(c, m)
                        if m == BEHIND and has(c, 1):
                            turn_in(c + 1)
                        if m < BEHIND and has(c, -1):
                            project(c - 1, MT - BEHIND + m)
                        if m >= BEHIND and has(c, 0):
                            project(c, m - BEHIND)
                        if m in (4, 5) and has(c, -1):
                            turn_back(c - 1, m - 4)
                        if m == 6 and has(c, 1):
                            low_rank(c + 1)

                turn_in(0)
                low_rank(0)
                chunk_pipeline(pe, step)

            @block.scalar
            def _(act):
                def split_hi(c):
                    at_least(act, x_turned, c + 1)
                    for k in range(KD):
                        ins = act.copy(part_of(xn_hi, c, k), xt_ps[k][:, :])
                    ins.then_inc(xn_hi_done, 1)

                def low_rank_hi(c):
                    at_least(act, lr_summed, c + 1)
                    at_least(act, lr_done, c)
                    act.copy(lr_hi[:, :], lr_ps[:, :]).then_inc(lr_hi_done, 1)

                def relu_tile(c, m):
                    at_least(act, fc_summed, tile(c, m) + 1)
                    at_least(act, sq_done, tile(c, m) - 1)
                    at_least(act, sq_hi_done, tile(c, m) - 1)
                    act.activation(relu[m % 2], fc_ps[m % 2][:, :], ACT.Relu, scale=fc_scale[:, m:m + 1]
                                   ).then_inc(relu_done, 1)

                def square_hi(c, m):
                    at_least(act, relu_done, tile(c, m) + 1)
                    at_least(act, proj_tile, tile(c, m) + 1 - MT)
                    at_least(act, sq_lo_done, tile(c, m) + 1 - MT)
                    act.activation(sq_hi[:, m, :], relu[m % 2], ACT.Square).then_inc(sq_hi_done, 1)

                def result_scaled(c):
                    at_least(act, proj_tile, (c + 1) * MT)
                    if isinstance(c, int) and c == 0:
                        act.wait_ge(y_stored3, 16 * NB)
                    at_least(act, back_turned, 2 * c)
                    for k in range(KD):
                        ins = act.mul(yT[:, k, :], proj_ps[k][:, :], proj_scale[:, k:k + 1])
                    ins.then_inc(yT_done, 1)

                def step(c):
                    for m in range(MT):
                        if has(c, 0):
                            if m == 7 and has(c, 1):
                                low_rank_hi(c + 1)
                            relu_tile(c, m)
                            if m >= 1:
                                square_hi(c, m - 1)
                        if m == 0 and has(c, -1):
                            square_hi(c - 1, MT - 1)
                        if m == BEHIND - 1 and has(c, -1):
                            result_scaled(c - 1)
                        if m == BEHIND and has(c, 1):
                            split_hi(c + 1)
                        if m == 5 and has(c, 2):
                            norm_y(act, c + 2)

                split_hi(0)
                norm_y(act, 1)
                low_rank_hi(0)
                chunk_pipeline(act, step)

            @block.gpsimd
            def _(pool):
                def square_lo(c, m):
                    at_least(pool, sq_done, tile(c, m) + 1)
                    at_least(pool, sq_hi_done, tile(c, m) + 1)
                    at_least(pool, proj_tile, tile(c, m) + 1 - MT)
                    pool.tensor_tensor(sq_lo[:, m, :], sq[m % SQ], sq_hi[:, m, :].bitcast(F32), ALU.subtract
                                       ).then_inc(sq_lo_done, 1)

                def step(c):
                    for m in range(MT):
                        if m == 0 and has(c, 1):
                            deviation_x(pool, c + 1)
                        if m == 4 and has(c, 2):
                            deviation_y(pool, c + 2)
                        if m == 5 and has(c, 2):
                            times_gamma(pool, c + 2)
                        if has(c, 0):
                            square_lo(c, m)

                times_gamma(pool, 1)
                chunk_pipeline(pool, step)

            @block.vector
            def _(dve):
                def split_lo(c):
                    at_least(dve, xn_hi_done, c + 1)
                    for k in range(KD):
                        ins = dve.tensor_tensor(part_of(xn_lo, c, k), xt_ps[k][:, :], part_of(xn_hi, c, k).bitcast(F32),
                                                ALU.subtract)
                    ins.then_inc(xn_lo_done, 1)

                def low_rank_parts(c):
                    at_least(dve, lr_hi_done, c + 1)
                    at_least(dve, fc_summed, c * MT)
                    dve.scalar_tensor_tensor(out=lr_parts[:, :], in0=lr_hi[:, :].bitcast(F32), scalar=minus_lo[:, 0:1],
                                             in1=lr_ps[:, :], op0=ALU.mult, op1=ALU.add).then_inc(lr_done, 1)

                def square(c, m):
                    at_least(dve, relu_done, tile(c, m) + 1)
                    at_least(dve, sq_lo_done, tile(c, m) + 1 - SQ)
                    dve.tensor_tensor(sq[m % SQ], relu[m % 2], relu[m % 2], ALU.mult
                                      ).then_inc(sq_done, 1)

                def result(c, half):
                    at_least(dve, back_turned, 2 * c + half + 1)
                    bank = (lr_ps, back_ps)[half]
                    part = resid[:, bass.ds(c * CH + 2 * half, 2), :]
                    dve.tensor_tensor(part, bank[:, :].rearrange("p (r d) -> p r d", r=2), part, ALU.add
                                      ).then_inc(out_ready, 1)

                def step(c):
                    for m in range(MT):
                        if m == 7 and has(c, 1):
                            low_rank_parts(c + 1)
                        if m == 5 and has(c, 2):
                            shift(dve, c + 2)
                        if m == 0 and has(c, 1):
                            x_stats(dve, c + 1)
                        if has(c, 0):
                            square(c, m)
                        if m == 1 and has(c, 1):
                            norm_x(dve, c + 1)
                        if m == 3 and has(c, 2):
                            y_stats(dve, c + 2)
                        if m == 3 and has(c, 1):
                            split_lo(c + 1)
                        if m in (5, 6) and has(c, -1):
                            result(c - 1, m - 5)
                        if m == 7 and has(c, 2):
                            add_y(dve, c + 2)

                split_lo(0)
                low_rank_parts(0)
                add_y(dve, 1)
                chunk_pipeline(dve, step)


_INS = ['x', 'ctx_1024', 'L0_xattn_w_sim', 'L0_xattn_b_sim', 'L0_xattn_W_qv', 'L0_xattn_b_qv', 'L0_attn_A',
        'L0_attn_Bp', 'L0_attn_Cp', 'L0_attn_Dp', 'L0_attn_Wg', 'L0_attn_bg', 'L0_attn_gamma', 'L0_attn_beta',
        'L0_ffn_fast_b', 'L0_ffn_w_fc', 'L0_ffn_w_proj', 'L0_ffn_u', 'L0_ffn_v', 'L0_ffn_gate']


def kernel(**inputs):
    import concourse.bacc as _bacc
    from concourse.bass_utils import run_bass_kernel_spmd as _run

    nc = _bacc.Bacc("TRN2", target_bir_lowering=False, num_devices=1)
    arrays, args = {}, []
    for name in _INS:
        a = np.ascontiguousarray(inputs[name])
        if a.ndim == 0:
            a = a.reshape(1)
        arrays[f"in_{name}"] = a
        args.append(nc.dram_tensor(f"in_{name}", a.shape, mybir.dt.from_np(a.dtype), kind="ExternalInput").ap())
    shape = inputs['x'].shape
    args.append(nc.dram_tensor("out_0", shape, F32, kind="ExternalOutput").ap())
    perceiver_layer(nc, *args)
    r = _run(nc, [arrays], core_ids=[0])
    return r.results[0]["out_0"]
```
